# Optimizing a Trainium2 kernel written in Bass

```python
import numpy as np
import jax
import jax.numpy as jnp

def _softmax(x, axis=-1):
    return jax.nn.softmax(x, axis=axis)
def _gelu(x):
    return jax.nn.gelu(x, approximate=True)
def _silu(x):
    return jax.nn.silu(x)
def _sigmoid(x):
    return jax.nn.sigmoid(x)
def _layernorm(x, axis=-1, eps=1e-5):
    m = jnp.mean(x, axis=axis, keepdims=True)
    v = jnp.var(x, axis=axis, keepdims=True)
    return (x - m) / jnp.sqrt(v + eps)
def _scatter_add(tgt, idx, src, axis=0):
    return tgt.at[idx].add(src)
def _segment_sum(src, seg, n):
    return jax.ops.segment_sum(src, seg, n)

kernel_name = 'mk_conv_preact_d1_conv_nchw256_4d78be'

def setup_inputs(seed: int = 0):
    np.random.seed(seed)
    _w = jnp.asarray
    def _rec_inputs():
        import jax
        import jax.numpy as jnp
        _gk = jax.random.key(seed)
        x = -0.0002928 + 1 * jax.random.normal(jax.random.fold_in(_gk, 1), (4, 256, 64, 64), jnp.float32)
        return x
    x = _rec_inputs()
    def _L0_conv_setup():
        import jax, jax.numpy as jnp
        import numpy as np
        EPS_LN = 1e-05
        EPS_BN = 1e-05
        NUM_HEADS = 8

        def _gelu(x):
            return jax.nn.gelu(x, approximate=False)

        def _ln(x, w, b):
            mu = jnp.mean(x, axis=-1, keepdims=True)
            var = jnp.mean((x - mu) ** 2, axis=-1, keepdims=True)
            return (x - mu) / jnp.sqrt(var + EPS_LN) * w + b

        def _bn(x, g, b):
            scale = g * (1.0 + EPS_BN) ** (-0.5)
            return x * scale[None, :, None, None] + b[None, :, None, None]

        def _conv1x1(x, w):
            return jnp.einsum('bchw,oc->bohw', x, w)

        def _unfold3(x, r):
            B, C, H, W = x.shape
            xp = jnp.pad(x, ((0, 0), (0, 0), (r, r), (r, r)))
            pats = [xp[:, :, i * r:i * r + H, j * r:j * r + W] for i in range(3) for j in range(3)]
            return jnp.stack(pats, axis=2)

        def _atrous_attn(q, k, v, num_heads, r):
            B, C, H, W = q.shape
            hd = C // num_heads
            scale = hd ** (-0.5)
            qh = q.reshape(B, num_heads, hd, H, W)
            kp = _unfold3(k, r).reshape(B, num_heads, hd, 9, H, W)
            attn = jax.nn.softmax(jnp.einsum('bnchw,bnckhw->bnkhw', qh, kp) * scale, axis=2)
            vp = _unfold3(v, r).reshape(B, num_heads, hd, 9, H, W)
            out = jnp.einsum('bnkhw,bnckhw->bnchw', attn, vp)
            return out.reshape(B, C, H, W).transpose(0, 2, 3, 1)

        def _window_attn(x_bhwc, qkv_w, proj_w, proj_b, num_heads, r):
            xc = x_bhwc.transpose(0, 3, 1, 2)
            C = xc.shape[1]
            qkv = _conv1x1(xc, qkv_w)
            out = _atrous_attn(qkv[:, :C], qkv[:, C:2 * C], qkv[:, 2 * C:], num_heads, r)
            return jnp.einsum('bhwc,oc->bhwo', out, proj_w) + proj_b

        def _mlp(x_bhwc, c1_w, c1_b, bn1_g, bn1_b, dw_w, dw_b, bn2_g, bn2_b, c2_w, c2_b, bn3_g, bn3_b):
            xc = x_bhwc.transpose(0, 3, 1, 2)
            h = _bn(_gelu(_conv1x1(xc, c1_w) + c1_b[None, :, None, None]), bn1_g, bn1_b)
            dw = jax.lax.conv_general_dilated(h, dw_w, (1, 1), 'SAME', feature_group_count=h.shape[1], dimension_numbers=('NCHW', 'OIHW', 'NCHW'))
            dw = dw + dw_b[None, :, None, None]
            h = _bn(_gelu(dw + h), bn2_g, bn2_b)
            out = _bn(_conv1x1(h, c2_w) + c2_b[None, :, None, None], bn3_g, bn3_b)
            return out.transpose(0, 2, 3, 1)
        key = jax.random.key(seed)
        B, C, H, W = (4, 256, 64, 64)
        HID = 4 * C
        ks = iter(jax.random.split(key, 64))

        def nrm(shape, scale=0.02):
            return jax.random.normal(next(ks), shape, dtype=jnp.float32) * scale
        inp = {'x': jax.random.normal(next(ks), (B, C, H, W), dtype=jnp.float32), 'ln1_w': jnp.ones((C,), jnp.float32), 'ln1_b': jnp.zeros((C,), jnp.float32), 'ln2_w': jnp.ones((C,), jnp.float32), 'ln2_b': jnp.zeros((C,), jnp.float32)}
        for i in (1, 2, 3):
            inp[f'qkv{i}_w'] = nrm((3 * C, C))
            inp[f'proj{i}_w'] = nrm((C, C))
            inp[f'proj{i}_b'] = jnp.zeros((C,), jnp.float32)
        inp.update(tc_conv_w=nrm((C, C)), tc_conv_b=jnp.zeros((C,), jnp.float32), tc_bn1_g=jnp.ones((C,), jnp.float32), tc_bn1_b=jnp.zeros((C,), jnp.float32), tc_pool_w=nrm((C, C)), tc_bn2_g=jnp.ones((C,), jnp.float32), tc_bn2_b=jnp.zeros((C,), jnp.float32), tc_trans_w=nrm((C, 5 * C)), tc_trans_b=jnp.zeros((C,), jnp.float32), tc_bn3_g=jnp.ones((C,), jnp.float32), tc_bn3_b=jnp.zeros((C,), jnp.float32), mlp_c1_w=nrm((HID, C)), mlp_c1_b=jnp.zeros((HID,), jnp.float32), mlp_bn1_g=jnp.ones((HID,), jnp.float32), mlp_bn1_b=jnp.zeros((HID,), jnp.float32), mlp_dw_w=nrm((HID, 1, 3, 3), 0.1), mlp_dw_b=jnp.zeros((HID,), jnp.float32), mlp_bn2_g=jnp.ones((HID,), jnp.float32), mlp_bn2_b=jnp.zeros((HID,), jnp.float32), mlp_c2_w=nrm((C, HID)), mlp_c2_b=jnp.zeros((C,), jnp.float32), mlp_bn3_g=jnp.ones((C,), jnp.float32), mlp_bn3_b=jnp.zeros((C,), jnp.float32))
        return inp
    _L0_conv_all = _L0_conv_setup()
    _L0_conv_in = {k: v for k, v in _L0_conv_all.items() if k in ('ln1_w', 'ln1_b', 'ln2_w', 'ln2_b', 'qkv1_w', 'proj1_w', 'proj1_b', 'qkv2_w', 'proj2_w', 'proj2_b', 'qkv3_w', 'proj3_w', 'proj3_b', 'tc_conv_w', 'tc_conv_b', 'tc_bn1_g', 'tc_bn1_b', 'tc_pool_w', 'tc_bn2_g', 'tc_bn2_b', 'tc_trans_w', 'tc_trans_b', 'tc_bn3_g', 'tc_bn3_b', 'mlp_c1_w', 'mlp_c1_b', 'mlp_bn1_g', 'mlp_bn1_b', 'mlp_dw_w', 'mlp_dw_b', 'mlp_bn2_g', 'mlp_bn2_b', 'mlp_c2_w', 'mlp_c2_b', 'mlp_bn3_g', 'mlp_bn3_b', )}
    del _L0_conv_all

    return {
        "x": x,
        "L0_conv_ln1_w": _L0_conv_in["ln1_w"],
        "L0_conv_ln1_b": _L0_conv_in["ln1_b"],
        "L0_conv_ln2_w": _L0_conv_in["ln2_w"],
        "L0_conv_ln2_b": _L0_conv_in["ln2_b"],
        "L0_conv_qkv1_w": _L0_conv_in["qkv1_w"],
        "L0_conv_proj1_w": _L0_conv_in["proj1_w"],
        "L0_conv_proj1_b": _L0_conv_in["proj1_b"],
        "L0_conv_qkv2_w": _L0_conv_in["qkv2_w"],
        "L0_conv_proj2_w": _L0_conv_in["proj2_w"],
        "L0_conv_proj2_b": _L0_conv_in["proj2_b"],
        "L0_conv_qkv3_w": _L0_conv_in["qkv3_w"],
        "L0_conv_proj3_w": _L0_conv_in["proj3_w"],
        "L0_conv_proj3_b": _L0_conv_in["proj3_b"],
        "L0_conv_tc_conv_w": _L0_conv_in["tc_conv_w"],
        "L0_conv_tc_conv_b": _L0_conv_in["tc_conv_b"],
        "L0_conv_tc_bn1_g": _L0_conv_in["tc_bn1_g"],
        "L0_conv_tc_bn1_b": _L0_conv_in["tc_bn1_b"],
        "L0_conv_tc_pool_w": _L0_conv_in["tc_pool_w"],
        "L0_conv_tc_bn2_g": _L0_conv_in["tc_bn2_g"],
        "L0_conv_tc_bn2_b": _L0_conv_in["tc_bn2_b"],
        "L0_conv_tc_trans_w": _L0_conv_in["tc_trans_w"],
        "L0_conv_tc_trans_b": _L0_conv_in["tc_trans_b"],
        "L0_conv_tc_bn3_g": _L0_conv_in["tc_bn3_g"],
        "L0_conv_tc_bn3_b": _L0_conv_in["tc_bn3_b"],
        "L0_conv_mlp_c1_w": _L0_conv_in["mlp_c1_w"],
        "L0_conv_mlp_c1_b": _L0_conv_in["mlp_c1_b"],
        "L0_conv_mlp_bn1_g": _L0_conv_in["mlp_bn1_g"],
        "L0_conv_mlp_bn1_b": _L0_conv_in["mlp_bn1_b"],
        "L0_conv_mlp_dw_w": _L0_conv_in["mlp_dw_w"],
        "L0_conv_mlp_dw_b": _L0_conv_in["mlp_dw_b"],
        "L0_conv_mlp_bn2_g": _L0_conv_in["mlp_bn2_g"],
        "L0_conv_mlp_bn2_b": _L0_conv_in["mlp_bn2_b"],
        "L0_conv_mlp_c2_w": _L0_conv_in["mlp_c2_w"],
        "L0_conv_mlp_c2_b": _L0_conv_in["mlp_c2_b"],
        "L0_conv_mlp_bn3_g": _L0_conv_in["mlp_bn3_g"],
        "L0_conv_mlp_bn3_b": _L0_conv_in["mlp_bn3_b"],
    }

def reference(x, L0_conv_ln1_w, L0_conv_ln1_b, L0_conv_ln2_w, L0_conv_ln2_b, L0_conv_qkv1_w, L0_conv_proj1_w, L0_conv_proj1_b, L0_conv_qkv2_w, L0_conv_proj2_w, L0_conv_proj2_b, L0_conv_qkv3_w, L0_conv_proj3_w, L0_conv_proj3_b, L0_conv_tc_conv_w, L0_conv_tc_conv_b, L0_conv_tc_bn1_g, L0_conv_tc_bn1_b, L0_conv_tc_pool_w, L0_conv_tc_bn2_g, L0_conv_tc_bn2_b, L0_conv_tc_trans_w, L0_conv_tc_trans_b, L0_conv_tc_bn3_g, L0_conv_tc_bn3_b, L0_conv_mlp_c1_w, L0_conv_mlp_c1_b, L0_conv_mlp_bn1_g, L0_conv_mlp_bn1_b, L0_conv_mlp_dw_w, L0_conv_mlp_dw_b, L0_conv_mlp_bn2_g, L0_conv_mlp_bn2_b, L0_conv_mlp_c2_w, L0_conv_mlp_c2_b, L0_conv_mlp_bn3_g, L0_conv_mlp_bn3_b):
    import jax
    import jax.numpy as jnp
    def _L0_conv_ref(x, ln1_w, ln1_b, ln2_w, ln2_b, qkv1_w, proj1_w, proj1_b, qkv2_w, proj2_w, proj2_b, qkv3_w, proj3_w, proj3_b, tc_conv_w, tc_conv_b, tc_bn1_g, tc_bn1_b, tc_pool_w, tc_bn2_g, tc_bn2_b, tc_trans_w, tc_trans_b, tc_bn3_g, tc_bn3_b, mlp_c1_w, mlp_c1_b, mlp_bn1_g, mlp_bn1_b, mlp_dw_w, mlp_dw_b, mlp_bn2_g, mlp_bn2_b, mlp_c2_w, mlp_c2_b, mlp_bn3_g, mlp_bn3_b):
        import jax, jax.numpy as jnp
        import numpy as np
        EPS_LN = 1e-05
        EPS_BN = 1e-05
        NUM_HEADS = 8

        def _gelu(x):
            return jax.nn.gelu(x, approximate=False)

        def _ln(x, w, b):
            mu = jnp.mean(x, axis=-1, keepdims=True)
            var = jnp.mean((x - mu) ** 2, axis=-1, keepdims=True)
            return (x - mu) / jnp.sqrt(var + EPS_LN) * w + b

        def _bn(x, g, b):
            scale = g * (1.0 + EPS_BN) ** (-0.5)
            return x * scale[None, :, None, None] + b[None, :, None, None]

        def _conv1x1(x, w):
            return jnp.einsum('bchw,oc->bohw', x, w)

        def _unfold3(x, r):
            B, C, H, W = x.shape
            xp = jnp.pad(x, ((0, 0), (0, 0), (r, r), (r, r)))
            pats = [xp[:, :, i * r:i * r + H, j * r:j * r + W] for i in range(3) for j in range(3)]
            return jnp.stack(pats, axis=2)

        def _atrous_attn(q, k, v, num_heads, r):
            B, C, H, W = q.shape
            hd = C // num_heads
            scale = hd ** (-0.5)
            qh = q.reshape(B, num_heads, hd, H, W)
            kp = _unfold3(k, r).reshape(B, num_heads, hd, 9, H, W)
            attn = jax.nn.softmax(jnp.einsum('bnchw,bnckhw->bnkhw', qh, kp) * scale, axis=2)
            vp = _unfold3(v, r).reshape(B, num_heads, hd, 9, H, W)
            out = jnp.einsum('bnkhw,bnckhw->bnchw', attn, vp)
            return out.reshape(B, C, H, W).transpose(0, 2, 3, 1)

        def _window_attn(x_bhwc, qkv_w, proj_w, proj_b, num_heads, r):
            xc = x_bhwc.transpose(0, 3, 1, 2)
            C = xc.shape[1]
            qkv = _conv1x1(xc, qkv_w)
            out = _atrous_attn(qkv[:, :C], qkv[:, C:2 * C], qkv[:, 2 * C:], num_heads, r)
            return jnp.einsum('bhwc,oc->bhwo', out, proj_w) + proj_b

        def _mlp(x_bhwc, c1_w, c1_b, bn1_g, bn1_b, dw_w, dw_b, bn2_g, bn2_b, c2_w, c2_b, bn3_g, bn3_b):
            xc = x_bhwc.transpose(0, 3, 1, 2)
            h = _bn(_gelu(_conv1x1(xc, c1_w) + c1_b[None, :, None, None]), bn1_g, bn1_b)
            dw = jax.lax.conv_general_dilated(h, dw_w, (1, 1), 'SAME', feature_group_count=h.shape[1], dimension_numbers=('NCHW', 'OIHW', 'NCHW'))
            dw = dw + dw_b[None, :, None, None]
            h = _bn(_gelu(dw + h), bn2_g, bn2_b)
            out = _bn(_conv1x1(h, c2_w) + c2_b[None, :, None, None], bn3_g, bn3_b)
            return out.transpose(0, 2, 3, 1)
        tx = x.transpose(0, 2, 3, 1)
        n1 = _ln(tx, ln1_w, ln1_b)
        t1 = tx + _window_attn(n1, qkv1_w, proj1_w, proj1_b, NUM_HEADS, 1)
        t2 = tx + _window_attn(n1, qkv2_w, proj2_w, proj2_b, NUM_HEADS, 2)
        t3 = tx + _window_attn(n1, qkv3_w, proj3_w, proj3_b, NUM_HEADS, 3)
        xc1 = jax.nn.relu(_bn(_conv1x1(x, tc_conv_w) + tc_conv_b[None, :, None, None], tc_bn1_g, tc_bn1_b))
        pool = jnp.mean(x, axis=(2, 3), keepdims=True)
        pool = jax.nn.relu(_bn(_conv1x1(pool, tc_pool_w), tc_bn2_g, tc_bn2_b))
        pool = jnp.broadcast_to(pool, x.shape)
        cat = jnp.concatenate([xc1, t1.transpose(0, 3, 1, 2), t2.transpose(0, 3, 1, 2), t3.transpose(0, 3, 1, 2), pool], axis=1)
        tr = jax.nn.relu(_bn(_conv1x1(cat, tc_trans_w) + tc_trans_b[None, :, None, None], tc_bn3_g, tc_bn3_b)).transpose(0, 2, 3, 1)
        tr = tr + _mlp(_ln(tr, ln2_w, ln2_b), mlp_c1_w, mlp_c1_b, mlp_bn1_g, mlp_bn1_b, mlp_dw_w, mlp_dw_b, mlp_bn2_g, mlp_bn2_b, mlp_c2_w, mlp_c2_b, mlp_bn3_g, mlp_bn3_b)
        return tr.transpose(0, 3, 1, 2)

    def _gn(v, G=32, eps=1e-5):
        B_, C_, H_, W_ = v.shape
        g = v.reshape(B_, G, C_ // G, H_, W_)
        m = jnp.mean(g, axis=(2, 3, 4), keepdims=True)
        s = jnp.var(g, axis=(2, 3, 4), keepdims=True)
        return ((g - m) / jnp.sqrt(s + eps)).reshape(v.shape)

    def _ln_c(v, eps=1e-6):
        m = jnp.mean(v, axis=1, keepdims=True)
        s = jnp.var(v, axis=1, keepdims=True)
        return (v - m) / jnp.sqrt(s + eps)

    def _ln_t(v, eps=1e-5):
        m = jnp.mean(v, axis=-1, keepdims=True)
        s = jnp.var(v, axis=-1, keepdims=True)
        return (v - m) / jnp.sqrt(s + eps)

    def _to_tokens(v):
        B_, C_, H_, W_ = v.shape
        return v.reshape(B_, C_, H_ * W_).transpose(0, 2, 1)
    def _from_tokens(t, like):
        B_, C_, H_, W_ = like.shape
        return t.transpose(0, 2, 1).reshape(B_, C_, H_, W_)

    x = x + _L0_conv_ref(_gn(x), L0_conv_ln1_w, L0_conv_ln1_b, L0_conv_ln2_w, L0_conv_ln2_b, L0_conv_qkv1_w, L0_conv_proj1_w, L0_conv_proj1_b, L0_conv_qkv2_w, L0_conv_proj2_w, L0_conv_proj2_b, L0_conv_qkv3_w, L0_conv_proj3_w, L0_conv_proj3_b, L0_conv_tc_conv_w, L0_conv_tc_conv_b, L0_conv_tc_bn1_g, L0_conv_tc_bn1_b, L0_conv_tc_pool_w, L0_conv_tc_bn2_g, L0_conv_tc_bn2_b, L0_conv_tc_trans_w, L0_conv_tc_trans_b, L0_conv_tc_bn3_g, L0_conv_tc_bn3_b, L0_conv_mlp_c1_w, L0_conv_mlp_c1_b, L0_conv_mlp_bn1_g, L0_conv_mlp_bn1_b, L0_conv_mlp_dw_w, L0_conv_mlp_dw_b, L0_conv_mlp_bn2_g, L0_conv_mlp_bn2_b, L0_conv_mlp_c2_w, L0_conv_mlp_c2_b, L0_conv_mlp_bn3_g, L0_conv_mlp_bn3_b)
    return x


_drawn_inputs = setup_inputs


def setup_inputs(seed=0):
    import zlib

    import numpy as np

    out = dict(_drawn_inputs(seed))
    spreads = {'L0_conv_ln1_w': (1.0, 0.6),
     'L0_conv_ln1_b': (0.0, 0.8),
     'L0_conv_ln2_w': (1.0, 0.6),
     'L0_conv_ln2_b': (0.0, 0.8),
     'L0_conv_proj1_b': (0.0, 1.094),
     'L0_conv_proj2_b': (0.0, 1.339),
     'L0_conv_proj3_b': (0.0, 1.314),
     'L0_conv_tc_conv_b': (0.0, 0.524),
     'L0_conv_tc_bn1_g': (1.0, 0.6),
     'L0_conv_tc_bn1_b': (0.0, 1.805),
     'L0_conv_tc_bn2_g': (1.0, 0.6),
     'L0_conv_tc_bn2_b': (0.0, 1.739),
     'L0_conv_tc_trans_b': (0.0, 0.394),
     'L0_conv_tc_bn3_g': (1.0, 0.2),
     'L0_conv_tc_bn3_b': (0.0, 0.381),
     'L0_conv_mlp_c1_b': (0.0, 0.316),
     'L0_conv_mlp_bn1_g': (1.0, 0.6),
     'L0_conv_mlp_bn1_b': (0.0, 0.424),
     'L0_conv_mlp_dw_b': (0.0, 0.435),
     'L0_conv_mlp_bn2_g': (1.0, 0.6),
     'L0_conv_mlp_bn2_b': (0.0, 0.343),
     'L0_conv_mlp_c2_b': (0.0, 0.1),
     'L0_conv_mlp_bn3_g': (1.0, 0.6),
     'L0_conv_mlp_bn3_b': (0.0, 0.292)}
    factors = {'L0_conv_qkv1_w': 7.067,
     'L0_conv_proj1_w': 7.119,
     'L0_conv_qkv2_w': 7.116,
     'L0_conv_proj2_w': 7.091,
     'L0_conv_qkv3_w': 7.147,
     'L0_conv_proj3_w': 7.206,
     'L0_conv_tc_pool_w': 198.458,
     'L0_conv_tc_conv_w': 2.866}
    for name, (base, spread) in spreads.items():
        noise = np.random.default_rng([zlib.crc32(name.encode()), seed]).standard_normal(out[name].shape)
        drawn = base * np.exp(spread * noise) if base else spread * noise
        out[name] = jnp.asarray(drawn.astype(out[name].dtype))
    for name, factor in factors.items():
        out[name] = (out[name] * factor).astype(out[name].dtype)
    return out
```

```python
from contextlib import ExitStack

import concourse.bass as bass
from concourse import mybir

F32 = mybir.dt.float32
BF16 = mybir.dt.bfloat16
ALU = mybir.AluOpType
ACT = mybir.ActivationFunctionType
AX_X = mybir.AxisListType.X

B, C, H, W = 4, 256, 64, 64
HID = 4 * C
P = 128
CT = C // P
HT = HID // P
PX = H * W
CH_ROWS = 8
CHUNK = CH_ROWS * W
NCH = H // CH_ROWS
HEADS, HD = 8, C // 8
PAIRS = HEADS // 2
QB, KB = 8, 10
NQ, NK = QB * QB, KB * KB
HALO = 3
EPS = 1e-5
START = 1
BN_SCALE = (1.0 + EPS) ** -0.5
ROWS3 = 3 * 3 * QB
N1H, N1W = ROWS3 + 2 * HALO, W + 2 * HALO

STRIPS = {1: 8, 2: 8, 3: 9}


def blocks_of(r):
    out = []
    for px in range(r):
        n = len(range(px, W, r))
        starts = list(range(0, n - QB + 1, QB))
        if starts[-1] + QB < n:
            starts.append(n - QB)
        done = 0
        for s in starts:
            out.append((px + r * s, done - s))
            done = s + QB
    return out


def runs_of(r):
    starts = [c0 for c0, _ in blocks_of(r)]
    out, i = [], 0
    while i < len(starts):
        n, d = 1, QB * r
        while i + n < len(starts) and starts[i + n] - starts[i + n - 1] == d:
            n += 1
        out.append((i, n, starts[i], d))
        i += n
    return out


BLOCKS = {r: blocks_of(r) for r in (1, 2, 3)}
NBMAX = 9
KBANK = 512 // NK
STRIP_BASE = {1: 0, 2: 8, 3: 16}
BLOCK_BASE = {1: 0, 2: 8 * len(BLOCKS[1]), 3: 8 * len(BLOCKS[1]) + 8 * len(BLOCKS[2])}
STRIPS_PER_B = 25
BLOCKS_PER_B = BLOCK_BASE[3] + 9 * len(BLOCKS[3])
TAIL_STRIPS = NCH + 1

VECS = ["ln1_w", "ln1_b", "ln2_w", "ln2_b", "proj1_b", "proj2_b", "proj3_b", "tc_conv_b", "tc_bn1_g", "tc_bn1_b",
        "tc_bn2_g", "tc_bn2_b", "tc_trans_b", "tc_bn3_g", "tc_bn3_b", "mlp_c2_b", "mlp_bn3_g", "mlp_bn3_b"]
HVECS = ["mlp_c1_b", "mlp_bn1_g", "mlp_bn1_b", "mlp_dw_b", "mlp_bn2_g", "mlp_bn2_b"]
CO = {}
_at = 0
for _n, _w in (("ident", P), ("cdiag", P), ("coff", P), ("mean", P), ("group", P), ("pairI", P), ("mask", 4 * NK),
               ("left", 4 * NK), ("right", P)):
    CO[_n] = (_at, _at + _w)
    _at += _w
CONST_COLS = _at


def build(nc, x, wqkv, wproj, wtrans, wconv, wpool, wc1, wc2, wdw, vecs, hvecs, consts, out):
    with ExitStack() as ctx:
        def sb(name, shape, dt=F32):
            return ctx.enter_context(nc.sbuf_tensor(name, shape, dt))

        def sem(name):
            return ctx.enter_context(nc.semaphore(name))

        bank = [ctx.enter_context(nc.psum_tensor(f"bank{i}", [P, 512], F32)) for i in range(8)]

        qkv_w = sb("qkv_w", [P, 3, CT, 3 * C])
        comp_w = sb("comp_w", [P, 3, 2, C])
        conv_w = sb("conv_w", [P, CT, C])
        t0_w = sb("t0_w", [P, CT, C])
        tsum_w = sb("tsum_w", [P, CT, C])
        c1_w = sb("c1_w", [P, CT, HID])
        c2_w = sb("c2_w", [P, HT, C])
        dw_w = sb("dw_w", [P, HT, 9])
        vec = sb("vec", [P, len(VECS), CT])
        hvec = sb("hvec", [P, len(HVECS), HT])
        V = {n: vec[:, i, :] for i, n in enumerate(VECS)}
        HV = {n: hvec[:, i, :] for i, n in enumerate(HVECS)}
        small = sb("small", [P, 48])
        matc = sb("matc", [P, 5, P])
        ident, cdiag, coff, meanm, groupm = (matc[:, i, :] for i in range(5))
        identb = sb("identb", [P, P], BF16)
        pair_b = sb("pair_b", [NQ, P], BF16)
        mask_b = sb("mask_b", [NQ, 4 * NK], BF16)
        left_b = sb("left_b", [96, 4, NK], BF16)
        right_b = sb("right_b", [96, 2, P], BF16)

        g = sb("g", [P, CT, PX])
        n1p = sb("n1p", [P, CT, N1H, N1W])
        acc = sb("acc", [P, CT, ROWS3, W])
        KW = NBMAX * NK
        work = sb("work", [P, 2 * KW + 2 * KW + 2 * CHUNK + 3 * PAIRS * 65 + 2 * 512])
        o = 0
        nbk = work[:, o:o + 2 * KW].rearrange("p (k i n) -> p k i n", k=CT, i=NBMAX); o += 2 * KW
        ks = work[:, o:o + 2 * KW].rearrange("p (k i n) -> p k i n", k=CT, i=NBMAX); o += 2 * KW
        attn = work[:, o:o + 2 * CHUNK].rearrange("p (a r w) -> p a r w", a=2, r=CH_ROWS); o += 2 * CHUNK
        vb = [work[0:NK, o + i * PAIRS * 65:o + (i + 1) * PAIRS * 65].rearrange("p (j c) -> p j c", j=PAIRS)
              for i in range(3)]
        o += 3 * PAIRS * 65
        pb = [work[0:NK, o + i * 512:o + (i + 1) * 512] for i in range(2)]
        qd = sb("qd", [P, CT, NBMAX, 4, NQ])
        mx = sb("mx", [P, 2, PAIRS], BF16)
        rec = sb("rec", [P, 2, PAIRS])
        an = sb("an", [P, 2, PAIRS, HD])
        sq = work[:, 0:2 * CHUNK].rearrange("p (a n) -> p a n", a=2)
        std = work[:, 1024:1536]
        rstd = work[:, 1536:2048]
        nt = work[:, 2048:3072].rearrange("p (a n) -> p a n", a=2)
        xc = work[:, 3072:4096].rearrange("p (a n) -> p a n", a=2)
        gflat = g[:].rearrange("p a n -> p (a n)")
        HSW = W + 2
        hs = gflat[:, 0:HT * KB * HSW].rearrange("p (m r w) -> p m r w", m=HT, r=KB)
        o = HT * KB * HSW
        gt = [gflat[:, o + i * CHUNK:o + (i + 1) * CHUNK] for i in range(2)]; o += 2 * CHUNK
        cv = [gflat[:, o + i * CHUNK:o + (i + 1) * CHUNK] for i in range(2)]; o += 2 * CHUNK
        h2 = [sq[:, i, :] for i in range(2)]
        xr = work[:, 3072:4096].rearrange("p (t r w) -> p t r w", t=CT, r=CH_ROWS)
        obv = work[:, 4096:5120].rearrange("p (t r w) -> p t r w", t=CT, r=CH_ROWS)
        pr_w = n1p[:].rearrange("p a r w -> p (a r w)")[:, 0:3 * CT * C].rearrange("p (i k c) -> p i k c", i=3, k=CT)
        tr_w = n1p[:].rearrange("p a r w -> p (a r w)")[:, 1536:1536 + 10 * C].rearrange("p (k c) -> p k c", k=10)
        cst = n1p[:].rearrange("p a r w -> p (a r w)")[:, 4096:4096 + CONST_COLS]
        pool_w = work[:, 4096:4608].rearrange("p (k c) -> p k c", k=CT)
        t4_w = work[:, 4608:5120].rearrange("p (k c) -> p k c", k=CT)
        st = sb("st", [P, CT, NCH, 6])
        mv = sb("mv", [P, CT, 2])

        def sm(i, n=CT):
            return small[:, i:i + n]
        s1, s2, s3, f3 = sm(0), sm(2), sm(4), sm(6)
        b1c, bias0, fb, tb3 = sm(8), sm(10), sm(12), sm(14)
        hb, hs1, hs2 = sm(16, HT), sm(24, HT), sm(32, HT)
        eps = sm(40, 1)
        ps = sb("ps", [P, 24])
        gstat = ps[:, 0:4]; gm = ps[:, 4:6]; gr = ps[:, 6:8]; gnb = ps[:, 8:10]; pg = ps[:, 10:12]; pv_ = ps[:, 12:14]
        gt2 = ps[:, 14:16]; gsd = ps[:, 16:18]; pin = ps[:, 18:20]

        w_in, setup_v, setup_p = sem("w_in"), sem("setup_v"), sem("setup_p")
        pool_passed, pe_passed, dve_passed = sem("pool_passed"), sem("pe_passed"), sem("dve_passed")
        pads_zero, pw_in = sem("pads_zero"), sem("pw_in")
        x_in, stats, group_ready, gstd_done, g_ready = sem("x_in"), sem("stats"), sem("group_ready"), sem("gstd_done"), sem("g_ready")
        gn_chain, pool_ready, pool_done, tbias_ready = sem("gn_chain"), sem("pool_ready"), sem("pool_done"), sem("tbias_ready")
        tb3_done = sem("tb3_done")
        cen_ready, sq_done, var_ready, std_done, rs_done = sem("cen_ready"), sem("sq_done"), sem("var_ready"), sem("std_done"), sem("rs_done")
        n_done, n1_done = sem("n_done"), sem("n1_done")
        conv_ready, xc_done, init_ready, acc_init = sem("conv_ready"), sem("xc_done"), sem("init_ready"), sem("acc_init")
        strip_in, qk_ready, dq_done, aq_done = sem("strip_in"), sem("qk_ready"), sem("dq_done"), sem("aq_done")
        v_ready, v_copied, s_ready, max_done = sem("v_ready"), sem("v_copied"), sem("s_ready"), sem("max_done")
        mt_ready, mt_copied, st_ready, exp_done = sem("mt_ready"), sem("mt_copied"), sem("st_ready"), sem("exp_done")
        pv_ready, rec_done, norm_done, at_ready, at_copied = sem("pv_ready"), sem("rec_done"), sem("norm_done"), sem("at_ready"), sem("at_copied")
        comp_ready, acc_added = sem("comp_ready"), sem("acc_added")
        hs_zero, t_done = sem("hs_zero"), sem("t_done")
        c1_ready, gelu1_done, h_done, tap_done, shift_done = sem("c1_ready"), sem("gelu1_done"), sem("h_done"), sem("tap_done"), sem("shift_done")
        gelu2_done, c2_ready, res_done, fin_done, xr_in, out_sent = sem("gelu2_done"), sem("c2_ready"), sem("res_done"), sem("fin_done"), sem("xr_in"), sem("out_sent")
        cen2_ready, sq2_done, var2_ready, std2_done, rs2_done, n2_done = (sem(n) for n in ("cen2_ready", "sq2_done", "var2_ready", "std2_done", "rs2_done", "n2_done"))

        xv = x.rearrange("b (t p) h w -> b p t (h w)", p=P)
        x4 = x.rearrange("b (t p) h w -> b p t h w", p=P)
        out4 = out.rearrange("b (t p) h w -> b p t h w", p=P)

        def halves(nb):
            return (0, KBANK), (KBANK, nb)

        block = ctx.enter_context(nc.Block())

        @block.sync
        def _(sp):
            for q in (out_sent,):
                sp.sem_inc(q, START)
            for dst, src in ((pr_w, wproj), (tr_w, wtrans), (cst, consts), (vec[:], vecs), (hvec[:], hvecs),
                             (qkv_w[:], wqkv), (conv_w[:], wconv), (c1_w[:], wc1), (c2_w[:], wc2),
                             (dw_w[:], wdw)):
                sp.dma_start(dst, src).then_inc(w_in, 16)

            def residual(b, s, k0, k1):
                sp.wait_ge(fin_done, (b * TAIL_STRIPS + s) * CT + START)
                row = s * CH_ROWS - 1 + k0
                for t in range(CT):
                    sp.dma_start(xr[:, t, k0:k1, :], x4[b, :, t, bass.ds(row, k1 - k0), :]).then_inc(xr_in, 16)
                sp.wait_ge(fin_done, (b * TAIL_STRIPS + s + 1) * CT + START)
                for t in range(CT):
                    sp.dma_start(out4[b, :, t, bass.ds(row, k1 - k0), :], obv[:, t, k0:k1, :]).then_inc(out_sent, 16)

            with sp.Fori(0, B) as b:
                sp.wait_ge(fin_done, b * TAIL_STRIPS * CT + START)
                for t in range(CT):
                    sp.dma_start(g[:, t, :], xv[b, :, t, :]).then_inc(x_in, 16)
                sp.wait_ge(out_sent, b * (TAIL_STRIPS * CT * 16) + START)
                sp.dma_start(pool_w, wpool).then_inc(pw_in, 16)
                sp.dma_start(t4_w, wtrans[:, 8:10, :]).then_inc(pw_in, 16)
                sp.wait_ge(acc_added, (b + 1) * STRIPS_PER_B * CT + START)
                residual(b, 0, 1, CH_ROWS)
                with sp.Fori(1, NCH) as s:
                    residual(b, s, 0, CH_ROWS)
                residual(b, NCH, 0, 1)
            sp.wait_ge(out_sent, B * TAIL_STRIPS * CT * 16 + START)

        @block.gpsimd
        def _(pool):
            for q in (h_done, shift_done, hs_zero):
                pool.sem_inc(q, START)
            nc.gpsimd.memset(qd[:], 0.0).then_inc(pads_zero, 1)
            nc.gpsimd.memset(acc[:], 0.0).then_inc(pads_zero, 1)
            pool.wait_ge(setup_v, 1)
            pool.wait_ge(setup_p, 2)
            nc.gpsimd.memset(n1p[:], 0.0).then_inc(pads_zero, 1)
            pool.wait_ge(pads_zero, 3)

            def settle():
                pool.sem_inc(pool_passed, 1)

            def affine1(b, m, s):
                n = (b * NCH + s) * HT + m
                pool.wait_ge(gelu1_done, n + 1 + START)
                settle()
                nc.gpsimd.tensor_scalar(hs[:, m, 2:KB, 1:W + 1], gt[m % 2].rearrange("p (r w) -> p r w", r=CH_ROWS),
                                        hs1[:, m:m + 1], HV["mlp_bn1_b"][:, m:m + 1], ALU.mult, ALU.add).then_inc(h_done, 1)

            def shift(b, m, s):
                n = (b * NCH + s) * HT + m
                pool.wait_ge(tap_done, ((b * TAIL_STRIPS + s) * HT + m + 1) * 9 + START)
                settle()
                nc.gpsimd.tensor_copy(hs[:, m, 0:2, 1:W + 1], hs[:, m, CH_ROWS:KB, 1:W + 1]).then_inc(shift_done, 1)

            def strip(b, s):
                for m in range(HT):
                    if isinstance(s, int):
                        pass
                    else:
                        pool.wait_ge(shift_done, (b * NCH + s) * HT + START)
                    affine1(b, m, s)
                    if m >= 1:
                        shift(b, m - 1, s)
                shift(b, HT - 1, s)

            with pool.Fori(0, B) as b:
                pool.wait_ge(init_ready, (b + 1) * NCH + START)
                pool.wait_ge(var_ready, (b + 1) * NCH + START)
                settle()
                nc.gpsimd.memset(hs, 0.0).then_inc(hs_zero, 1)
                pool.wait_ge(hs_zero, b * 2 + 1 + START)
                strip(b, 0)
                with pool.Fori(1, NCH) as s:
                    strip(b, s)
                pool.wait_ge(shift_done, (b + 1) * NCH * HT + START)
                settle()
                nc.gpsimd.memset(hs[:, :, 2:3, :], 0.0).then_inc(hs_zero, 1)

        @block.tensor
        def _(pe):
            for q in (cen_ready, var_ready, conv_ready, init_ready, group_ready, pool_ready, tbias_ready, qk_ready,
                      v_ready, s_ready, mt_ready, st_ready, pv_ready, at_ready, comp_ready, cen2_ready, var2_ready,
                      c1_ready, c2_ready):
                pe.sem_inc(q, START)
            mm = nc.tensor.matmul
            pe.wait_ge(w_in, 10 * 16)
            for i in range(3):
                for j in range(PAIRS):
                    for hp in range(2):
                        a = (2 * j + hp) * HD
                        for k in range(CT):
                            last = mm(bank[i][j * HD:(j + 1) * HD, hp * C:(hp + 1) * C], pr_w[:, i, k, a:a + HD],
                                      tr_w[:, 2 * (i + 1) + k, :], start=(k == 0), stop=(k == CT - 1))
            last.then_inc(setup_p, 1)
            for t in range(CT):
                n = 0
                for i in range(3):
                    for k in range(CT):
                        last = mm(bank[3][:, t:t + 1], tr_w[:, 2 * (i + 1) + k, t * P:(t + 1) * P],
                                  V[f"proj{i + 1}_b"][:, k:k + 1], start=(n == 0), stop=(n == 5))
                        n += 1
            for m in range(HT):
                for k in range(CT):
                    mm(bank[4][:, m:m + 1], c1_w[:, k, m * P:(m + 1) * P], V["ln2_b"][:, k:k + 1],
                       start=(k == 0), stop=(k == CT - 1))
            for t in range(CT):
                for m in range(HT):
                    last = mm(bank[5][:, t:t + 1], c2_w[:, m, t * P:(t + 1) * P], HV["mlp_bn2_b"][:, m:m + 1],
                              start=(m == 0), stop=(m == HT - 1))
            last.then_inc(setup_p, 1)
            pe.wait_ge(setup_v, 3)
            pe.wait_ge(pads_zero, 3)

            def gn_and_pool(b):
                pe.wait_ge(stats, b + 1 + START)
                mm(bank[7][:, 0:4], groupm, gstat, start=True, stop=True).then_inc(group_ready, 1)
                pe.wait_ge(g_ready, b + 1 + START)
                pe.wait_ge(pw_in, (b + 1) * 32)
                for t in range(CT):
                    for k in range(CT):
                        last = mm(bank[7][:, 8 + t:9 + t], pool_w[:, k, t * P:(t + 1) * P], pg[:, k:k + 1],
                                  start=(k == 0), stop=(k == CT - 1))
                last.then_inc(pool_ready, 1)
                pe.wait_ge(pool_done, b + 1 + START)
                for t in range(CT):
                    for k in range(CT):
                        last = mm(bank[7][:, 16 + t:17 + t], t4_w[:, k, t * P:(t + 1) * P], pv_[:, k:k + 1],
                                  start=(k == 0), stop=(k == CT - 1))
                last.then_inc(tbias_ready, 1)

            def front(b, c):
                n = b * NCH + c
                gc = [g[:, k, bass.ds(c * CHUNK, CHUNK)] for k in range(CT)]
                pe.wait_ge(n_done, n + START)
                for t in range(CT):
                    for k in range(CT):
                        last = mm(bank[t][:, :], cdiag if t == k else coff, gc[k], start=(k == 0), stop=(k == CT - 1))
                last.then_inc(cen_ready, 1)
                pe.wait_ge(xc_done, n + START)
                for t in range(CT):
                    for k in range(CT):
                        last = mm(bank[3 + t][:, :], conv_w[:, k, t * P:(t + 1) * P], gc[k], start=(k == 0), stop=(k == CT - 1))
                last.then_inc(conv_ready, 1)
                pe.wait_ge(sq_done, n + 1 + START)
                pe.wait_ge(std_done, n + START)
                for k in range(CT):
                    last = mm(bank[2][:, :], meanm, sq[:, k, :], start=(k == 0), stop=(k == CT - 1))
                last.then_inc(var_ready, 1)
                pe.wait_ge(acc_init, n + START)
                for t in range(CT):
                    for k in range(CT):
                        mm(bank[5 + t][:, :], tsum_w[:, k, t * P:(t + 1) * P], gc[k], start=(k == 0), stop=False)
                pe.wait_ge(xc_done, n + 1 + START)
                for t in range(CT):
                    for k in range(CT):
                        last = mm(bank[5 + t][:, :], t0_w[:, k, t * P:(t + 1) * P], xc[:, k, :], start=False, stop=(k == CT - 1))
                last.then_inc(init_ready, 1)

            def strip(b, s, r):
                sc = b * STRIPS_PER_B + STRIP_BASE[r] + s
                nb = len(BLOCKS[r])
                bc0 = b * BLOCKS_PER_B + BLOCK_BASE[r] + s * nb
                wr = qkv_w[:, r - 1]
                def inner(k, i0, i1):
                    return nbk[:, k, i0:i1, :].rearrange("p i (y x) -> p i y x", y=KB)[:, :, 1:1 + QB, 1:1 + QB]

                pe.wait_ge(strip_in, sc + 1 + START)
                pe.wait_ge(at_copied, bc0 + START)
                for t in range(CT):
                    for k in range(CT):
                        last = mm(bank[t][:, :], wr[:, k, t * P:(t + 1) * P], inner(k, 0, 8), start=(k == 0), stop=(k == CT - 1))
                    last.then_inc(qk_ready, 1)
                for half in range(2):
                    i0, i1 = halves(nb)[half]
                    for t in range(CT):
                        for k in range(CT):
                            last = mm(bank[4 + t + 2 * half][:, 0:(i1 - i0) * NK], wr[:, k, C + t * P:C + (t + 1) * P],
                                      nbk[:, k, i0:i1, :].rearrange("p i n -> p (i n)"), start=(k == 0), stop=(k == CT - 1))
                        if half == 1 and nb > 8:
                            for k in range(CT):
                                last = mm(bank[4 + t + 2 * half][:, 448:512], wr[:, k, t * P:(t + 1) * P], inner(k, 8, 9),
                                          start=(k == 0), stop=(k == CT - 1))
                        last.then_inc(qk_ready, 1)
                pe.wait_ge(acc_added, sc * CT + START)

                def values(i):
                    if i >= 1:
                        pe.wait_ge(v_copied, bc0 + i + START)
                    for k in range(CT):
                        last = mm(bank[2][0:NK, 0:C], nbk[:, k, i, :], wr[:, k, 2 * C:3 * C],
                                  start=(k == 0), stop=(k == CT - 1))
                    last.then_inc(v_ready, 1)

                def scores(i):
                    if i == 0:
                        pe.wait_ge(dq_done, sc + 1 + START)
                        pe.wait_ge(aq_done, sc + 1 + START)
                    if i >= 2:
                        pe.wait_ge(max_done, bc0 + i - 1 + START)
                    mm(bank[i % 2][:, 0:4 * NK], pair_b[:], mask_b[:], start=True, stop=False)
                    for j in range(PAIRS):
                        t, u = j // 2, j % 2
                        last = mm(bank[i % 2][:, j * NK:(j + 1) * NK],
                                  qd[:, t, i, 2 * u:2 * u + 2, :].rearrange("p h q -> p (h q)"), ks[:, t, i, :], start=False, stop=(j == PAIRS - 1))
                    last.then_inc(s_ready, 1)

                def turn_max(i):
                    pe.wait_ge(max_done, bc0 + i + 1 + START)
                    if i >= 1:
                        pe.wait_ge(mt_copied, bc0 + i + START)
                    nc.tensor.transpose(bank[3][0:PAIRS, 0:P // 2].bitcast(BF16), mx[:, i % 2, :], identb[:]).then_inc(mt_ready, 1)

                def scores_t(i):
                    bk = bank[4 + i % 2]
                    pe.wait_ge(mt_copied, bc0 + i + 1 + START)
                    if i >= 2:
                        pe.wait_ge(exp_done, bc0 + i - 1 + START)
                    for t in range(CT):
                        mm(bk[0:NK, t * 256:(t + 1) * 256], ks[:, t, i, :], qd[:, t, i].rearrange("p h q -> p (h q)"),
                           start=(t == 0), stop=False)
                    for j in range(PAIRS):
                        last = mm(bk[0:NK, j * P:(j + 1) * P], left_b[:, j, :], right_b[:, i % 2, :], start=False, stop=(j == PAIRS - 1))
                    last.then_inc(st_ready, 1)

                def weigh(i):
                    pe.wait_ge(exp_done, bc0 + i + 1 + START)
                    if i >= 1:
                        pe.wait_ge(norm_done, bc0 + i + START)
                    for j in range(PAIRS):
                        last = mm(bank[6][:, j * 65:(j + 1) * 65], pb[i % 2][:, j * P:(j + 1) * P], vb[i % 3][:, j, :], start=True, stop=True)
                    last.then_inc(pv_ready, 1)

                def turn_out(i):
                    pe.wait_ge(norm_done, bc0 + i + 1 + START)
                    if i >= 1:
                        pe.wait_ge(at_copied, bc0 + i + START)
                    nc.tensor.transpose(bank[7][:, 0:P], an[:, i % 2].rearrange("p j c -> p (j c)"), ident).then_inc(at_ready, 1)

                for i in range(nb + 3):
                    if i < nb:
                        values(i)
                        scores(i)
                    if 0 <= i - 1 < nb:
                        turn_max(i - 1)
                    if 0 <= i - 2 < nb:
                        weigh(i - 2)
                    if 0 <= i - 3 < nb:
                        turn_out(i - 3)
                    if 0 <= i - 1 < nb:
                        scores_t(i - 1)
                pe.wait_ge(at_copied, bc0 + nb + START)
                for t in range(CT):
                    for hp in range(2):
                        last = mm(bank[2 + t][:, :], comp_w[:, r - 1, hp, t * P:(t + 1) * P],
                                  attn[:, hp].rearrange("p r w -> p (r w)"), start=(hp == 0), stop=(hp == 1))
                    last.then_inc(comp_ready, 1)

            def tail(b, s, k0, k1, fresh):
                n = b * NCH + s
                f = b * TAIL_STRIPS + s
                tc = [acc[:, k, bass.ds(s * CH_ROWS, CH_ROWS), :] for k in range(CT)] if fresh else None
                if fresh:
                    pe.wait_ge(t_done, n + 1 + START)
                    pe.wait_ge(n2_done, n + START)
                    for t in range(CT):
                        for k in range(CT):
                            last = mm(bank[t][:, :], cdiag if t == k else coff, tc[k], start=(k == 0), stop=(k == CT - 1))
                    last.then_inc(cen2_ready, 1)
                    pe.wait_ge(sq2_done, n + 1 + START)
                    pe.wait_ge(std2_done, n + START)
                    for k in range(CT):
                        last = mm(bank[2][:, :], meanm, sq[:, k, :], start=(k == 0), stop=(k == CT - 1))
                    last.then_inc(var2_ready, 1)
                    pe.wait_ge(n2_done, n + 1 + START)

                def up(m):
                    q = n * HT + m
                    if m >= 2:
                        pe.wait_ge(gelu1_done, q - 1 + START)
                    for k in range(CT):
                        last = mm(bank[3 + m % 2][:, :], c1_w[:, k, m * P:(m + 1) * P], nt[:, k, :], start=(k == 0), stop=(k == CT - 1))
                    last.then_inc(c1_ready, 1)

                def down(m):
                    q = f * HT + m
                    pe.wait_ge(gelu2_done, q + 1 + START)
                    if m == 0:
                        pe.wait_ge(res_done, f * CT + START)
                    for t in range(CT):
                        last = mm(bank[5 + t][:, k0 * W:k1 * W], c2_w[:, m, t * P:(t + 1) * P], h2[m % 2][:, k0 * W:k1 * W],
                                  start=(m == 0), stop=(m == HT - 1))
                    last.then_inc(c2_ready, 1)
                if fresh:
                    up(0)
                for m in range(HT):
                    if fresh and m + 1 < HT:
                        up(m + 1)
                    if m >= 1:
                        down(m - 1)
                down(HT - 1)

            with pe.Fori(0, B) as b:
                gn_and_pool(b)
                with pe.Fori(0, NCH) as c:
                    front(b, c)
                pe.wait_ge(acc_init, (b + 1) * NCH + START)
                pe.sem_inc(pe_passed, 1)
                for r in (1, 2, 3):
                    with pe.Fori(0, STRIPS[r]) as s:
                        strip(b, s, r)
                pe.wait_ge(acc_added, (b + 1) * STRIPS_PER_B * CT + START)
                tail(b, 0, 1, CH_ROWS, True)
                with pe.Fori(1, NCH) as s:
                    tail(b, s, 0, CH_ROWS, True)
                tail(b, NCH, 0, 1, False)

        @block.vector
        def _(dve):
            for q in (stats, g_ready, pool_done, tb3_done, rs_done, n_done, acc_init, strip_in, dq_done, max_done,
                      mt_copied, rec_done, norm_done, at_copied, acc_added, tap_done, res_done, fin_done, rs2_done,
                      n2_done):
                dve.sem_inc(q, START)
            v = nc.vector
            dve.wait_ge(w_in, 10 * 16)
            nchain = [0]

            def link(ins):
                nchain[0] += 1
                ins.then_inc(gn_chain, 1)
                dve.wait_ge(gn_chain, nchain[0])

            def cc(name):
                a, e = CO[name]
                return cst[:, a:e]
            v.memset(eps, EPS)
            for i, n in enumerate(("ident", "cdiag", "coff", "mean", "group")):
                v.tensor_copy(matc[:, i, :], cc(n))
            v.tensor_copy(identb[:], cc("ident"))
            v.tensor_copy(pair_b[:], cc("pairI")[0:NQ, :])
            v.tensor_copy(mask_b[:], cc("mask")[0:NQ, :])
            v.tensor_copy(left_b[:].rearrange("p j n -> p (j n)"), cc("left")[0:96, :])
            for i in range(2):
                v.tensor_copy(right_b[:, i, :], cc("right")[0:96, :])
            v.tensor_copy(t0_w[:].rearrange("p k c -> p (k c)"), tr_w[:, 0:2, :].rearrange("p k c -> p (k c)"))
            link(v.tensor_tensor(tsum_w[:], tr_w[:, 2:4, :], tr_w[:, 4:6, :], ALU.add))
            v.tensor_tensor(tsum_w[:], tsum_w[:], tr_w[:, 6:8, :], ALU.add).then_inc(setup_v, 1)
            for dst, n in ((s1, "tc_bn1_g"), (s2, "tc_bn2_g"), (s3, "tc_bn3_g"), (f3, "mlp_bn3_g")):
                v.tensor_scalar(dst, V[n], BN_SCALE, None, ALU.mult)
            v.tensor_scalar(hs1, HV["mlp_bn1_g"], BN_SCALE, None, ALU.mult)
            link(v.tensor_scalar(hs2, HV["mlp_bn2_g"], BN_SCALE, None, ALU.mult))
            link(v.tensor_tensor(b1c, s1, V["tc_conv_b"], ALU.mult))
            link(v.tensor_tensor(b1c, b1c, V["tc_bn1_b"], ALU.add))
            dve.wait_ge(setup_p, 2)
            for i in range(3):
                v.tensor_copy(comp_w[:, i].rearrange("p e c -> p (e c)"), bank[i][:, :])
            v.tensor_tensor(bias0, bank[3][:, 0:CT], V["tc_trans_b"], ALU.add)
            v.tensor_tensor(hb, bank[4][:, 0:HT], HV["mlp_c1_b"], ALU.add)
            link(v.tensor_tensor(fb, bank[5][:, 0:CT], V["mlp_c2_b"], ALU.add))
            link(v.tensor_tensor(fb, fb, f3, ALU.mult))
            link(v.tensor_tensor(fb, fb, V["mlp_bn3_b"], ALU.add))
            for k in range(CT):
                v.tensor_scalar(c1_w[:, k, :], c1_w[:, k, :], V["ln2_w"][:, k:k + 1], None, ALU.mult)
            for m in range(HT):
                v.tensor_scalar(c2_w[:, m, :], c2_w[:, m, :], hs2[:, m:m + 1], None, ALU.mult)
            v.tensor_scalar(dw_w[:, :, 4:5], dw_w[:, :, 4:5], 1.0, None, ALU.add).then_inc(setup_v, 2)
            dve.wait_ge(setup_v, 3)
            SETUP = nchain[0]
            assert SETUP == SETUP_LINKS
            PER_B = [0]

            def group_norm(b):
                cnt = [0]

                def step(ins):
                    cnt[0] += 1
                    ins.then_inc(gn_chain, 1)
                    dve.wait_ge(gn_chain, b * GN_STEPS + (SETUP + cnt[0]))
                dve.wait_ge(x_in, (b + 1) * CT * 16)
                for t in range(CT):
                    for c in range(NCH):
                        last = v.bn_stats(st[:, t, c, :], g[:, t, c * CHUNK:(c + 1) * CHUNK])
                step(last)
                dve.sem_inc(dve_passed, 1)
                for t in range(CT):
                    last = v.bn_aggr(mv[:, t, :], st[:, t, :, :])
                step(last)
                v.tensor_copy(gstat[:, 0:2], mv[:, :, 0])
                step(v.tensor_tensor(gt2, mv[:, :, 0], mv[:, :, 0], ALU.mult))
                v.tensor_tensor(gstat[:, 2:4], gt2, mv[:, :, 1], ALU.add).then_inc(stats, 1)
                dve.wait_ge(group_ready, b + 1 + START)
                step(v.tensor_copy(gm, bank[7][:, 0:2]))
                step(v.tensor_tensor(gt2, gm, gm, ALU.mult))
                step(v.scalar_tensor_tensor(gt2, bank[7][:, 2:4], EPS, gt2, ALU.add, ALU.subtract))
                dve.wait_ge(gstd_done, b + 1 + START)
                step(v.reciprocal(gr, gsd))
                step(v.tensor_tensor(gnb, gm, gr, ALU.mult))
                v.tensor_tensor(pin, mv[:, :, 0], gm, ALU.subtract)
                for t in range(CT):
                    last = v.tensor_scalar(g[:, t, :], g[:, t, :], gr[:, t:t + 1], gnb[:, t:t + 1], ALU.mult, ALU.subtract)
                step(last)
                v.tensor_tensor(pg, pin, gr, ALU.mult).then_inc(g_ready, 1)
                dve.wait_ge(pool_ready, b + 1 + START)
                step(v.tensor_tensor(pv_, bank[7][:, 8:10], s2, ALU.mult))
                step(v.tensor_tensor(pv_, pv_, V["tc_bn2_b"], ALU.add))
                v.tensor_scalar(pv_, pv_, 0.0, None, ALU.max).then_inc(pool_done, 1)
                dve.wait_ge(tbias_ready, b + 1 + START)
                step(v.tensor_tensor(tb3, bank[7][:, 16:18], bias0, ALU.add))
                step(v.tensor_tensor(tb3, tb3, s3, ALU.mult))
                v.tensor_tensor(tb3, tb3, V["tc_bn3_b"], ALU.add).then_inc(tb3_done, 1)
                return cnt[0]

            GN_STEPS = 13

            def front(b, c):
                n = b * NCH + c
                dve.wait_ge(std_done, n + 1 + START)
                v.reciprocal(rstd, std).then_inc(rs_done, 1)
                dve.wait_ge(rs_done, n + 1 + START)
                dve.wait_ge(n1_done, n * CT + START)
                for t in range(CT):
                    last = v.tensor_tensor(nt[:, t, :], bank[t][:, :], rstd, ALU.mult)
                last.then_inc(n_done, 1)
                dve.wait_ge(init_ready, n + 1 + START)
                for t in range(CT):
                    last = v.tensor_copy(acc[:, t, bass.ds(c * CH_ROWS, CH_ROWS), :], bank[5 + t][:, :].rearrange("p (r w) -> p r w", r=CH_ROWS))
                last.then_inc(acc_init, 1)

            def strip(b, s, row0, r):
                sc = b * STRIPS_PER_B + STRIP_BASE[r] + s
                nb = len(BLOCKS[r])
                bc0 = b * BLOCKS_PER_B + BLOCK_BASE[r] + s * nb
                dve.wait_ge(v_ready, bc0 + START)
                for k in range(CT):
                    for i0, n, c0, d in runs_of(r):
                        for i in range(n):
                            a = c0 + i * d + HALO - r
                            last = v.tensor_copy(nbk[:, k, i0 + i, :].rearrange("p (y x) -> p y x", y=KB),
                                                 n1p[:, k, bass.ds(row0 + HALO - r, KB, r), a:a + (KB - 1) * r + 1:r])
                last.then_inc(strip_in, 1)
                dve.wait_ge(qk_ready, sc * 6 + 1 + START)
                for h in range(4):
                    hp = slice(HD * h, HD * h + HD)
                    v.tensor_copy(qd[hp, 0, 0:8, h, :], bank[0][hp, :].rearrange("p (i q) -> p i q", q=NQ))
                for half in range(2):
                    i0, i1 = halves(nb)[half]
                    dve.wait_ge(qk_ready, sc * 6 + 3 + 2 * half + START)
                    last = v.tensor_copy(ks[:, 0, i0:i1, :].rearrange("p i n -> p (i n)"), bank[4 + 2 * half][:, 0:(i1 - i0) * NK])
                if nb > 8:
                    for h in range(4):
                        hp = slice(HD * h, HD * h + HD)
                        last = v.tensor_copy(qd[hp, 0, 8, h, :], bank[6][hp, 448:512])
                last.then_inc(dq_done, 1)

                def take_max(i):
                    dve.wait_ge(s_ready, bc0 + i + 1 + START)
                    if i >= 2:
                        dve.wait_ge(mt_ready, bc0 + i - 1 + START)
                    v.tensor_reduce(mx[:, i % 2, :], bank[i % 2][:, 0:4 * NK].rearrange("p (j n) -> p j n", j=PAIRS), AX_X, ALU.max).then_inc(max_done, 1)

                def copy_max(i):
                    dve.wait_ge(mt_ready, bc0 + i + 1 + START)
                    if i >= 2:
                        dve.wait_ge(st_ready, bc0 + i - 1 + START)
                    v.tensor_copy(right_b[0:PAIRS, i % 2, :], bank[3][0:PAIRS, 0:P // 2].bitcast(BF16)).then_inc(mt_copied, 1)

                def normalise(i):
                    dve.wait_ge(pv_ready, bc0 + i + 1 + START)
                    o_ = bank[6][:, 0:PAIRS * 65].rearrange("p (j c) -> p j c", j=PAIRS)
                    v.reciprocal(rec[:, i % 2, :], o_[:, :, 64]).then_inc(rec_done, 1)
                    dve.wait_ge(rec_done, bc0 + i + 1 + START)
                    if i >= 2:
                        dve.wait_ge(at_ready, bc0 + i - 1 + START)
                    for hp in range(2):
                        q = slice(NQ * hp, NQ * hp + NQ)
                        last = v.tensor_tensor(an[q, i % 2], o_[q, :, HD * hp:HD * hp + HD],
                                               rec[q, i % 2, :].unsqueeze(2).to_broadcast([NQ, PAIRS, HD]), ALU.mult)
                    last.then_inc(norm_done, 1)

                def copy_out(i):
                    c0, skip = BLOCKS[r][i]
                    dve.wait_ge(at_ready, bc0 + i + 1 + START)
                    if i == 0:
                        dve.wait_ge(comp_ready, sc * CT + START)
                    c0, skip = BLOCKS[r][i]
                    a = c0 + skip * r
                    v.tensor_copy(attn[:, :, :, a:c0 + (QB - 1) * r + 1:r],
                                  bank[7][:, 0:P].rearrange("p (e y x) -> p e y x", e=2, y=QB)[:, :, :, skip:]).then_inc(at_copied, 1)

                for i in range(nb + 3):
                    if 0 <= i - 1 < nb and i - 1 >= 0:
                        pass
                    if i < nb:
                        take_max(i)
                    if 0 <= i - 1 < nb:
                        copy_max(i - 1)
                    if 0 <= i - 2 < nb:
                        normalise(i - 2)
                    if 0 <= i - 3 < nb:
                        copy_out(i - 3)
                for t in range(CT):
                    dve.wait_ge(comp_ready, sc * CT + t + 1 + START)
                    dve.wait_ge(acc_added, sc * CT + t + START)
                    a = acc[:, t, bass.ds(row0, QB, r), :]
                    v.tensor_tensor(a, bank[2 + t][:, :].rearrange("p (r w) -> p r w", r=QB), a, ALU.add).then_inc(acc_added, 1)

            def tail(b, s, k0, k1, fresh):
                n = b * NCH + s
                f = b * TAIL_STRIPS + s
                if fresh:
                    dve.wait_ge(std2_done, n + 1 + START)
                    v.reciprocal(rstd, std).then_inc(rs2_done, 1)
                    dve.wait_ge(rs2_done, n + 1 + START)
                    dve.wait_ge(c1_ready, n * HT + START)
                    for t in range(CT):
                        last = v.tensor_tensor(nt[:, t, :], bank[t][:, :], rstd, ALU.mult)
                    last.then_inc(n2_done, 1)
                for m in range(HT):
                    q = f * HT + m
                    if fresh:
                        dve.wait_ge(h_done, n * HT + m + 1 + START)
                    elif m == 0:
                        dve.wait_ge(hs_zero, b * 2 + 2 + START)
                    if m >= 2:
                        dve.wait_ge(gelu2_done, q - 1 + START)
                    else:
                        dve.wait_ge(gelu2_done, f * HT + START)
                    cvm = cv[m % 2][:, k0 * W:k1 * W].rearrange("p (r w) -> p r w", r=k1 - k0)
                    for k in range(9):
                        win = hs[:, m, k0 + k // 3:k1 + k // 3, k % 3:k % 3 + W]
                        if k == 0:
                            v.tensor_scalar(cvm, win, dw_w[:, m, 0:1], HV["mlp_dw_b"][:, m:m + 1], ALU.mult, ALU.add).then_inc(tap_done, 1)
                        else:
                            dve.wait_ge(tap_done, q * 9 + k + START)
                            v.scalar_tensor_tensor(cvm, win, dw_w[:, m, k:k + 1], cvm, ALU.mult, ALU.add).then_inc(tap_done, 1)
                dve.wait_ge(c2_ready, (f + 1) * HT + START)
                for t in range(CT):
                    o_ = obv[:, t, k0:k1, :]
                    dve.wait_ge(out_sent, f * CT * 16 + START)
                    v.scalar_tensor_tensor(o_, bank[5 + t][:, k0 * W:k1 * W].rearrange("p (r w) -> p r w", r=k1 - k0), f3[:, t:t + 1],
                                           acc[:, t, bass.ds(s * CH_ROWS - 1 + k0, k1 - k0), :], ALU.mult, ALU.add).then_inc(res_done, 1)
                dve.wait_ge(xr_in, (f + 1) * CT * 16)
                for t in range(CT):
                    o_ = obv[:, t, k0:k1, :]
                    dve.wait_ge(res_done, f * CT + t + 1 + START)
                    v.scalar_tensor_tensor(o_, o_, fb[:, t:t + 1], xr[:, t, k0:k1, :], ALU.add, ALU.add).then_inc(fin_done, 1)

            with dve.Fori(0, B) as b:
                assert group_norm(b) == GN_STEPS
                with dve.Fori(0, NCH) as c:
                    front(b, c)
                dve.wait_ge(n1_done, (b + 1) * NCH * CT + START)
                dve.wait_ge(init_ready, (b + 1) * NCH + START)
                dve.wait_ge(acc_init, (b + 1) * NCH + START)
                for i in range(3):
                    v.memset(vb[i][:, :, 64:65], 1.0)
                with dve.Fori(0, STRIPS[1]) as s:
                    strip(b, s, s * QB, 1)
                with dve.Fori(0, 4) as by:
                    with dve.Fori(0, 2) as py:
                        strip(b, by * 2 + py, by * (2 * QB) + py, 2)
                with dve.Fori(0, 3) as by:
                    with dve.Fori(0, 3) as py:
                        strip(b, by * 3 + py, by * (3 * QB) + py, 3)
                tail(b, 0, 1, CH_ROWS, True)
                with dve.Fori(1, NCH) as s:
                    tail(b, s, 0, CH_ROWS, True)
                tail(b, NCH, 0, 1, False)

        @block.scalar
        def _(act):
            for q in (gstd_done, sq_done, xc_done, std_done, n1_done, aq_done, v_copied, exp_done, gelu1_done,
                      gelu2_done, t_done, sq2_done, std2_done):
                act.sem_inc(q, START)
            fn = nc.scalar.activation
            act.wait_ge(setup_v, 3)

            def group_std(b):
                act.wait_ge(gn_chain, b * 13 + GN_BASE + 6)
                fn(gsd, gt2, ACT.Sqrt).then_inc(gstd_done, 1)

            def front(b, c):
                n = b * NCH + c
                act.wait_ge(cen_ready, n + 1 + START)
                act.wait_ge(var_ready, n + START)
                for t in range(CT):
                    last = fn(sq[:, t, :], bank[t][:, :], ACT.Square)
                last.then_inc(sq_done, 1)
                act.wait_ge(conv_ready, n + 1 + START)
                act.wait_ge(init_ready, n + START)
                for t in range(CT):
                    last = fn(xc[:, t, :], bank[3 + t][:, :], ACT.Relu, bias=b1c[:, t:t + 1], scale=s1[:, t:t + 1])
                last.then_inc(xc_done, 1)
                act.wait_ge(var_ready, n + 1 + START)
                act.wait_ge(rs_done, n + START)
                fn(std, bank[2][:, :], ACT.Sqrt, bias=eps).then_inc(std_done, 1)
                act.wait_ge(n_done, n + 1 + START)
                act.wait_ge(pads_zero, 3)
                for t in range(CT):
                    fn(n1p[:, t, bass.ds(c * CH_ROWS + HALO, CH_ROWS), HALO:HALO + W],
                       nt[:, t, :].rearrange("p (r w) -> p r w", r=CH_ROWS), ACT.Identity,
                       scale=V["ln1_w"][:, t:t + 1], bias=V["ln1_b"][:, t:t + 1]).then_inc(n1_done, 1)

            def strip(b, s, r):
                sc = b * STRIPS_PER_B + STRIP_BASE[r] + s
                nb = len(BLOCKS[r])
                bc0 = b * BLOCKS_PER_B + BLOCK_BASE[r] + s * nb
                act.wait_ge(qk_ready, sc * 6 + 2 + START)
                for h in range(4):
                    hp = slice(HD * h, HD * h + HD)
                    fn(qd[hp, 1, 0:8, h, :], bank[1][hp, :].rearrange("p (i q) -> p i q", q=NQ), ACT.Copy)
                for half in range(2):
                    i0, i1 = halves(nb)[half]
                    act.wait_ge(qk_ready, sc * 6 + 4 + 2 * half + START)
                    last = fn(ks[:, 1, i0:i1, :].rearrange("p i n -> p (i n)"), bank[5 + 2 * half][:, 0:(i1 - i0) * NK], ACT.Copy)
                if nb > 8:
                    for h in range(4):
                        hp = slice(HD * h, HD * h + HD)
                        last = fn(qd[hp, 1, 8, h, :], bank[7][hp, 448:512], ACT.Copy)
                last.then_inc(aq_done, 1)

                def copy_v(i):
                    act.wait_ge(v_ready, bc0 + i + 1 + START)
                    if i >= 3:
                        act.wait_ge(pv_ready, bc0 + i - 2 + START)
                    fn(vb[i % 3][:, :, 0:64], bank[2][0:NK, 0:C].rearrange("p (j c) -> p j c", j=PAIRS), ACT.Copy).then_inc(v_copied, 1)

                def exps(i):
                    act.wait_ge(st_ready, bc0 + i + 1 + START)
                    if i >= 2:
                        act.wait_ge(pv_ready, bc0 + i - 1 + START)
                    fn(pb[i % 2], bank[4 + i % 2][0:NK, :], ACT.Exp, scale=HD ** -0.5).then_inc(exp_done, 1)

                for i in range(nb + 1):
                    if i < nb:
                        copy_v(i)
                    if i >= 1:
                        exps(i - 1)

            def tail(b, s, k0, k1, fresh):
                n = b * NCH + s
                f = b * TAIL_STRIPS + s
                if fresh:
                    if isinstance(s, int):
                        act.wait_ge(acc_added, (b + 1) * STRIPS_PER_B * CT + START)
                        act.wait_ge(tb3_done, b + 1 + START)
                    for t in range(CT):
                        a = acc[:, t, bass.ds(s * CH_ROWS, CH_ROWS), :]
                        last = fn(a, a, ACT.Relu, bias=tb3[:, t:t + 1], scale=s3[:, t:t + 1])
                    last.then_inc(t_done, 1)
                    act.wait_ge(cen2_ready, n + 1 + START)
                    act.wait_ge(var2_ready, n + START)
                    for t in range(CT):
                        last = fn(sq[:, t, :], bank[t][:, :], ACT.Square)
                    last.then_inc(sq2_done, 1)
                    act.wait_ge(var2_ready, n + 1 + START)
                    act.wait_ge(rs2_done, n + START)
                    fn(std, bank[2][:, :], ACT.Sqrt, bias=eps).then_inc(std2_done, 1)

                def gelu1(m):
                    q = n * HT + m
                    act.wait_ge(c1_ready, q + 1 + START)
                    if m >= 2:
                        act.wait_ge(h_done, q - 1 + START)
                    else:
                        act.wait_ge(h_done, n * HT + START)
                    if isinstance(s, int) and m == 0:
                        act.wait_ge(hs_zero, b * 2 + 1 + START)
                    fn(gt[m % 2], bank[3 + m % 2][:, :], ACT.Gelu, bias=hb[:, m:m + 1]).then_inc(gelu1_done, 1)

                def gelu2(m):
                    q = f * HT + m
                    act.wait_ge(tap_done, (q + 1) * 9 + START)
                    if m >= 2:
                        act.wait_ge(c2_ready, q - 1 + START)
                    fn(h2[m % 2][:, k0 * W:k1 * W], cv[m % 2][:, k0 * W:k1 * W], ACT.Gelu).then_inc(gelu2_done, 1)

                if fresh:
                    gelu1(0)
                for m in range(HT):
                    if fresh and m + 1 < HT:
                        gelu1(m + 1)
                    gelu2(m)

            GN_BASE = SETUP_LINKS
            with act.Fori(0, B) as b:
                group_std(b)
                with act.Fori(0, NCH) as c:
                    front(b, c)
                for r in (1, 2, 3):
                    with act.Fori(0, STRIPS[r]) as s:
                        strip(b, s, r)
                tail(b, 0, 1, CH_ROWS, True)
                with act.Fori(1, NCH) as s:
                    tail(b, s, 0, CH_ROWS, True)
                tail(b, NCH, 0, 1, False)


SETUP_LINKS = 7


def constants():
    import numpy as np
    c = np.zeros((P, CONST_COLS), np.float32)

    def put(name, a):
        c[:a.shape[0], CO[name][0]:CO[name][0] + a.shape[1]] = a
    eye = np.eye(P, dtype=np.float32)
    put("ident", eye)
    put("cdiag", eye - np.float32(1 / C))
    put("coff", np.full((P, P), -1 / C, np.float32))
    put("mean", np.full((P, P), 1 / C, np.float32))
    per = C // 32
    put("group", np.kron(np.eye(P // per), np.full((per, per), 1 / per)).astype(np.float32))
    i64 = np.eye(NQ, dtype=np.float32)
    put("pairI", np.concatenate([i64, i64], 1))
    mask = np.full((QB, QB, KB, KB), -1e30, np.float32)
    for y in range(QB):
        for x in range(QB):
            mask[y, x, y:y + 3, x:x + 3] = 0
    mask = mask.reshape(NQ, NK)
    put("mask", np.tile(mask, (1, 4)))
    left = np.zeros((96, 4, NK), np.float32)
    for j in range(4):
        left[j, j] = -1
        left[32:96, j] = mask
    put("left", left.reshape(96, 4 * NK))
    right = np.zeros((96, P), np.float32)
    right[32:96] = np.concatenate([i64, i64], 1)
    put("right", right)
    return c


def kernel(**inputs):
    import numpy as np
    import concourse.bacc as bacc
    from concourse import mybir as mb
    from concourse.bass_utils import run_bass_kernel_spmd

    w = {k[len("L0_conv_"):]: np.asarray(a) for k, a in inputs.items() if k != "x"}

    def transposed(a):
        a = np.transpose(a)
        return np.ascontiguousarray(a.reshape(-1, P, a.shape[1]).transpose(1, 0, 2))
    arrays = {
        "x": np.ascontiguousarray(inputs["x"]),
        "wqkv": np.ascontiguousarray(np.stack([transposed(w[f"qkv{i}_w"]) for i in (1, 2, 3)], 1)),
        "wproj": np.ascontiguousarray(np.stack([w[f"proj{i}_w"].reshape(CT, P, C).transpose(1, 0, 2) for i in (1, 2, 3)], 1)),
        "wtrans": transposed(w["tc_trans_w"]),
        "wconv": transposed(w["tc_conv_w"]),
        "wpool": transposed(w["tc_pool_w"]),
        "wc1": transposed(w["mlp_c1_w"]),
        "wc2": transposed(w["mlp_c2_w"]),
        "wdw": np.ascontiguousarray(w["mlp_dw_w"].reshape(HT, P, 9).transpose(1, 0, 2)),
        "vecs": np.ascontiguousarray(np.stack([w[n].reshape(CT, P).T for n in VECS], 1)),
        "hvecs": np.ascontiguousarray(np.stack([w[n].reshape(HT, P).T for n in HVECS], 1)),
        "consts": constants(),
    }
    nc = bacc.Bacc("TRN2", target_bir_lowering=False, num_devices=1)
    feed, args = {}, []
    for name, a in arrays.items():
        feed[f"{name}_dram"] = a
        args.append(nc.dram_tensor(f"{name}_dram", a.shape, mb.dt.from_np(a.dtype), kind="ExternalInput").ap())
    args.append(nc.dram_tensor("out_dram", (B, C, H, W), F32, kind="ExternalOutput").ap())
    build(nc, *args)
    r = run_bass_kernel_spmd(nc, [feed], core_ids=[0])
    return r.results[0]["out_dram"]
```

```python
from contextlib import ExitStack

import concourse.bass as bass
from concourse import mybir

F32 = mybir.dt.float32
BF16 = mybir.dt.bfloat16
F16 = mybir.dt.float16
ALU = mybir.AluOpType
ACT = mybir.ActivationFunctionType
AX_X = mybir.AxisListType.X

B, C, H, W = 4, 256, 64, 64
HID = 4 * C
P = 128
CT = C // P
HT = HID // P
PX = H * W
CH_ROWS = 8
CHUNK = CH_ROWS * W
NCH = H // CH_ROWS
HEADS, HD = 8, C // 8
PAIRS = HEADS // 2
QB, KB = 8, 10
NQ, NK = QB * QB, KB * KB
HALO = 3
EPS = 1e-5
START = 1
BN_SCALE = (1.0 + EPS) ** -0.5
ROWS3 = 3 * 3 * QB
N1H, N1W = ROWS3 + 2 * HALO, W + 2 * HALO

LOOPS = {1: ((2 * QB, 0), (2 * QB, QB), 3), 2: ((2 * QB, 0), (2 * QB, 1), 3), 3: ((3 * QB, 0), (3 * QB, 1), 2)}
REST = {1: (6 * QB, 7 * QB), 2: (6 * QB, 6 * QB + 1), 3: (6 * QB, 6 * QB + 1, 2, 3 * QB + 2, 6 * QB + 2)}


def blocks_of(r):
    out = []
    for px in range(r):
        n = len(range(px, W, r))
        starts = list(range(0, n - QB + 1, QB))
        if starts[-1] + QB < n:
            starts.append(n - QB)
        done = 0
        for s in starts:
            out.append((px + r * s, done - s))
            done = s + QB
    return out


def runs_of(r):
    starts = [c0 for c0, _ in blocks_of(r)]
    out, i = [], 0
    while i < len(starts):
        n, d = 1, QB * r
        while i + n < len(starts) and starts[i + n] - starts[i + n - 1] == d:
            n += 1
        out.append((i, n, starts[i], d))
        i += n
    return out


BLOCKS = {r: blocks_of(r) for r in (1, 2, 3)}
NBMAX = 9
KBANK = 512 // NK
STRIP_BASE = {1: 0, 2: 8, 3: 16}
BLOCK_BASE = {1: 0, 2: 8 * len(BLOCKS[1]), 3: 8 * len(BLOCKS[1]) + 8 * len(BLOCKS[2])}
STRIPS_PER_B = 25
BLOCKS_PER_B = BLOCK_BASE[3] + 9 * len(BLOCKS[3])
TAIL_STRIPS = NCH + 1

PE_TAPS = (1, 2)
V_TAPS = tuple(9 - n for n in PE_TAPS)
STRIP_TAPS = HT // 2 * sum(V_TAPS)


def taps_before(m):
    return m // 2 * sum(V_TAPS) + m % 2 * V_TAPS[0]


VECS = ["ln1_w", "ln1_b", "ln2_w", "ln2_b", "proj1_b", "proj2_b", "proj3_b", "tc_conv_b", "tc_bn1_g", "tc_bn1_b",
        "tc_bn2_g", "tc_bn2_b", "tc_trans_b", "tc_bn3_g", "tc_bn3_b", "mlp_c2_b", "mlp_bn3_g", "mlp_bn3_b"]
HVECS = ["mlp_c1_b", "mlp_bn1_g", "mlp_bn1_b", "mlp_dw_b", "mlp_bn2_g", "mlp_bn2_b"]
CO = {}
_at = 0
for _n, _w in (("ident", P), ("cdiag", P), ("coff", P), ("mean", P), ("group", P), ("pairI", P), ("mask", 4 * NK),
               ("left", 4 * NK), ("right", P)):
    CO[_n] = (_at, _at + _w)
    _at += _w
CONST_COLS = _at


def build(nc, x, wqkv, wproj, wtrans, wconv, wpool, wc1, wc2, wdw, vecs, hvecs, consts, out):
    with ExitStack() as ctx:
        def sb(name, shape, dt=F32):
            return ctx.enter_context(nc.sbuf_tensor(name, shape, dt))

        def sem(name):
            return ctx.enter_context(nc.semaphore(name))

        bank = [ctx.enter_context(nc.psum_tensor(f"bank{i}", [P, 512], F32)) for i in range(8)]

        qkv_w = sb("qkv_w", [P, 2, 3, CT, 3 * C], F16)
        comp_w = sb("comp_w", [P, 3, 2, C])
        conv_w = sb("conv_w", [P, CT, C])
        t0_w = sb("t0_w", [P, CT, C])
        tsum_w = sb("tsum_w", [P, CT, C])
        c1_w = sb("c1_w", [P, 2, CT, HID], F16)
        c2_w = sb("c2_w", [P, HT, C])
        dw_w = sb("dw_w", [P, HT, 9])
        vec = sb("vec", [P, len(VECS), CT])
        hvec = sb("hvec", [P, len(HVECS), HT])
        V = {n: vec[:, i, :] for i, n in enumerate(VECS)}
        HV = {n: hvec[:, i, :] for i, n in enumerate(HVECS)}
        small = sb("small", [P, 48])
        matc = sb("matc", [P, 5, P])
        ident, cdiag, coff, meanm, groupm = (matc[:, i, :] for i in range(5))
        identb = sb("identb", [P, P], BF16)
        pair_b = sb("pair_b", [NQ, P], BF16)
        mask_b = sb("mask_b", [NQ, 4 * NK], BF16)
        left_b = sb("left_b", [96, 4, NK], BF16)
        right_b = sb("right_b", [96, 2, P], BF16)

        g = sb("g", [P, CT, PX])
        n1p = sb("n1p", [P, 2, CT, N1H, N1W], F16)
        acc = sb("acc", [P, CT, ROWS3, W])
        KW = 2 * CT * NBMAX * NK // 2
        QW = 2 * CT * NBMAX * 4 * NQ // 2
        VW = PAIRS * 65
        gflat = g[:].rearrange("p a n -> p (a n)")
        work = sb("work", [P, 3 * KW + 2 * CHUNK + VW])

        def blocks16(a):
            return a.bitcast(F16).rearrange("p (s k i n) -> p s k i n", s=2, k=CT, i=NBMAX)
        qd0 = sb("qd0", [P, QW])
        nbk = [blocks16(work[:, 0:KW]), blocks16(work[:, KW:2 * KW])]
        ks = [blocks16(work[:, 2 * KW:3 * KW]), blocks16(gflat[:, QW:QW + KW])]
        qd = [a.bitcast(F16).rearrange("p (s t i h q) -> p s t i h q", s=2, t=CT, i=NBMAX, h=4) for a in (qd0[:], gflat[:, 0:QW])]
        attn = work[:, 3 * KW:3 * KW + 2 * CHUNK].rearrange("p (a r w) -> p a r w", a=2, r=CH_ROWS)
        o = QW + KW
        pb = [gflat[0:NK, o + i * 512:o + (i + 1) * 512] for i in range(2)]
        o += 2 * 512
        vb = [a.rearrange("p (j c) -> p j c", j=PAIRS) for a in (
            gflat[0:NK, o:o + VW], gflat[0:NK, o + VW:o + 2 * VW], work[0:NK, 3 * KW + 2 * CHUNK:3 * KW + 2 * CHUNK + VW])]
        mx = sb("mx", [P, 2, PAIRS], BF16)
        rec = sb("rec", [P, 2, PAIRS])
        an = sb("an", [P, 2, PAIRS, HD])
        sq = work[:, 0:2 * CHUNK].rearrange("p (a n) -> p a n", a=2)
        std = work[:, 1024:1536]
        rstd = work[:, 1536:2048]
        nt = work[:, 2048:3072].rearrange("p (a n) -> p a n", a=2)
        xc = work[:, 3072:4096].rearrange("p (a n) -> p a n", a=2)
        HSW = W + 2
        hs = gflat[:, 0:HT * KB * HSW].rearrange("p (m r w) -> p m r w", m=HT, r=KB)
        o = HT * KB * HSW
        gt = [gflat[:, o + i * CHUNK:o + (i + 1) * CHUNK] for i in range(2)]; o += 2 * CHUNK
        cv = [gflat[:, o + i * CHUNK:o + (i + 1) * CHUNK] for i in range(2)]; o += 2 * CHUNK
        sq2 = [work[:, i * 1024:(i + 1) * 1024].rearrange("p (a n) -> p a n", a=2) for i in range(2)]
        std2 = [work[:, 2048 + i * 512:2560 + i * 512] for i in range(2)]
        nt2 = [work[:, 3072 + i * 1024:4096 + i * 1024].rearrange("p (a n) -> p a n", a=2) for i in range(2)]
        h2 = [sq[:, i, :] for i in range(2)]
        NDG = HT // 2 * sum(PE_TAPS)
        diag = work[:, 5120:5120 + NDG * P].rearrange("p (n c) -> p n c", n=NDG)
        xr = work[:, 3072:4096].rearrange("p (t r w) -> p t r w", t=CT, r=CH_ROWS)
        obv = work[:, 4096:5120].rearrange("p (t r w) -> p t r w", t=CT, r=CH_ROWS)
        stage = n1p[:].rearrange("p s a r w -> p (s a r w)").bitcast(F32)
        qkv32 = gflat[:, 0:3 * CT * 3 * C].rearrange("p (i k c) -> p i k c", i=3, k=CT)
        pr_w = stage[:, 0:3 * CT * C].rearrange("p (i k c) -> p i k c", i=3, k=CT)
        c132 = gflat[:, 5120:5120 + CT * HID].rearrange("p (k c) -> p k c", k=CT)
        tr_w = stage[:, 1536:1536 + 10 * C].rearrange("p (k c) -> p k c", k=10)
        cst = stage[:, 4096:4096 + CONST_COLS]
        pool_w = work[:, 4096:4608].rearrange("p (k c) -> p k c", k=CT)
        t4_w = work[:, 4608:5120].rearrange("p (k c) -> p k c", k=CT)
        st = work[:, 0:CT * NCH * 6].rearrange("p (t c n) -> p t c n", t=CT, c=NCH)
        mv = sb("mv", [P, CT, 2])

        def sm(i, n=CT):
            return small[:, i:i + n]
        s1, s2, s3, f3 = sm(0), sm(2), sm(4), sm(6)
        b1c, bias0, fb, tb3 = sm(8), sm(10), sm(12), sm(14)
        hb, hs1, hs2 = sm(16, HT), sm(24, HT), sm(32, HT)
        eps = sm(40, 1)
        ps = sb("ps", [P, 24])
        gstat = ps[:, 0:4]; gm = ps[:, 4:6]; gr = ps[:, 6:8]; gnb = ps[:, 8:10]; pg = ps[:, 10:12]; pv_ = ps[:, 12:14]
        gt2 = ps[:, 14:16]; gsd = ps[:, 16:18]; pin = ps[:, 18:20]

        w_in, setup_v, setup_p = sem("w_in"), sem("setup_v"), sem("setup_p")
        pool_passed, pe_passed, dve_passed, act_passed = sem("pool_passed"), sem("pe_passed"), sem("dve_passed"), sem("act_passed")
        pads_zero, pw_in = sem("pads_zero"), sem("pw_in")
        x_in, stats, group_ready, gstd_done, g_ready = sem("x_in"), sem("stats"), sem("group_ready"), sem("gstd_done"), sem("g_ready")
        gn_chain, pool_ready, pool_done, tbias_ready = sem("gn_chain"), sem("pool_ready"), sem("pool_done"), sem("tbias_ready")
        tb3_done = sem("tb3_done")
        cen_ready, sq_done, var_ready, std_done, rs_done = sem("cen_ready"), sem("sq_done"), sem("var_ready"), sem("std_done"), sem("rs_done")
        affine_done, n1_high = sem("affine_done"), sem("n1_high")
        n_done, n1_done = sem("n_done"), sem("n1_done")
        conv_ready, xc_done, init_ready, acc_init = sem("conv_ready"), sem("xc_done"), sem("init_ready"), sem("acc_init")
        strip_in, piece_ready, hi_done, lo_done = sem("strip_in"), sem("piece_ready"), sem("hi_done"), sem("lo_done")
        v_ready, v_copied, s_ready, max_done = sem("v_ready"), sem("v_copied"), sem("s_ready"), sem("max_done")
        mt_ready, mt_copied, st_ready, exp_done = sem("mt_ready"), sem("mt_copied"), sem("st_ready"), sem("exp_done")
        pv_ready, rec_done, norm_done, at_ready, at_copied = sem("pv_ready"), sem("rec_done"), sem("norm_done"), sem("at_ready"), sem("at_copied")
        comp_ready, acc_added = sem("comp_ready"), sem("acc_added")
        qd_zero = sem("qd_zero")
        hs_zero, t_done = sem("hs_zero"), sem("t_done")
        c1_ready, gelu1_done, h_done, tap_done, shift_done = sem("c1_ready"), sem("gelu1_done"), sem("h_done"), sem("tap_done"), sem("shift_done")
        gelu2_done, c2_ready, res_done, fin_done, xr_in, out_sent = sem("gelu2_done"), sem("c2_ready"), sem("res_done"), sem("fin_done"), sem("xr_in"), sem("out_sent")
        n2_high, n2_stored, affine2_done = sem("n2_high"), sem("n2_stored"), sem("affine2_done")
        dw_ready, diag_done = sem("dw_ready"), sem("diag_done")
        cen2_ready, sq2_done, var2_ready, std2_done, rs2_done, n2_done = (sem(n) for n in ("cen2_ready", "sq2_done", "var2_ready", "std2_done", "rs2_done", "n2_done"))

        xv = x.rearrange("b (t p) h w -> b p t (h w)", p=P)
        x4 = x.rearrange("b (t p) h w -> b p t h w", p=P)
        out4 = out.rearrange("b (t p) h w -> b p t h w", p=P)

        def halves(nb):
            return (0, KBANK), (KBANK, nb)

        PIECES = (("k", 0, 0), ("k", 1, 0), ("q", 0, 0), ("q", 1, 0), ("k", 0, 1), ("k", 1, 1))
        NP = len(PIECES)
        PIECE_AT = {1: 0, 2: 1, 3: 2, 5: 3, 7: 4, 9: 5}

        def copies(nb, step):
            return {0: range(0, KBANK), 1: range(KBANK, nb)}.get(step, ())

        def walk(eng, b, first, strip):
            first(b)
            for r in (1, 2, 3):
                one, two, steps = LOOPS[r]
                base = STRIP_BASE[r]
                with eng.Fori(0, steps) as p:
                    strip(b, base, p * 2, 0, r, r, p * two[0] + two[1], p * one[0] + one[1])
                    strip(b, base, p * 2 + 1, 1, r, r, p * one[0] + (one[0] + one[1]), p * two[0] + two[1])
                rest = REST[r]
                for n, row in enumerate(rest):
                    if n + 1 < len(rest):
                        nxt = (r, rest[n + 1])
                    else:
                        nxt = (r + 1, LOOPS[r + 1][0][1]) if r < 3 else None
                    strip(b, base, 2 * steps + n, n % 2, r, *(nxt or (None, None)), row)

        block = ctx.enter_context(nc.Block())

        @block.sync
        def _(sp):
            for q in (out_sent,):
                sp.sem_inc(q, START)
            for dst, src in ((pr_w, wproj), (tr_w, wtrans), (cst, consts), (vec[:], vecs), (hvec[:], hvecs),
                             (qkv32, wqkv), (conv_w[:], wconv), (c132, wc1), (c2_w[:], wc2),
                             (dw_w[:], wdw)):
                sp.dma_start(dst, src).then_inc(w_in, 16)

            def residual(b, s, k0, k1):
                sp.wait_ge(fin_done, (b * TAIL_STRIPS + s) * CT + START)
                row = s * CH_ROWS - 1 + k0
                for t in range(CT):
                    sp.dma_start(xr[:, t, k0:k1, :], x4[b, :, t, bass.ds(row, k1 - k0), :]).then_inc(xr_in, 16)
                sp.wait_ge(fin_done, (b * TAIL_STRIPS + s + 1) * CT + START)
                for t in range(CT):
                    sp.dma_start(out4[b, :, t, bass.ds(row, k1 - k0), :], obv[:, t, k0:k1, :]).then_inc(out_sent, 16)

            with sp.Fori(0, B) as b:
                sp.wait_ge(setup_v, 3)
                sp.wait_ge(fin_done, b * TAIL_STRIPS * CT + START)
                for t in range(CT):
                    sp.dma_start(g[:, t, :], xv[b, :, t, :]).then_inc(x_in, 16)
                sp.wait_ge(out_sent, b * (TAIL_STRIPS * CT * 16) + START)
                sp.dma_start(pool_w, wpool).then_inc(pw_in, 16)
                sp.dma_start(t4_w, wtrans[:, 8:10, :]).then_inc(pw_in, 16)
                sp.wait_ge(n2_stored, (b + 1) * NCH + START)
                residual(b, 0, 1, CH_ROWS)
                with sp.Fori(1, NCH) as s:
                    residual(b, s, 0, CH_ROWS)
                residual(b, NCH, 0, 1)
            sp.wait_ge(out_sent, B * TAIL_STRIPS * CT * 16 + START)

        @block.gpsimd
        def _(pool):
            for q in (h_done, shift_done, hs_zero, qd_zero):
                pool.sem_inc(q, START)
            nc.gpsimd.memset(qd0[:], 0.0).then_inc(pads_zero, 1)
            nc.gpsimd.memset(acc[:], 0.0).then_inc(pads_zero, 1)
            pool.wait_ge(setup_v, 1)
            pool.wait_ge(setup_p, 2)
            nc.gpsimd.memset(n1p[:], 0.0).then_inc(pads_zero, 1)
            pool.wait_ge(pads_zero, 3)

            def settle():
                pool.sem_inc(pool_passed, 1)

            def affine1(b, m, s):
                n = (b * NCH + s) * HT + m
                pool.wait_ge(gelu1_done, n + 1 + START)
                settle()
                nc.gpsimd.tensor_scalar(hs[:, m, 2:KB, 1:W + 1], gt[m % 2].rearrange("p (r w) -> p r w", r=CH_ROWS),
                                        hs1[:, m:m + 1], HV["mlp_bn1_b"][:, m:m + 1], ALU.mult, ALU.add).then_inc(h_done, 1)

            def shift(b, m, s):
                n = (b * NCH + s) * HT + m
                pool.wait_ge(tap_done, (b * TAIL_STRIPS + s) * STRIP_TAPS + taps_before(m + 1) + START)
                settle()
                nc.gpsimd.tensor_copy(hs[:, m, 0:2, 1:W + 1], hs[:, m, CH_ROWS:KB, 1:W + 1]).then_inc(shift_done, 1)

            def strip(b, s):
                for m in range(HT):
                    if isinstance(s, int):
                        pass
                    else:
                        pool.wait_ge(shift_done, (b * NCH + s) * HT + START)
                    affine1(b, m, s)
                    if m >= 1:
                        shift(b, m - 1, s)
                shift(b, HT - 1, s)

            with pool.Fori(0, B) as b:
                pool.wait_ge(init_ready, (b + 1) * NCH + START)
                pool.wait_ge(var_ready, (b + 1) * NCH + START)
                settle()
                nc.gpsimd.memset(gflat[:, 0:QW], 0.0).then_inc(qd_zero, 1)
                pool.wait_ge(acc_added, (b + 1) * STRIPS_PER_B * CT + START)
                settle()
                nc.gpsimd.memset(hs[:, :, :, 0:HSW:HSW - 1], 0.0)
                nc.gpsimd.memset(hs[:, :, 0:2, 1:W + 1], 0.0).then_inc(hs_zero, 1)
                strip(b, 0)
                with pool.Fori(1, NCH) as s:
                    strip(b, s)
                pool.wait_ge(shift_done, (b + 1) * NCH * HT + START)
                settle()
                nc.gpsimd.memset(hs[:, :, 2:3, :], 0.0).then_inc(hs_zero, 1)

        @block.tensor
        def _(pe):
            for q in (cen_ready, var_ready, conv_ready, init_ready, group_ready, pool_ready, tbias_ready, piece_ready,
                      v_ready, s_ready, mt_ready, st_ready, pv_ready, at_ready, comp_ready, cen2_ready, var2_ready,
                      c1_ready, c2_ready, dw_ready):
                pe.sem_inc(q, START)
            mm = nc.tensor.matmul
            pe.wait_ge(w_in, 10 * 16)
            for i in range(3):
                for j in range(PAIRS):
                    for hp in range(2):
                        a = (2 * j + hp) * HD
                        for k in range(CT):
                            last = mm(bank[i][j * HD:(j + 1) * HD, hp * C:(hp + 1) * C], pr_w[:, i, k, a:a + HD],
                                      tr_w[:, 2 * (i + 1) + k, :], start=(k == 0), stop=(k == CT - 1))
            last.then_inc(setup_p, 1)
            for t in range(CT):
                n = 0
                for i in range(3):
                    for k in range(CT):
                        last = mm(bank[3][:, t:t + 1], tr_w[:, 2 * (i + 1) + k, t * P:(t + 1) * P],
                                  V[f"proj{i + 1}_b"][:, k:k + 1], start=(n == 0), stop=(n == 5))
                        n += 1
            for m in range(HT):
                for k in range(CT):
                    mm(bank[4][:, m:m + 1], c132[:, k, m * P:(m + 1) * P], V["ln2_b"][:, k:k + 1],
                       start=(k == 0), stop=(k == CT - 1))
            for t in range(CT):
                for m in range(HT):
                    last = mm(bank[5][:, t:t + 1], c2_w[:, m, t * P:(t + 1) * P], HV["mlp_bn2_b"][:, m:m + 1],
                              start=(m == 0), stop=(m == HT - 1))
            last.then_inc(setup_p, 1)
            pe.wait_ge(setup_v, 3)
            pe.wait_ge(pads_zero, 3)

            def gn_and_pool(b):
                pe.wait_ge(stats, b + 1 + START)
                mm(bank[7][:, 0:4], groupm, gstat, start=True, stop=True).then_inc(group_ready, 1)
                pe.wait_ge(g_ready, b + 1 + START)
                pe.wait_ge(pw_in, (b + 1) * 32)
                for t in range(CT):
                    for k in range(CT):
                        last = mm(bank[7][:, 8 + t:9 + t], pool_w[:, k, t * P:(t + 1) * P], pg[:, k:k + 1],
                                  start=(k == 0), stop=(k == CT - 1))
                last.then_inc(pool_ready, 1)
                pe.wait_ge(pool_done, b + 1 + START)
                for t in range(CT):
                    for k in range(CT):
                        last = mm(bank[7][:, 16 + t:17 + t], t4_w[:, k, t * P:(t + 1) * P], pv_[:, k:k + 1],
                                  start=(k == 0), stop=(k == CT - 1))
                last.then_inc(tbias_ready, 1)

            def front(b, c):
                n = b * NCH + c
                gc = [g[:, k, bass.ds(c * CHUNK, CHUNK)] for k in range(CT)]
                pe.wait_ge(n_done, n + START)
                for t in range(CT):
                    for k in range(CT):
                        last = mm(bank[t][:, :], cdiag if t == k else coff, gc[k], start=(k == 0), stop=(k == CT - 1))
                last.then_inc(cen_ready, 1)
                pe.wait_ge(xc_done, n + START)
                for t in range(CT):
                    for k in range(CT):
                        last = mm(bank[3 + t][:, :], conv_w[:, k, t * P:(t + 1) * P], gc[k], start=(k == 0), stop=(k == CT - 1))
                last.then_inc(conv_ready, 1)
                pe.wait_ge(sq_done, n + 1 + START)
                pe.wait_ge(std_done, n + START)
                for k in range(CT):
                    last = mm(bank[2][:, :], meanm, sq[:, k, :], start=(k == 0), stop=(k == CT - 1))
                last.then_inc(var_ready, 1)
                pe.wait_ge(acc_init, n + START)
                for t in range(CT):
                    for k in range(CT):
                        mm(bank[5 + t][:, :], tsum_w[:, k, t * P:(t + 1) * P], gc[k], start=(k == 0), stop=False)
                pe.wait_ge(xc_done, n + 1 + START)
                for t in range(CT):
                    for k in range(CT):
                        last = mm(bank[5 + t][:, :], t0_w[:, k, t * P:(t + 1) * P], xc[:, k, :], start=False, stop=(k == CT - 1))
                last.then_inc(init_ready, 1)

            def piece(sc, par, r, n):
                kind, t, half = PIECES[n]
                nb, x = len(BLOCKS[r]), nbk[par]
                pe.wait_ge(strip_in, sc * 2 + (1 if n < 2 else 2) + START)
                pe.wait_ge(lo_done, sc * NP + n + START)

                def inner(s, k, i0, i1):
                    return x[:, s, k, i0:i1, :].rearrange("p i (y x) -> p i y x", y=KB)[:, :, 1:1 + QB, 1:1 + QB]

                def product(to, col, moving):
                    for m, (s, k) in enumerate([(s, k) for s in ((0, 0), (0, 1), (1, 0)) for k in range(CT)]):
                        last = mm(to, qkv_w[:, s[0], r - 1, k, col:col + P], moving(s[1], k), start=(m == 0), stop=(m == 5))
                    return last
                if kind == "q":
                    last = product(bank[3][:, :], t * P, lambda s, k: inner(s, k, 0, 8))
                else:
                    i0, i1 = halves(nb)[half]
                    last = product(bank[3][:, 0:(i1 - i0) * NK], C + t * P, lambda s, k: x[:, s, k, i0:i1, :].rearrange("p i n -> p (i n)"))
                    if half == 1 and nb > 8:
                        last = product(bank[3][:, 448:512], t * P, lambda s, k: inner(s, k, 8, 9))
                last.then_inc(piece_ready, 1)

            def values(bc, par, r, i):
                x = nbk[par]
                pe.wait_ge(v_copied, bc + i + START)
                for m, (s0, s1, k) in enumerate([(0, 0, 0), (0, 1, 0), (0, 0, 1), (0, 1, 1), (1, 0, 0), (1, 0, 1)]):
                    last = mm(bank[2][0:NK, 0:C], x[:, s0, k, i, :], qkv_w[:, s1, r - 1, k, 2 * C:3 * C], start=(m == 0), stop=(m == 5))
                last.then_inc(v_ready, 1)

            def scores(sc, bc, par, i):
                q, kk = qd[par], ks[par]
                if i == 0:
                    pe.wait_ge(lo_done, (sc + 1) * NP + START)
                pe.wait_ge(max_done, bc + max(i - 1, 0) + START)
                mm(bank[i % 2][:, 0:4 * NK], pair_b[:], mask_b[:], start=True, stop=False)
                for j in range(PAIRS):
                    t, u = j // 2, j % 2
                    last = mm(bank[i % 2][:, j * NK:(j + 1) * NK],
                              q[:, 0, t, i, 2 * u:2 * u + 2, :].rearrange("p h q -> p (h q)"), kk[:, 0, t, i, :], start=False, stop=(j == PAIRS - 1))
                last.then_inc(s_ready, 1)

            def first(b):
                for n in range(NP):
                    piece(b * STRIPS_PER_B, 0, 1, n)
                values(b * BLOCKS_PER_B, 0, 1, 0)
                scores(b * STRIPS_PER_B, b * BLOCKS_PER_B, 0, 0)

            def strip(b, base, s, par, r, nxt, nxt_row, row0):
                sc = b * STRIPS_PER_B + (s + base)
                nb = len(BLOCKS[r])
                bc0 = b * BLOCKS_PER_B + (s * nb + BLOCK_BASE[r])
                q, kk = qd[par], ks[par]

                def turn_max(i):
                    pe.wait_ge(max_done, bc0 + i + 1 + START)
                    if i == 0:
                        pe.wait_ge(acc_added, sc * CT + START)
                    pe.wait_ge(at_copied, bc0 + max(i - 2, 0) + START)
                    nc.tensor.transpose(bank[7][0:PAIRS, 128:128 + P // 2].bitcast(BF16), mx[:, i % 2, :], identb[:]).then_inc(mt_ready, 1)

                def scores_t(i):
                    bk = bank[4 + i % 2]
                    pe.wait_ge(mt_copied, bc0 + i + 1 + START)
                    pe.wait_ge(exp_done, bc0 + max(i - 1, 0) + START)
                    for t in range(CT):
                        for m, (s0, s1) in enumerate([(0, 0), (0, 1), (1, 0)]):
                            mm(bk[0:NK, t * 256:(t + 1) * 256], kk[:, s0, t, i, :], q[:, s1, t, i].rearrange("p h q -> p (h q)"),
                               start=(t == 0 and m == 0), stop=False)
                    for j in range(PAIRS):
                        last = mm(bk[0:NK, j * P:(j + 1) * P], left_b[:, j, :], right_b[:, i % 2, :], start=False, stop=(j == PAIRS - 1))
                    last.then_inc(st_ready, 1)

                def weigh(i):
                    pe.wait_ge(exp_done, bc0 + i + 1 + START)
                    pe.wait_ge(norm_done, bc0 + i + START)
                    for j in range(PAIRS):
                        last = mm(bank[6][:, j * 65:(j + 1) * 65], pb[i % 2][:, j * P:(j + 1) * P], vb[i % 3][:, j, :], start=True, stop=True)
                    last.then_inc(pv_ready, 1)

                def turn_out(i):
                    pe.wait_ge(norm_done, bc0 + i + 1 + START)
                    pe.wait_ge(mt_copied, bc0 + min(i + 3, nb) + START)
                    if i + 2 >= nb:
                        pe.wait_ge(at_copied, bc0 + i + START)
                    nc.tensor.transpose(bank[7][:, 0:P], an[:, i % 2].rearrange("p j c -> p (j c)"), ident).then_inc(at_ready, 1)

                for i in range(nb + 3):
                    if i + 1 < nb:
                        values(bc0, par, r, i + 1)
                    if 1 <= i < nb:
                        scores(sc, bc0, par, i)
                    if 0 <= i - 1 < nb:
                        turn_max(i - 1)
                    if 0 <= i - 2 < nb:
                        weigh(i - 2)
                    if 0 <= i - 3 < nb:
                        turn_out(i - 3)
                    if 0 <= i - 1 < nb:
                        scores_t(i - 1)
                    if nxt and i in PIECE_AT:
                        piece(sc + 1, 1 - par, nxt, PIECE_AT[i])
                    if nxt and i == nb + 1:
                        values(bc0 + nb, 1 - par, nxt, 0)
                if nxt:
                    scores(sc + 1, bc0 + nb, 1 - par, 0)
                pe.wait_ge(at_copied, bc0 + nb + START)
                for t in range(CT):
                    for hp in range(2):
                        last = mm(bank[6 + t][:, :], comp_w[:, r - 1, hp, t * P:(t + 1) * P],
                                  attn[:, hp].rearrange("p r w -> p (r w)"), start=(hp == 0), stop=(hp == 1))
                    last.then_inc(comp_ready, 1)

            def layer_norm2(b, p):
                n0 = b * NCH + p * 2
                pe.wait_ge(n2_done, n0 + START)
                for j in range(2):
                    pe.wait_ge(t_done, n0 + j + 1 + START)
                    tc = [acc[:, k, bass.ds(p * (2 * CH_ROWS) + j * CH_ROWS, CH_ROWS), :] for k in range(CT)]
                    for t in range(CT):
                        for k in range(CT):
                            last = mm(bank[3 * j + t][:, :], cdiag if t == k else coff, tc[k], start=(k == 0), stop=(k == CT - 1))
                    last.then_inc(cen2_ready, 1)
                for j in range(2):
                    pe.wait_ge(sq2_done, n0 + j + 1 + START)
                    for k in range(CT):
                        last = mm(bank[3 * j + 2][:, :], meanm, sq2[j][:, k, :], start=(k == 0), stop=(k == CT - 1))
                    last.then_inc(var2_ready, 1)

            def tail(b, s, k0, k1, fresh):
                n = b * NCH + s
                f = b * TAIL_STRIPS + s

                def up(m):
                    q = n * HT + m
                    if m == 0:
                        pe.wait_ge(n2_stored, (b + 1) * NCH + START)
                    pe.wait_ge(gelu1_done, n * HT + max(m - 1, 0) + START)
                    for i, (s0, s1, k) in enumerate([(0, 0, 0), (0, 1, 0), (1, 0, 0), (0, 0, 1), (0, 1, 1), (1, 0, 1)]):
                        last = mm(bank[3 + m % 2][:, :], c1_w[:, s0, k, m * P:(m + 1) * P],
                                  n1p[:, s1, k, bass.ds(s * CH_ROWS + HALO, CH_ROWS), HALO:HALO + W], start=(i == 0), stop=(i == 5))
                    last.then_inc(c1_ready, 1)

                def taps(m):
                    if fresh:
                        pe.wait_ge(h_done, n * HT + m + 1 + START)
                    if m == 0:
                        pe.wait_ge(diag_done, b + 1 + START)
                        if not fresh:
                            pe.wait_ge(hs_zero, b * 2 + 2 + START)
                    pe.wait_ge(tap_done, f * STRIP_TAPS + (taps_before(m - 2) + 1 if m >= 2 else 0) + START)
                    for k in range(PE_TAPS[m % 2]):
                        last = mm(bank[m % 2][:, k0 * W:k1 * W], diag[:, m // 2 * sum(PE_TAPS) + m % 2 * PE_TAPS[0] + k, :],
                                  hs[:, m, k0 + k // 3:k1 + k // 3, k % 3:k % 3 + W], start=(k == 0), stop=(k == PE_TAPS[m % 2] - 1))
                    last.then_inc(dw_ready, 1)

                def down(m):
                    q = f * HT + m
                    pe.wait_ge(gelu2_done, q + 1 + START)
                    if m == 0:
                        pe.wait_ge(res_done, f * CT + START)
                    for t in range(CT):
                        last = mm(bank[5 + t][:, k0 * W:k1 * W], c2_w[:, m, t * P:(t + 1) * P], h2[m % 2][:, k0 * W:k1 * W],
                                  start=(m == 0), stop=(m == HT - 1))
                    last.then_inc(c2_ready, 1)
                if fresh:
                    up(0)
                for m in range(HT):
                    if fresh and m + 1 < HT:
                        up(m + 1)
                    taps(m)
                    if m >= 1:
                        down(m - 1)
                down(HT - 1)

            with pe.Fori(0, B) as b:
                gn_and_pool(b)
                with pe.Fori(0, NCH) as c:
                    front(b, c)
                pe.wait_ge(acc_init, (b + 1) * NCH + START)
                pe.sem_inc(pe_passed, 1)
                walk(pe, b, first, strip)
                with pe.Fori(0, NCH // 2) as p:
                    layer_norm2(b, p)
                tail(b, 0, 1, CH_ROWS, True)
                with pe.Fori(1, NCH) as s:
                    tail(b, s, 0, CH_ROWS, True)
                tail(b, NCH, 0, 1, False)

        @block.vector
        def _(dve):
            for q in (stats, g_ready, pool_done, tb3_done, rs_done, n_done, n1_high, n1_done, acc_init, lo_done, max_done,
                      mt_copied, rec_done, norm_done, at_copied, acc_added, tap_done, res_done, fin_done, rs2_done,
                      n2_done, n2_high, n2_stored, diag_done):
                dve.sem_inc(q, START)
            v = nc.vector
            dve.wait_ge(w_in, 10 * 16)
            nchain = [0]

            def link(ins):
                nchain[0] += 1
                ins.then_inc(gn_chain, 1)
                dve.wait_ge(gn_chain, nchain[0])

            def cc(name):
                a, e = CO[name]
                return cst[:, a:e]
            v.memset(eps, EPS)
            for i, n in enumerate(("ident", "cdiag", "coff", "mean", "group")):
                v.tensor_copy(matc[:, i, :], cc(n))
            v.tensor_copy(identb[:], cc("ident"))
            v.tensor_copy(pair_b[:], cc("pairI")[0:NQ, :])
            v.tensor_copy(mask_b[:], cc("mask")[0:NQ, :])
            v.tensor_copy(left_b[:].rearrange("p j n -> p (j n)"), cc("left")[0:96, :])
            for i in range(2):
                v.tensor_copy(right_b[:, i, :], cc("right")[0:96, :])
            v.tensor_copy(t0_w[:].rearrange("p k c -> p (k c)"), tr_w[:, 0:2, :].rearrange("p k c -> p (k c)"))
            link(v.tensor_tensor(tsum_w[:], tr_w[:, 2:4, :], tr_w[:, 4:6, :], ALU.add))
            v.tensor_tensor(tsum_w[:], tsum_w[:], tr_w[:, 6:8, :], ALU.add).then_inc(setup_v, 1)
            for i in range(3):
                last = v.tensor_copy(qkv_w[:, 0, i], qkv32[:, i])
            link(last)
            for i in range(3):
                v.tensor_tensor(qkv_w[:, 1, i], qkv32[:, i], qkv_w[:, 0, i], ALU.subtract)
            for dst, n in ((s1, "tc_bn1_g"), (s2, "tc_bn2_g"), (s3, "tc_bn3_g"), (f3, "mlp_bn3_g")):
                v.tensor_scalar(dst, V[n], BN_SCALE, None, ALU.mult)
            v.tensor_scalar(hs1, HV["mlp_bn1_g"], BN_SCALE, None, ALU.mult)
            link(v.tensor_scalar(hs2, HV["mlp_bn2_g"], BN_SCALE, None, ALU.mult))
            link(v.tensor_tensor(b1c, s1, V["tc_conv_b"], ALU.mult))
            link(v.tensor_tensor(b1c, b1c, V["tc_bn1_b"], ALU.add))
            dve.wait_ge(setup_p, 2)
            for i in range(3):
                v.tensor_copy(comp_w[:, i].rearrange("p e c -> p (e c)"), bank[i][:, :])
            v.tensor_tensor(bias0, bank[3][:, 0:CT], V["tc_trans_b"], ALU.add)
            v.tensor_tensor(hb, bank[4][:, 0:HT], HV["mlp_c1_b"], ALU.add)
            link(v.tensor_tensor(fb, bank[5][:, 0:CT], V["mlp_c2_b"], ALU.add))
            link(v.tensor_tensor(fb, fb, f3, ALU.mult))
            link(v.tensor_tensor(fb, fb, V["mlp_bn3_b"], ALU.add))
            for k in range(CT):
                last = v.tensor_scalar(c132[:, k, :], c132[:, k, :], V["ln2_w"][:, k:k + 1], None, ALU.mult)
            link(last)
            link(v.tensor_copy(c1_w[:, 0], c132))
            v.tensor_tensor(c1_w[:, 1], c132, c1_w[:, 0], ALU.subtract)
            for m in range(HT):
                v.tensor_scalar(c2_w[:, m, :], c2_w[:, m, :], hs2[:, m:m + 1], None, ALU.mult)
            v.tensor_scalar(dw_w[:, :, 4:5], dw_w[:, :, 4:5], 1.0, None, ALU.add).then_inc(setup_v, 2)
            dve.wait_ge(setup_v, 3)
            SETUP = nchain[0]
            assert SETUP == SETUP_LINKS
            PER_B = [0]

            def group_norm(b):
                cnt = [0]

                def step(ins):
                    cnt[0] += 1
                    ins.then_inc(gn_chain, 1)
                    dve.wait_ge(gn_chain, b * GN_STEPS + (SETUP + cnt[0]))
                dve.wait_ge(x_in, (b + 1) * CT * 16)
                for t in range(CT):
                    for c in range(NCH):
                        last = v.bn_stats(st[:, t, c, :], g[:, t, c * CHUNK:(c + 1) * CHUNK])
                step(last)
                dve.sem_inc(dve_passed, 1)
                for t in range(CT):
                    last = v.bn_aggr(mv[:, t, :], st[:, t, :, :])
                step(last)
                v.tensor_copy(gstat[:, 0:2], mv[:, :, 0])
                step(v.tensor_tensor(gt2, mv[:, :, 0], mv[:, :, 0], ALU.mult))
                v.tensor_tensor(gstat[:, 2:4], gt2, mv[:, :, 1], ALU.add).then_inc(stats, 1)
                dve.wait_ge(group_ready, b + 1 + START)
                step(v.tensor_copy(gm, bank[7][:, 0:2]))
                step(v.tensor_tensor(gt2, gm, gm, ALU.mult))
                step(v.scalar_tensor_tensor(gt2, bank[7][:, 2:4], EPS, gt2, ALU.add, ALU.subtract))
                dve.wait_ge(gstd_done, b + 1 + START)
                step(v.reciprocal(gr, gsd))
                step(v.tensor_tensor(gnb, gm, gr, ALU.mult))
                v.tensor_tensor(pin, mv[:, :, 0], gm, ALU.subtract)
                for t in range(CT):
                    last = v.tensor_scalar(g[:, t, :], g[:, t, :], gr[:, t:t + 1], gnb[:, t:t + 1], ALU.mult, ALU.subtract)
                step(last)
                v.tensor_tensor(pg, pin, gr, ALU.mult).then_inc(g_ready, 1)
                dve.wait_ge(pool_ready, b + 1 + START)
                step(v.tensor_tensor(pv_, bank[7][:, 8:10], s2, ALU.mult))
                step(v.tensor_tensor(pv_, pv_, V["tc_bn2_b"], ALU.add))
                v.tensor_scalar(pv_, pv_, 0.0, None, ALU.max).then_inc(pool_done, 1)
                dve.wait_ge(tbias_ready, b + 1 + START)
                step(v.tensor_tensor(tb3, bank[7][:, 16:18], bias0, ALU.add))
                step(v.tensor_tensor(tb3, tb3, s3, ALU.mult))
                v.tensor_tensor(tb3, tb3, V["tc_bn3_b"], ALU.add).then_inc(tb3_done, 1)
                return cnt[0]

            GN_STEPS = 13

            def front(b, c):
                n = b * NCH + c
                dve.wait_ge(std_done, n + 1 + START)
                v.reciprocal(rstd, std).then_inc(rs_done, 1)
                dve.wait_ge(rs_done, n + 1 + START)
                dve.wait_ge(n1_done, n + START)
                for t in range(CT):
                    last = v.tensor_tensor(nt[:, t, :], bank[t][:, :], rstd, ALU.mult)
                last.then_inc(n_done, 1)
                dve.wait_ge(init_ready, n + 1 + START)
                for t in range(CT):
                    last = v.tensor_copy(acc[:, t, bass.ds(c * CH_ROWS, CH_ROWS), :], bank[5 + t][:, :].rearrange("p (r w) -> p r w", r=CH_ROWS))
                last.then_inc(acc_init, 1)
                dve.wait_ge(affine_done, n + 1 + START)
                rows = [[n1p[:, h, t, bass.ds(c * CH_ROWS + HALO, CH_ROWS), HALO:HALO + W] for t in range(CT)] for h in range(2)]
                nr = [nt[:, t, :].rearrange("p (r w) -> p r w", r=CH_ROWS) for t in range(CT)]
                for t in range(CT):
                    last = v.tensor_copy(rows[0][t], nr[t])
                last.then_inc(n1_high, 1)
                dve.wait_ge(n1_high, n + 1 + START)
                for t in range(CT):
                    last = v.tensor_tensor(rows[1][t], nr[t], rows[0][t], ALU.subtract)
                last.then_inc(n1_done, 1)

            def low_part(sc, par, r, n, heads=range(4)):
                kind, t, half = PIECES[n]
                nb = len(BLOCKS[r])
                q, kk = qd[par], ks[par]
                if 0 in heads:
                    dve.wait_ge(hi_done, sc * NP + n + 1 + START)

                def queries(i0, i1, psum):
                    for h in heads:
                        hp = slice(HD * h, HD * h + HD)
                        last = v.tensor_tensor(q[hp, 1, t, i0:i1, h, :], psum[hp, :].rearrange("p (i q) -> p i q", q=NQ), q[hp, 0, t, i0:i1, h, :], ALU.subtract)
                    return last
                if kind == "q":
                    last = queries(0, 8, bank[3])
                else:
                    i0, i1 = halves(nb)[half]
                    n_ = (i1 - i0) * NK
                    last = v.tensor_tensor(kk[:, 1, t, i0:i1, :].rearrange("p i n -> p (i n)"), bank[3][:, 0:n_],
                                           kk[:, 0, t, i0:i1, :].rearrange("p i n -> p (i n)"), ALU.subtract)
                    if half == 1 and nb > 8:
                        last = queries(8, 9, bank[3][:, 448:512])
                if 3 in heads:
                    last.then_inc(lo_done, 1)

            def take_max(bc, i):
                dve.wait_ge(s_ready, bc + i + 1 + START)
                if i >= 2:
                    dve.wait_ge(mt_ready, bc + i - 1 + START)
                v.tensor_reduce(mx[:, i % 2, :], bank[i % 2][:, 0:4 * NK].rearrange("p (j n) -> p j n", j=PAIRS), AX_X, ALU.max).then_inc(max_done, 1)

            def first(b):
                for n in range(NP):
                    low_part(b * STRIPS_PER_B, 0, 1, n)
                take_max(b * BLOCKS_PER_B, 0)

            def strip(b, base, s, par, r, nxt, nxt_row, row0):
                sc = b * STRIPS_PER_B + (s + base)
                nb = len(BLOCKS[r])
                bc0 = b * BLOCKS_PER_B + (s * nb + BLOCK_BASE[r])

                def copy_max(i):
                    dve.wait_ge(mt_ready, bc0 + i + 1 + START)
                    if i >= 2:
                        dve.wait_ge(st_ready, bc0 + i - 1 + START)
                    v.tensor_copy(right_b[0:PAIRS, i % 2, :], bank[7][0:PAIRS, 128:128 + P // 2].bitcast(BF16)).then_inc(mt_copied, 1)

                def normalise(i):
                    dve.wait_ge(pv_ready, bc0 + i + 1 + START)
                    o_ = bank[6][:, 0:PAIRS * 65].rearrange("p (j c) -> p j c", j=PAIRS)
                    v.reciprocal(rec[:, i % 2, :], o_[:, :, 64]).then_inc(rec_done, 1)
                    dve.wait_ge(rec_done, bc0 + i + 1 + START)
                    if i >= 2:
                        dve.wait_ge(at_ready, bc0 + i - 1 + START)
                    for hp in range(2):
                        q = slice(NQ * hp, NQ * hp + NQ)
                        last = v.tensor_tensor(an[q, i % 2], o_[q, :, HD * hp:HD * hp + HD],
                                               rec[q, i % 2, :].unsqueeze(2).to_broadcast([NQ, PAIRS, HD]), ALU.mult)
                    last.then_inc(norm_done, 1)

                def copy_out(i):
                    c0, skip = BLOCKS[r][i]
                    dve.wait_ge(at_ready, bc0 + i + 1 + START)
                    if i == 0:
                        dve.wait_ge(comp_ready, sc * CT + START)
                    c0, skip = BLOCKS[r][i]
                    a = c0 + skip * r
                    v.tensor_copy(attn[:, :, :, a:c0 + (QB - 1) * r + 1:r],
                                  bank[7][:, 0:P].rearrange("p (e y x) -> p e y x", e=2, y=QB)[:, :, :, skip:]).then_inc(at_copied, 1)

                for i in range(nb + 3):
                    if 1 <= i < nb:
                        take_max(bc0, i)
                    if 0 <= i - 1 < nb:
                        copy_max(i - 1)
                    split = nxt and i - 1 in PIECE_AT
                    query = split and PIECES[PIECE_AT[i - 1]][0] == "q"
                    if query:
                        low_part(sc + 1, 1 - par, nxt, PIECE_AT[i - 1], (0, 1))
                    if 0 <= i - 2 < nb:
                        normalise(i - 2)
                    if 0 <= i - 3 < nb:
                        copy_out(i - 3)
                    if split:
                        low_part(sc + 1, 1 - par, nxt, PIECE_AT[i - 1], (2, 3) if query else range(4))
                if nxt:
                    take_max(bc0 + nb, 0)
                for t in range(CT):
                    dve.wait_ge(comp_ready, sc * CT + t + 1 + START)
                    dve.wait_ge(acc_added, sc * CT + t + START)
                    a = acc[:, t, bass.ds(row0, QB, r), :]
                    v.tensor_tensor(a, bank[6 + t][:, :].rearrange("p (r w) -> p r w", r=QB), a, ALU.add).then_inc(acc_added, 1)

            def layer_norm2(b, p):
                n0 = b * NCH + p * 2
                for j in range(2):
                    dve.wait_ge(std2_done, n0 + j + 1 + START)
                    v.reciprocal(std2[j], std2[j]).then_inc(rs2_done, 1)
                    dve.wait_ge(rs2_done, n0 + j + 1 + START)
                    for t in range(CT):
                        last = v.tensor_tensor(nt2[j][:, t, :], bank[3 * j + t][:, :], std2[j], ALU.mult)
                    last.then_inc(n2_done, 1)
                rows = [[[n1p[:, h, t, bass.ds(p * (2 * CH_ROWS) + (j * CH_ROWS + HALO), CH_ROWS), HALO:HALO + W] for t in range(CT)] for h in range(2)] for j in range(2)]
                nr = [[nt2[j][:, t, :].rearrange("p (r w) -> p r w", r=CH_ROWS) for t in range(CT)] for j in range(2)]
                dve.wait_ge(n2_done, n0 + 2 + START)
                for j in range(2):
                    for t in range(CT):
                        last = v.tensor_copy(rows[j][0][t], nr[j][t])
                    last.then_inc(n2_high, 1)
                for j in range(2):
                    dve.wait_ge(n2_high, n0 + j + 1 + START)
                    for t in range(CT):
                        last = v.tensor_tensor(rows[j][1][t], nr[j][t], rows[j][0][t], ALU.subtract)
                    last.then_inc(n2_stored, 1)

            def diagonals(b):
                for m in range(HT):
                    for k in range(PE_TAPS[m % 2]):
                        last = v.tensor_scalar(diag[:, m // 2 * sum(PE_TAPS) + m % 2 * PE_TAPS[0] + k, :], ident, dw_w[:, m, k:k + 1], None, ALU.mult)
                last.then_inc(diag_done, 1)

            def tail(b, s, k0, k1, fresh):
                n = b * NCH + s
                f = b * TAIL_STRIPS + s
                for m in range(HT):
                    q = f * HT + m
                    tap0 = f * STRIP_TAPS + taps_before(m)
                    if fresh:
                        dve.wait_ge(h_done, n * HT + m + 1 + START)
                    elif m == 0:
                        dve.wait_ge(hs_zero, b * 2 + 2 + START)
                    dve.wait_ge(gelu2_done, f * HT + max(m - 1, 0) + START)
                    dve.wait_ge(dw_ready, q + 1 + START)
                    cvm = cv[m % 2][:, k0 * W:k1 * W].rearrange("p (r w) -> p r w", r=k1 - k0)
                    for i, k in enumerate(range(PE_TAPS[m % 2], 9)):
                        win = hs[:, m, k0 + k // 3:k1 + k // 3, k % 3:k % 3 + W]
                        so_far = bank[m % 2][:, k0 * W:k1 * W].rearrange("p (r w) -> p r w", r=k1 - k0) if i == 0 else cvm
                        if i:
                            dve.wait_ge(tap_done, tap0 + i + START)
                        v.scalar_tensor_tensor(cvm, win, dw_w[:, m, k:k + 1], so_far, ALU.mult, ALU.add).then_inc(tap_done, 1)
                dve.wait_ge(c2_ready, (f + 1) * HT + START)
                for t in range(CT):
                    o_ = obv[:, t, k0:k1, :]
                    dve.wait_ge(out_sent, f * CT * 16 + START)
                    v.scalar_tensor_tensor(o_, bank[5 + t][:, k0 * W:k1 * W].rearrange("p (r w) -> p r w", r=k1 - k0), f3[:, t:t + 1],
                                           acc[:, t, bass.ds(s * CH_ROWS - 1 + k0, k1 - k0), :], ALU.mult, ALU.add).then_inc(res_done, 1)
                dve.wait_ge(xr_in, (f + 1) * CT * 16)
                for t in range(CT):
                    o_ = obv[:, t, k0:k1, :]
                    dve.wait_ge(res_done, f * CT + t + 1 + START)
                    v.scalar_tensor_tensor(o_, o_, fb[:, t:t + 1], xr[:, t, k0:k1, :], ALU.add, ALU.add).then_inc(fin_done, 1)

            with dve.Fori(0, B) as b:
                assert group_norm(b) == GN_STEPS
                with dve.Fori(0, NCH) as c:
                    front(b, c)
                dve.wait_ge(n1_done, (b + 1) * NCH + START)
                dve.wait_ge(init_ready, (b + 1) * NCH + START)
                dve.wait_ge(acc_init, (b + 1) * NCH + START)
                for i in range(3):
                    v.memset(vb[i][:, :, 64:65], 1.0)
                walk(dve, b, first, strip)
                diagonals(b)
                with dve.Fori(0, NCH // 2) as p:
                    layer_norm2(b, p)
                tail(b, 0, 1, CH_ROWS, True)
                with dve.Fori(1, NCH) as s:
                    tail(b, s, 0, CH_ROWS, True)
                tail(b, NCH, 0, 1, False)

        @block.scalar
        def _(act):
            for q in (gstd_done, sq_done, xc_done, std_done, affine_done, hi_done, strip_in, v_copied, exp_done, gelu1_done,
                      gelu2_done, t_done, sq2_done, std2_done, affine2_done):
                act.sem_inc(q, START)
            fn = nc.scalar.activation
            act.wait_ge(setup_v, 3)

            def group_std(b):
                act.wait_ge(gn_chain, b * 13 + GN_BASE + 6)
                fn(gsd, gt2, ACT.Sqrt).then_inc(gstd_done, 1)

            def front(b, c):
                n = b * NCH + c
                act.wait_ge(cen_ready, n + 1 + START)
                act.wait_ge(var_ready, n + START)
                for t in range(CT):
                    last = fn(sq[:, t, :], bank[t][:, :], ACT.Square)
                last.then_inc(sq_done, 1)
                act.wait_ge(conv_ready, n + 1 + START)
                act.wait_ge(init_ready, n + START)
                for t in range(CT):
                    last = fn(xc[:, t, :], bank[3 + t][:, :], ACT.Relu, bias=b1c[:, t:t + 1], scale=s1[:, t:t + 1])
                last.then_inc(xc_done, 1)
                act.wait_ge(var_ready, n + 1 + START)
                act.wait_ge(rs_done, n + START)
                fn(std, bank[2][:, :], ACT.Sqrt, bias=eps).then_inc(std_done, 1)
                act.wait_ge(n_done, n + 1 + START)
                for t in range(CT):
                    last = fn(nt[:, t, :], nt[:, t, :], ACT.Identity, scale=V["ln1_w"][:, t:t + 1], bias=V["ln1_b"][:, t:t + 1])
                last.then_inc(affine_done, 1)

            def copy_blocks(par, r, row0, blocks):
                for i in blocks:
                    a = BLOCKS[r][i][0] + HALO - r
                    last = fn(nbk[par][:, :, :, i, :].rearrange("p s k (y x) -> p (s k) y x", y=KB),
                              n1p[:, :, :, bass.ds(row0 + HALO - r, KB, r), a:a + (KB - 1) * r + 1:r].rearrange("p s k y x -> p (s k) y x"), ACT.Copy)
                return last

            def high_part(sc, par, r, n, heads=range(4)):
                kind, t, half = PIECES[n]
                nb = len(BLOCKS[r])
                q, kk = qd[par], ks[par]
                if 0 in heads:
                    act.wait_ge(piece_ready, sc * NP + n + 1 + START)

                def queries(i0, i1, psum):
                    for h in heads:
                        hp = slice(HD * h, HD * h + HD)
                        last = fn(q[hp, 0, t, i0:i1, h, :], psum[hp, :].rearrange("p (i q) -> p i q", q=NQ), ACT.Copy)
                    return last
                if kind == "q":
                    last = queries(0, 8, bank[3])
                else:
                    i0, i1 = halves(nb)[half]
                    last = fn(kk[:, 0, t, i0:i1, :].rearrange("p i n -> p (i n)"), bank[3][:, 0:(i1 - i0) * NK], ACT.Copy)
                    if half == 1 and nb > 8:
                        last = queries(8, 9, bank[3][:, 448:512])
                if 3 in heads:
                    last.then_inc(hi_done, 1)

            def copy_v(bc, i):
                act.wait_ge(v_ready, bc + i + 1 + START)
                act.wait_ge(pv_ready, bc + max(i - 2, 0) + START)
                fn(vb[i % 3][:, :, 0:64], bank[2][0:NK, 0:C].rearrange("p (j c) -> p j c", j=PAIRS), ACT.Copy).then_inc(v_copied, 1)

            def first(b):
                act.wait_ge(n1_done, (b + 1) * NCH + START)
                act.wait_ge(init_ready, (b + 1) * NCH + START)
                act.sem_inc(act_passed, 1)
                copy_blocks(0, 1, 0, range(len(BLOCKS[1]))).then_inc(strip_in, 2)
                for n in range(NP):
                    high_part(b * STRIPS_PER_B, 0, 1, n)
                act.wait_ge(qd_zero, b + 1 + START)
                copy_v(b * BLOCKS_PER_B, 0)

            def strip(b, base, s, par, r, nxt, nxt_row, row0):
                sc = b * STRIPS_PER_B + (s + base)
                nb = len(BLOCKS[r])
                bc0 = b * BLOCKS_PER_B + (s * nb + BLOCK_BASE[r])

                def exps(i):
                    act.wait_ge(st_ready, bc0 + i + 1 + START)
                    if i >= 2:
                        act.wait_ge(pv_ready, bc0 + i - 1 + START)
                    fn(pb[i % 2], bank[4 + i % 2][0:NK, :], ACT.Exp, scale=HD ** -0.5).then_inc(exp_done, 1)

                for i in range(nb + 3):
                    if i + 1 < nb:
                        copy_v(bc0, i + 1)
                    if nxt and i - 1 in PIECE_AT and PIECES[PIECE_AT[i - 1]][0] == "q":
                        high_part(sc + 1, 1 - par, nxt, PIECE_AT[i - 1], (2, 3))
                    if 0 <= i - 1 < nb:
                        exps(i - 1)
                    if nxt:
                        todo = copies(len(BLOCKS[nxt]), i)
                        if todo:
                            copy_blocks(1 - par, nxt, nxt_row, todo).then_inc(strip_in, 1)
                        if i in PIECE_AT:
                            high_part(sc + 1, 1 - par, nxt, PIECE_AT[i], (0, 1) if PIECES[PIECE_AT[i]][0] == "q" else range(4))
                if nxt:
                    copy_v(bc0 + nb, 0)

            def layer_norm2(b, p):
                n0 = b * NCH + p * 2
                act.wait_ge(acc_added, (b + 1) * STRIPS_PER_B * CT + START)
                act.wait_ge(tb3_done, b + 1 + START)
                act.sem_inc(act_passed, 1)
                for j in range(2):
                    for t in range(CT):
                        a = acc[:, t, bass.ds(p * (2 * CH_ROWS) + j * CH_ROWS, CH_ROWS), :]
                        last = fn(a, a, ACT.Relu, bias=tb3[:, t:t + 1], scale=s3[:, t:t + 1])
                    last.then_inc(t_done, 1)
                for j in range(2):
                    act.wait_ge(cen2_ready, n0 + j + 1 + START)
                    for t in range(CT):
                        last = fn(sq2[j][:, t, :], bank[3 * j + t][:, :], ACT.Square)
                    last.then_inc(sq2_done, 1)
                for j in range(2):
                    act.wait_ge(var2_ready, n0 + j + 1 + START)
                    act.wait_ge(n2_stored, n0 + START)
                    fn(std2[j], bank[3 * j + 2][:, :], ACT.Sqrt, bias=eps).then_inc(std2_done, 1)

            def tail(b, s, k0, k1, fresh):
                n = b * NCH + s
                f = b * TAIL_STRIPS + s

                def gelu1(m):
                    q = n * HT + m
                    act.wait_ge(c1_ready, q + 1 + START)
                    if m >= 2:
                        act.wait_ge(h_done, q - 1 + START)
                    else:
                        act.wait_ge(h_done, n * HT + START)
                    if isinstance(s, int) and m == 0:
                        act.wait_ge(hs_zero, b * 2 + 1 + START)
                    fn(gt[m % 2], bank[3 + m % 2][:, :], ACT.Gelu, bias=hb[:, m:m + 1]).then_inc(gelu1_done, 1)

                def gelu2(m):
                    q = f * HT + m
                    act.wait_ge(tap_done, f * STRIP_TAPS + taps_before(m + 1) + START)
                    if m >= 2:
                        act.wait_ge(c2_ready, q - 1 + START)
                    fn(h2[m % 2][:, k0 * W:k1 * W], cv[m % 2][:, k0 * W:k1 * W], ACT.Gelu, bias=HV["mlp_dw_b"][:, m:m + 1]).then_inc(gelu2_done, 1)

                if fresh:
                    gelu1(0)
                for m in range(HT):
                    if fresh and m + 1 < HT:
                        gelu1(m + 1)
                    gelu2(m)

            GN_BASE = SETUP_LINKS
            with act.Fori(0, B) as b:
                group_std(b)
                with act.Fori(0, NCH) as c:
                    front(b, c)
                walk(act, b, first, strip)
                with act.Fori(0, NCH // 2) as p:
                    layer_norm2(b, p)
                tail(b, 0, 1, CH_ROWS, True)
                with act.Fori(1, NCH) as s:
                    tail(b, s, 0, CH_ROWS, True)
                tail(b, NCH, 0, 1, False)


SETUP_LINKS = 10


def constants():
    import numpy as np
    c = np.zeros((P, CONST_COLS), np.float32)

    def put(name, a):
        c[:a.shape[0], CO[name][0]:CO[name][0] + a.shape[1]] = a
    eye = np.eye(P, dtype=np.float32)
    put("ident", eye)
    put("cdiag", eye - np.float32(1 / C))
    put("coff", np.full((P, P), -1 / C, np.float32))
    put("mean", np.full((P, P), 1 / C, np.float32))
    per = C // 32
    put("group", np.kron(np.eye(P // per), np.full((per, per), 1 / per)).astype(np.float32))
    i64 = np.eye(NQ, dtype=np.float32)
    put("pairI", np.concatenate([i64, i64], 1))
    mask = np.full((QB, QB, KB, KB), -1e30, np.float32)
    for y in range(QB):
        for x in range(QB):
            mask[y, x, y:y + 3, x:x + 3] = 0
    mask = mask.reshape(NQ, NK)
    put("mask", np.tile(mask, (1, 4)))
    left = np.zeros((96, 4, NK), np.float32)
    for j in range(4):
        left[j, j] = -1
        left[32:96, j] = mask
    put("left", left.reshape(96, 4 * NK))
    right = np.zeros((96, P), np.float32)
    right[32:96] = np.concatenate([i64, i64], 1)
    put("right", right)
    return c


def kernel(**inputs):
    import numpy as np
    import concourse.bacc as bacc
    from concourse import mybir as mb
    from concourse.bass_utils import run_bass_kernel_spmd

    w = {k[len("L0_conv_"):]: np.asarray(a) for k, a in inputs.items() if k != "x"}

    def transposed(a):
        a = np.transpose(a)
        return np.ascontiguousarray(a.reshape(-1, P, a.shape[1]).transpose(1, 0, 2))
    arrays = {
        "x": np.ascontiguousarray(inputs["x"]),
        "wqkv": np.ascontiguousarray(np.stack([transposed(w[f"qkv{i}_w"]) for i in (1, 2, 3)], 1)),
        "wproj": np.ascontiguousarray(np.stack([w[f"proj{i}_w"].reshape(CT, P, C).transpose(1, 0, 2) for i in (1, 2, 3)], 1)),
        "wtrans": transposed(w["tc_trans_w"]),
        "wconv": transposed(w["tc_conv_w"]),
        "wpool": transposed(w["tc_pool_w"]),
        "wc1": transposed(w["mlp_c1_w"]),
        "wc2": transposed(w["mlp_c2_w"]),
        "wdw": np.ascontiguousarray(w["mlp_dw_w"].reshape(HT, P, 9).transpose(1, 0, 2)),
        "vecs": np.ascontiguousarray(np.stack([w[n].reshape(CT, P).T for n in VECS], 1)),
        "hvecs": np.ascontiguousarray(np.stack([w[n].reshape(HT, P).T for n in HVECS], 1)),
        "consts": constants(),
    }
    nc = bacc.Bacc("TRN2", target_bir_lowering=False, num_devices=1)
    feed, args = {}, []
    for name, a in arrays.items():
        feed[f"{name}_dram"] = a
        args.append(nc.dram_tensor(f"{name}_dram", a.shape, mb.dt.from_np(a.dtype), kind="ExternalInput").ap())
    args.append(nc.dram_tensor("out_dram", (B, C, H, W), F32, kind="ExternalOutput").ap())
    build(nc, *args)
    r = run_bass_kernel_spmd(nc, [feed], core_ids=[0])
    return r.results[0]["out_dram"]
```

```python
from contextlib import ExitStack

import concourse.bass as bass
from concourse import mybir

F32 = mybir.dt.float32
BF16 = mybir.dt.bfloat16
F16 = mybir.dt.float16
ALU = mybir.AluOpType
ACT = mybir.ActivationFunctionType
AX_X = mybir.AxisListType.X

B, C, H, W = 4, 256, 64, 64
HID = 4 * C
P = 128
CT = C // P
HT = HID // P
PX = H * W
CH_ROWS = 8
CHUNK = CH_ROWS * W
NCH = H // CH_ROWS
HEADS, HD = 8, C // 8
PAIRS = HEADS // 2
QB, KB = 8, 10
NQ, NK = QB * QB, KB * KB
HALO = 3
EPS = 1e-5
START = 1
BN_SCALE = (1.0 + EPS) ** -0.5
ROWS3 = 3 * 3 * QB
N1H, N1W = ROWS3 + 2 * HALO, W + 2 * HALO

ORDER = {1: (0, (2 * QB, QB), (2 * QB, 2 * QB), 3), 2: (0, (2 * QB, 1), (2 * QB, 2 * QB), 3),
         3: (2, (3 * QB, 0), (3 * QB, 3 * QB + 2), 2)}
REST = {1: (7 * QB,), 2: (6 * QB + 1,), 3: (6 * QB, 1, 3 * QB + 1, 6 * QB + 1)}


def blocks_of(r):
    out = []
    for px in range(r):
        n = len(range(px, W, r))
        starts = list(range(0, n - QB + 1, QB))
        if starts[-1] + QB < n:
            starts.append(n - QB)
        done = 0
        for s in starts:
            out.append((px + r * s, done - s))
            done = s + QB
    return out


BLOCKS = {r: blocks_of(r) for r in (1, 2, 3)}
NBMAX = 9
KBANK = 512 // NK
STRIP_BASE = {1: 0, 2: 8, 3: 16}
BLOCK_BASE = {1: 0, 2: 8 * len(BLOCKS[1]), 3: 8 * len(BLOCKS[1]) + 8 * len(BLOCKS[2])}
STRIPS_PER_B = 25
BLOCKS_PER_B = BLOCK_BASE[3] + 9 * len(BLOCKS[3])
TAIL_STRIPS = NCH + 1

PE_TAPS = (2, 3)
V_TAPS = tuple(9 - n for n in PE_TAPS)
STRIP_TAPS = HT // 2 * sum(V_TAPS)


def taps_before(m):
    return m // 2 * sum(V_TAPS) + m % 2 * V_TAPS[0]


VECS = ["ln1_w", "ln1_b", "ln2_w", "ln2_b", "proj1_b", "proj2_b", "proj3_b", "tc_conv_b", "tc_bn1_g", "tc_bn1_b",
        "tc_bn2_g", "tc_bn2_b", "tc_trans_b", "tc_bn3_g", "tc_bn3_b", "mlp_c2_b", "mlp_bn3_g", "mlp_bn3_b"]
HVECS = ["mlp_c1_b", "mlp_bn1_g", "mlp_bn1_b", "mlp_dw_b", "mlp_bn2_g", "mlp_bn2_b"]
CO = {}
_at = 0
for _n, _w in (("ident", P), ("cdiag", P), ("coff", P), ("mean", P), ("group", P), ("pairI", P), ("mask", 4 * NK),
               ("left", 4 * NK), ("right", P)):
    CO[_n] = (_at, _at + _w)
    _at += _w
CONST_COLS = _at


def build(nc, x, wqkv, wproj, wtrans, wconv, wpool, wc1, wc2, wdw, vecs, hvecs, consts, out):
    with ExitStack() as ctx:
        def sb(name, shape, dt=F32):
            return ctx.enter_context(nc.sbuf_tensor(name, shape, dt))

        def sem(name):
            return ctx.enter_context(nc.semaphore(name))

        bank = [ctx.enter_context(nc.psum_tensor(f"bank{i}", [P, 512], F32)) for i in range(8)]

        qkv_w = sb("qkv_w", [P, 2, 3, CT, 3 * C], F16)
        comp_w = sb("comp_w", [P, 3, 2, C])
        conv_w = sb("conv_w", [P, CT, C])
        t0_w = sb("t0_w", [P, CT, C])
        tsum_w = sb("tsum_w", [P, CT, C])
        c1_w = sb("c1_w", [P, 2, CT, HID], F16)
        c2_w = sb("c2_w", [P, HT, C])
        dw_w = sb("dw_w", [P, HT, 9])
        vec = sb("vec", [P, len(VECS), CT])
        hvec = sb("hvec", [P, len(HVECS), HT])
        V = {n: vec[:, i, :] for i, n in enumerate(VECS)}
        HV = {n: hvec[:, i, :] for i, n in enumerate(HVECS)}
        small = sb("small", [P, 48])
        matc = sb("matc", [P, 5, P])
        ident, cdiag, coff, meanm, groupm = (matc[:, i, :] for i in range(5))
        identb = sb("identb", [P, P], BF16)
        pair_b = sb("pair_b", [NQ, P], BF16)
        mask_b = sb("mask_b", [NQ, 4 * NK], BF16)
        left_b = sb("left_b", [96, 4, NK], BF16)
        right_b = sb("right_b", [96, 2, P], BF16)

        g = sb("g", [P, CT, PX])
        n1p = sb("n1p", [P, 2, CT, N1H, N1W], F16)
        acc = sb("acc", [P, CT, ROWS3, W])
        KW = 2 * CT * NBMAX * NK // 2
        QW = 2 * CT * NBMAX * 4 * NQ // 2
        VW = PAIRS * 65
        gflat = g[:].rearrange("p a n -> p (a n)")
        work = sb("work", [P, 3 * KW + 2 * CHUNK + VW])

        def blocks16(a):
            return a.bitcast(F16).rearrange("p (s k i n) -> p s k i n", s=2, k=CT, i=NBMAX)
        qd0 = sb("qd0", [P, QW])
        nbk = [blocks16(work[:, 0:KW]), blocks16(work[:, KW:2 * KW])]
        ks = [blocks16(work[:, 2 * KW:3 * KW]), blocks16(gflat[:, QW:QW + KW])]
        qd = [a.bitcast(F16).rearrange("p (s t i h q) -> p s t i h q", s=2, t=CT, i=NBMAX, h=4) for a in (qd0[:], gflat[:, 0:QW])]
        attn = work[:, 3 * KW:3 * KW + 2 * CHUNK].rearrange("p (a r w) -> p a r w", a=2, r=CH_ROWS)
        o = QW + KW
        pb = [gflat[0:NK, o + i * 512:o + (i + 1) * 512] for i in range(2)]
        o += 2 * 512
        vb = [gflat[0:NK, o + i * VW:o + (i + 1) * VW].rearrange("p (j c) -> p j c", j=PAIRS) for i in range(2)]
        mx = sb("mx", [P, 2, PAIRS], BF16)
        rec = sb("rec", [P, 2, PAIRS])
        an = sb("an", [P, 2, PAIRS, HD])
        sq = work[:, 0:2 * CHUNK].rearrange("p (a n) -> p a n", a=2)
        std = work[:, 1024:1536]
        rstd = work[:, 1536:2048]
        nt = work[:, 2048:3072].rearrange("p (a n) -> p a n", a=2)
        xc = work[:, 3072:4096].rearrange("p (a n) -> p a n", a=2)
        HSW = W + 2
        hs = gflat[:, 0:HT * KB * HSW].rearrange("p (m r w) -> p m r w", m=HT, r=KB)
        o = HT * KB * HSW
        gt = [gflat[:, o + i * CHUNK:o + (i + 1) * CHUNK] for i in range(2)]; o += 2 * CHUNK
        cv = [gflat[:, o + i * CHUNK:o + (i + 1) * CHUNK] for i in range(2)]; o += 2 * CHUNK
        sq2 = [work[:, i * 1024:(i + 1) * 1024].rearrange("p (a n) -> p a n", a=2) for i in range(2)]
        std2 = [work[:, 2048 + i * 512:2560 + i * 512] for i in range(2)]
        nt2 = [work[:, 3072 + i * 1024:4096 + i * 1024].rearrange("p (a n) -> p a n", a=2) for i in range(2)]
        h2 = [sq[:, i, :] for i in range(2)]
        room = (work.shape[1] - 5120) // P
        diag = ([work[:, 5120 + n * P:5120 + (n + 1) * P] for n in range(room)]
                + [gflat[:, o + n * P:o + (n + 1) * P] for n in range((gflat.shape[1] - o) // P)]
                + [work[:, 1024 + n * P:1024 + (n + 1) * P] for n in range(8)])[:HT // 2 * sum(PE_TAPS)]
        xr = work[:, 3072:4096].rearrange("p (t r w) -> p t r w", t=CT, r=CH_ROWS)
        obv = work[:, 4096:5120].rearrange("p (t r w) -> p t r w", t=CT, r=CH_ROWS)
        stage = n1p[:].rearrange("p s a r w -> p (s a r w)").bitcast(F32)
        qkv32 = gflat[:, 0:3 * CT * 3 * C].rearrange("p (i k c) -> p i k c", i=3, k=CT)
        pr_w = stage[:, 0:3 * CT * C].rearrange("p (i k c) -> p i k c", i=3, k=CT)
        c132 = gflat[:, 5120:5120 + CT * HID].rearrange("p (k c) -> p k c", k=CT)
        tr_w = stage[:, 1536:1536 + 10 * C].rearrange("p (k c) -> p k c", k=10)
        cst = stage[:, 4096:4096 + CONST_COLS]
        pool_w = work[:, 4096:4608].rearrange("p (k c) -> p k c", k=CT)
        t4_w = work[:, 4608:5120].rearrange("p (k c) -> p k c", k=CT)
        st = work[:, 0:CT * NCH * 6].rearrange("p (t c n) -> p t c n", t=CT, c=NCH)
        mv = sb("mv", [P, CT, 2])

        def sm(i, n=CT):
            return small[:, i:i + n]
        s1, s2, s3, f3 = sm(0), sm(2), sm(4), sm(6)
        b1c, bias0, fb, tb3 = sm(8), sm(10), sm(12), sm(14)
        hb, hs1, hs2 = sm(16, HT), sm(24, HT), sm(32, HT)
        eps = sm(40, 1)
        ps = sb("ps", [P, 24])
        gstat = ps[:, 0:4]; gm = ps[:, 4:6]; gr = ps[:, 6:8]; gnb = ps[:, 8:10]; pg = ps[:, 10:12]; pv_ = ps[:, 12:14]
        gt2 = ps[:, 14:16]; gsd = ps[:, 16:18]; pin = ps[:, 18:20]

        w_in, setup_v, setup_p = sem("w_in"), sem("setup_v"), sem("setup_p")
        pool_passed, pe_passed, dve_passed, act_passed = sem("pool_passed"), sem("pe_passed"), sem("dve_passed"), sem("act_passed")
        pads_zero, pw_in = sem("pads_zero"), sem("pw_in")
        x_in, stats, group_ready, gstd_done, g_ready = sem("x_in"), sem("stats"), sem("group_ready"), sem("gstd_done"), sem("g_ready")
        gn_chain, pool_ready, pool_done, tbias_ready = sem("gn_chain"), sem("pool_ready"), sem("pool_done"), sem("tbias_ready")
        tb3_done = sem("tb3_done")
        cen_ready, sq_done, var_ready, std_done, rs_done = sem("cen_ready"), sem("sq_done"), sem("var_ready"), sem("std_done"), sem("rs_done")
        affine_done, n1_high = sem("affine_done"), sem("n1_high")
        n_done, n1_done = sem("n_done"), sem("n1_done")
        conv_ready, xc_done, init_ready, acc_init = sem("conv_ready"), sem("xc_done"), sem("init_ready"), sem("acc_init")
        strip_in, piece_ready, hi_done, lo_done = sem("strip_in"), sem("piece_ready"), sem("hi_done"), sem("lo_done")
        v_ready, v_copied, s_ready, max_done = sem("v_ready"), sem("v_copied"), sem("s_ready"), sem("max_done")
        mt_ready, mt_copied, st_ready, exp_done = sem("mt_ready"), sem("mt_copied"), sem("st_ready"), sem("exp_done")
        pv_ready, rec_done, norm_done, at_ready, at_copied = sem("pv_ready"), sem("rec_done"), sem("norm_done"), sem("at_ready"), sem("at_copied")
        comp_ready, acc_added = sem("comp_ready"), sem("acc_added")
        qd_zero = sem("qd_zero")
        hs_zero, t_done = sem("hs_zero"), sem("t_done")
        c1_ready, gelu1_done, h_done, tap_done, shift_done = sem("c1_ready"), sem("gelu1_done"), sem("h_done"), sem("tap_done"), sem("shift_done")
        gelu2_done, c2_ready, res_done, fin_done, xr_in, out_sent = sem("gelu2_done"), sem("c2_ready"), sem("res_done"), sem("fin_done"), sem("xr_in"), sem("out_sent")
        n2_high, n2_stored = sem("n2_high"), sem("n2_stored")
        dw_ready, diag_done = sem("dw_ready"), sem("diag_done")
        cen2_ready, sq2_done, var2_ready, std2_done, rs2_done, n2_done = (sem(n) for n in ("cen2_ready", "sq2_done", "var2_ready", "std2_done", "rs2_done", "n2_done"))

        xv = x.rearrange("b (t p) h w -> b p t (h w)", p=P)
        x4 = x.rearrange("b (t p) h w -> b p t h w", p=P)
        out4 = out.rearrange("b (t p) h w -> b p t h w", p=P)

        def halves(nb):
            return (0, KBANK), (KBANK, nb)

        PIECES = (("k", 0, 0), ("k", 1, 0), ("k", 0, 1), ("k", 1, 1), ("q", 0, 0), ("q", 1, 0))
        NP = len(PIECES)
        PIECE_AT = {8: {1: 0, 2: 1, 3: 2, 4: 3, 5: 4, 6: 5}, 9: {1: 0, 2: 1, 3: 2, 4: 3, 5: 4, 7: 5}}
        DEPTH = 4
        COMP_AT = DEPTH

        def copies(nb, step):
            return {0: range(0, KBANK), 1: range(KBANK, nb)}.get(step, ())

        class Strip:
            def __init__(self, b, r, s, par, row, prev, nxt):
                self.r, self.par, self.row, self.prev, self.nxt = r, par, row, prev, nxt
                self.nb = len(BLOCKS[r])
                self.sc = b * STRIPS_PER_B + (s + STRIP_BASE[r])
                self.bc = b * BLOCKS_PER_B + (s * self.nb + BLOCK_BASE[r])
                self.steps = range(self.nb if nxt else self.nb + DEPTH)

            def has(self, i):
                return (i >= 0 or self.prev is not None) and i < self.nb

            def before(self, n):
                return self.bc + (n if self.prev else max(n, 0)) + START

            def turn(self, i):
                return (self.nb * self.par + i) % 2

            def owner(self, i):
                return (self.r, self.par, i) if i >= 0 else (self.prev[0], 1 - self.par, len(BLOCKS[self.prev[0]]) + i)

        def walk(eng, b, first, strip):
            first(b)
            prev = None
            for r in (1, 2, 3):
                row0, one, two, steps = ORDER[r]
                strip(Strip(b, r, 0, 0, row0, prev, (r, one[1])))
                with eng.Fori(0, steps) as p:
                    a, z = p * one[0] + one[1], p * two[0] + two[1]
                    strip(Strip(b, r, p * 2 + 1, 1, a, (r, p * two[0] + (two[1] - two[0])), (r, z)))
                    strip(Strip(b, r, p * 2 + 2, 0, z, (r, a), (r, p * one[0] + (one[0] + one[1]))))
                prev = (r, steps * two[0] + two[1] - two[0])
                for n, row in enumerate(REST[r]):
                    if n + 1 < len(REST[r]):
                        nxt = (r, REST[r][n + 1])
                    else:
                        nxt = (r + 1, ORDER[r + 1][0]) if r < 3 else None
                    strip(Strip(b, r, 2 * steps + 1 + n, (1 + n) % 2, row, prev, nxt))
                    prev = (r, row)

        def walk_mlp(eng, b, strip):
            top, whole, end = (1, CH_ROWS), (0, CH_ROWS), (0, 1)
            strip(b, 0, top, True, None, True)
            strip(b, 1, whole, True, top, True)
            with eng.Fori(2, NCH - 1) as s:
                strip(b, s, whole, True, whole, True)
            strip(b, NCH - 1, whole, True, whole, False)
            strip(b, NCH, end, False, whole, False)

        block = ctx.enter_context(nc.Block())

        @block.sync
        def _(sp):
            for q in (out_sent,):
                sp.sem_inc(q, START)
            for dst, src in ((pr_w, wproj), (tr_w, wtrans), (cst, consts), (vec[:], vecs), (hvec[:], hvecs),
                             (qkv32, wqkv), (conv_w[:], wconv), (c132, wc1), (c2_w[:], wc2),
                             (dw_w[:], wdw)):
                sp.dma_start(dst, src).then_inc(w_in, 16)

            def residual(b, s, k0, k1):
                sp.wait_ge(fin_done, (b * TAIL_STRIPS + s) * CT + START)
                row = s * CH_ROWS - 1 + k0
                for t in range(CT):
                    sp.dma_start(xr[:, t, k0:k1, :], x4[b, :, t, bass.ds(row, k1 - k0), :]).then_inc(xr_in, 16)
                sp.wait_ge(fin_done, (b * TAIL_STRIPS + s + 1) * CT + START)
                for t in range(CT):
                    sp.dma_start(out4[b, :, t, bass.ds(row, k1 - k0), :], obv[:, t, k0:k1, :]).then_inc(out_sent, 16)

            with sp.Fori(0, B) as b:
                sp.wait_ge(setup_v, 3)
                sp.wait_ge(fin_done, b * TAIL_STRIPS * CT + START)
                for t in range(CT):
                    sp.dma_start(g[:, t, :], xv[b, :, t, :]).then_inc(x_in, 16)
                sp.wait_ge(out_sent, b * (TAIL_STRIPS * CT * 16) + START)
                sp.dma_start(pool_w, wpool).then_inc(pw_in, 16)
                sp.dma_start(t4_w, wtrans[:, 8:10, :]).then_inc(pw_in, 16)
                sp.wait_ge(n2_stored, (b + 1) * NCH + START)
                residual(b, 0, 1, CH_ROWS)
                with sp.Fori(1, NCH) as s:
                    residual(b, s, 0, CH_ROWS)
                residual(b, NCH, 0, 1)
            sp.wait_ge(out_sent, B * TAIL_STRIPS * CT * 16 + START)

        @block.gpsimd
        def _(pool):
            for q in (h_done, shift_done, hs_zero, qd_zero):
                pool.sem_inc(q, START)
            nc.gpsimd.memset(qd0[:], 0.0).then_inc(pads_zero, 1)
            nc.gpsimd.memset(acc[:], 0.0).then_inc(pads_zero, 1)
            pool.wait_ge(setup_v, 1)
            pool.wait_ge(setup_p, 2)
            nc.gpsimd.memset(n1p[:], 0.0).then_inc(pads_zero, 1)
            pool.wait_ge(pads_zero, 3)

            def settle():
                pool.sem_inc(pool_passed, 1)

            def affine1(b, m, s):
                n = (b * NCH + s) * HT + m
                pool.wait_ge(gelu1_done, n + 1 + START)
                settle()
                nc.gpsimd.tensor_scalar(hs[:, m, 2:KB, 1:W + 1], gt[m % 2].rearrange("p (r w) -> p r w", r=CH_ROWS),
                                        hs1[:, m:m + 1], HV["mlp_bn1_b"][:, m:m + 1], ALU.mult, ALU.add).then_inc(h_done, 1)

            def shift(b, m, s):
                n = (b * NCH + s) * HT + m
                pool.wait_ge(tap_done, (b * TAIL_STRIPS + s) * STRIP_TAPS + taps_before(m + 1) + START)
                settle()
                nc.gpsimd.tensor_copy(hs[:, m, 0:2, 1:W + 1], hs[:, m, CH_ROWS:KB, 1:W + 1]).then_inc(shift_done, 1)

            def strip(b, s, rows, fresh, before, more):
                if not fresh:
                    return
                for m in range(HT):
                    if before and m >= 1:
                        pool.wait_ge(shift_done, (b * NCH + s) * HT + START)
                    if not before or m >= 1:
                        affine1(b, m, s)
                    if m >= 1:
                        shift(b, m - 1, s)
                if more:
                    pool.wait_ge(shift_done, (b * NCH + s) * HT + 1 + START)
                    affine1(b, 0, s + 1)
                shift(b, HT - 1, s)

            with pool.Fori(0, B) as b:
                pool.wait_ge(init_ready, (b + 1) * NCH + START)
                pool.wait_ge(var_ready, (b + 1) * NCH + START)
                settle()
                nc.gpsimd.memset(gflat[:, 0:QW], 0.0).then_inc(qd_zero, 1)
                pool.wait_ge(acc_added, (b + 1) * STRIPS_PER_B * CT + START)
                settle()
                nc.gpsimd.memset(hs[:, :, :, 0:HSW:HSW - 1], 0.0)
                nc.gpsimd.memset(hs[:, :, 0:2, 1:W + 1], 0.0).then_inc(hs_zero, 1)
                walk_mlp(pool, b, strip)
                pool.wait_ge(shift_done, (b + 1) * NCH * HT + START)
                settle()
                nc.gpsimd.memset(hs[:, :, 2:3, :], 0.0).then_inc(hs_zero, 1)

        @block.tensor
        def _(pe):
            for q in (cen_ready, var_ready, conv_ready, init_ready, group_ready, pool_ready, tbias_ready, piece_ready,
                      v_ready, s_ready, mt_ready, st_ready, pv_ready, at_ready, comp_ready, cen2_ready, var2_ready,
                      c1_ready, c2_ready, dw_ready):
                pe.sem_inc(q, START)
            mm = nc.tensor.matmul
            pe.wait_ge(w_in, 10 * 16)
            for i in range(3):
                for j in range(PAIRS):
                    for hp in range(2):
                        a = (2 * j + hp) * HD
                        for k in range(CT):
                            last = mm(bank[i][j * HD:(j + 1) * HD, hp * C:(hp + 1) * C], pr_w[:, i, k, a:a + HD],
                                      tr_w[:, 2 * (i + 1) + k, :], start=(k == 0), stop=(k == CT - 1))
            last.then_inc(setup_p, 1)
            for t in range(CT):
                n = 0
                for i in range(3):
                    for k in range(CT):
                        last = mm(bank[3][:, t:t + 1], tr_w[:, 2 * (i + 1) + k, t * P:(t + 1) * P],
                                  V[f"proj{i + 1}_b"][:, k:k + 1], start=(n == 0), stop=(n == 5))
                        n += 1
            for m in range(HT):
                for k in range(CT):
                    mm(bank[4][:, m:m + 1], c132[:, k, m * P:(m + 1) * P], V["ln2_b"][:, k:k + 1],
                       start=(k == 0), stop=(k == CT - 1))
            for t in range(CT):
                for m in range(HT):
                    last = mm(bank[5][:, t:t + 1], c2_w[:, m, t * P:(t + 1) * P], HV["mlp_bn2_b"][:, m:m + 1],
                              start=(m == 0), stop=(m == HT - 1))
            last.then_inc(setup_p, 1)
            pe.wait_ge(setup_v, 3)
            pe.wait_ge(pads_zero, 3)

            def gn_and_pool(b):
                pe.wait_ge(stats, b + 1 + START)
                mm(bank[7][:, 0:4], groupm, gstat, start=True, stop=True).then_inc(group_ready, 1)
                pe.wait_ge(g_ready, b + 1 + START)
                pe.wait_ge(pw_in, (b + 1) * 32)
                for t in range(CT):
                    for k in range(CT):
                        last = mm(bank[7][:, 8 + t:9 + t], pool_w[:, k, t * P:(t + 1) * P], pg[:, k:k + 1],
                                  start=(k == 0), stop=(k == CT - 1))
                last.then_inc(pool_ready, 1)
                pe.wait_ge(pool_done, b + 1 + START)
                for t in range(CT):
                    for k in range(CT):
                        last = mm(bank[7][:, 16 + t:17 + t], t4_w[:, k, t * P:(t + 1) * P], pv_[:, k:k + 1],
                                  start=(k == 0), stop=(k == CT - 1))
                last.then_inc(tbias_ready, 1)

            def front(b, c):
                n = b * NCH + c
                gc = [g[:, k, bass.ds(c * CHUNK, CHUNK)] for k in range(CT)]
                pe.wait_ge(n_done, n + START)
                for t in range(CT):
                    for k in range(CT):
                        last = mm(bank[t][:, :], cdiag if t == k else coff, gc[k], start=(k == 0), stop=(k == CT - 1))
                last.then_inc(cen_ready, 1)
                pe.wait_ge(xc_done, n + START)
                for t in range(CT):
                    for k in range(CT):
                        last = mm(bank[3 + t][:, :], conv_w[:, k, t * P:(t + 1) * P], gc[k], start=(k == 0), stop=(k == CT - 1))
                last.then_inc(conv_ready, 1)
                pe.wait_ge(sq_done, n + 1 + START)
                pe.wait_ge(std_done, n + START)
                for k in range(CT):
                    last = mm(bank[2][:, :], meanm, sq[:, k, :], start=(k == 0), stop=(k == CT - 1))
                last.then_inc(var_ready, 1)
                pe.wait_ge(acc_init, n + START)
                for t in range(CT):
                    for k in range(CT):
                        mm(bank[5 + t][:, :], tsum_w[:, k, t * P:(t + 1) * P], gc[k], start=(k == 0), stop=False)
                pe.wait_ge(xc_done, n + 1 + START)
                for t in range(CT):
                    for k in range(CT):
                        last = mm(bank[5 + t][:, :], t0_w[:, k, t * P:(t + 1) * P], xc[:, k, :], start=False, stop=(k == CT - 1))
                last.then_inc(init_ready, 1)

            def piece(sc, par, r, n):
                kind, t, half = PIECES[n]
                nb, x = len(BLOCKS[r]), nbk[par]
                pe.wait_ge(strip_in, sc * 2 + (1 if n < 2 else 2) + START)
                pe.wait_ge(lo_done, sc * NP + n + START)

                def inner(s, k, i0, i1):
                    return x[:, s, k, i0:i1, :].rearrange("p i (y x) -> p i y x", y=KB)[:, :, 1:1 + QB, 1:1 + QB]

                def product(to, col, moving):
                    for m, (s, k) in enumerate([(s, k) for s in ((0, 0), (0, 1), (1, 0)) for k in range(CT)]):
                        last = mm(to, qkv_w[:, s[0], r - 1, k, col:col + P], moving(s[1], k), start=(m == 0), stop=(m == 5))
                    return last
                if kind == "q":
                    last = product(bank[3][:, :], t * P, lambda s, k: inner(s, k, 0, 8))
                else:
                    i0, i1 = halves(nb)[half]
                    last = product(bank[3][:, 0:(i1 - i0) * NK], C + t * P, lambda s, k: x[:, s, k, i0:i1, :].rearrange("p i n -> p (i n)"))
                    if half == 1 and nb > 8:
                        last = product(bank[3][:, 448:512], t * P, lambda s, k: inner(s, k, 8, 9))
                last.then_inc(piece_ready, 1)

            def first(b):
                for n in range(NP):
                    piece(b * STRIPS_PER_B, 0, 1, n)

            def strip(at):
                def scores(i):
                    q, kk, bk = qd[at.par], ks[at.par], bank[at.turn(i)]
                    if i == 0:
                        pe.wait_ge(hi_done, (at.sc + 1) * NP + START)
                    pe.wait_ge(max_done, at.before(i - 1))
                    mm(bk[:, 0:4 * NK], pair_b[:], mask_b[:], start=True, stop=False)
                    for j in range(PAIRS):
                        t, u = j // 2, j % 2
                        last = mm(bk[:, j * NK:(j + 1) * NK], q[:, 0, t, i, 2 * u:2 * u + 2, :].rearrange("p h q -> p (h q)"),
                                  kk[:, 0, t, i, :], start=False, stop=(j == PAIRS - 1))
                    last.then_inc(s_ready, 1)

                def weigh(i):
                    pe.wait_ge(exp_done, at.before(i + 1))
                    pe.wait_ge(norm_done, at.before(i))
                    for j in range(PAIRS):
                        last = mm(bank[6][:, j * 65:(j + 1) * 65], pb[at.turn(i)][:, j * P:(j + 1) * P], vb[at.turn(i)][:, j, :], start=True, stop=True)
                    last.then_inc(pv_ready, 1)

                def turn_out(i):
                    pe.wait_ge(norm_done, at.before(i + 1))
                    pe.wait_ge(mt_copied, at.before(min(i + 3, at.nb)))
                    pe.wait_ge(at_copied, at.before(i))
                    nc.tensor.transpose(bank[7][:, 0:P], an[:, at.turn(i)].rearrange("p j c -> p (j c)"), ident).then_inc(at_ready, 1)

                def project(sc, r):
                    for t in range(CT):
                        for hp in range(2):
                            last = mm(bank[3 - t][:, :], comp_w[:, r - 1, hp, t * P:(t + 1) * P],
                                      attn[:, hp].rearrange("p r w -> p (r w)"), start=(hp == 0), stop=(hp == 1))
                        last.then_inc(comp_ready, 1)

                def scores_t(i):
                    r, par, n = at.owner(i)
                    q, kk, bk = qd[par], ks[par], bank[4 + at.turn(i)]
                    if i == 0:
                        pe.wait_ge(lo_done, (at.sc + 1) * NP + START)
                    pe.wait_ge(mt_copied, at.before(i + 1))
                    pe.wait_ge(exp_done, at.before(i - 1))
                    for t in range(CT):
                        for m, (s0, s1) in enumerate([(0, 0), (0, 1), (1, 0)]):
                            mm(bk[0:NK, t * 256:(t + 1) * 256], kk[:, s0, t, n, :], q[:, s1, t, n].rearrange("p h q -> p (h q)"),
                               start=(t == 0 and m == 0), stop=False)
                    for j in range(PAIRS):
                        last = mm(bk[0:NK, j * P:(j + 1) * P], left_b[:, j, :], right_b[:, at.turn(i), :], start=False, stop=(j == PAIRS - 1))
                    last.then_inc(st_ready, 1)

                def values(i):
                    r, par, n = at.owner(i)
                    x = nbk[par]
                    if i == 0 and at.prev is None:
                        pe.wait_ge(strip_in, (at.sc + 1) * 2 + START)
                    if i == COMP_AT - 1 and at.prev:
                        pe.wait_ge(acc_added, at.sc * CT + START)
                    pe.wait_ge(v_copied, at.before(i))
                    for m, (s0, s1, k) in enumerate([(0, 0, 0), (0, 1, 0), (0, 0, 1), (0, 1, 1), (1, 0, 0), (1, 0, 1)]):
                        last = mm(bank[2][0:NK, 0:C], x[:, s0, k, n, :], qkv_w[:, s1, r - 1, k, 2 * C:3 * C], start=(m == 0), stop=(m == 5))
                    last.then_inc(v_ready, 1)

                def turn_max(i):
                    pe.wait_ge(max_done, at.before(i + 1))
                    pe.wait_ge(at_copied, at.before(i - 2))
                    pe.wait_ge(mt_copied, at.before(i))
                    nc.tensor.transpose(bank[7][0:PAIRS, 128:128 + P // 2].bitcast(BF16), mx[:, at.turn(i), :], identb[:]).then_inc(mt_ready, 1)

                for i in at.steps:
                    if i < at.nb:
                        scores(i)
                    if at.has(i - 3):
                        weigh(i - 3)
                    if at.has(i - 4):
                        turn_out(i - 4)
                    if i == COMP_AT and at.prev:
                        pe.wait_ge(at_copied, at.before(0))
                        pe.wait_ge(lo_done, (at.sc + 1) * NP + (COMP_AT - 1 if at.nxt else 0) + START)
                        pe.wait_ge(v_copied, at.before(COMP_AT - 1))
                        project(at.sc, at.prev[0])
                    if at.has(i - 2):
                        scores_t(i - 2)
                    if at.has(i - 1):
                        values(i - 1)
                        turn_max(i - 1)
                    if at.nxt and i in PIECE_AT[at.nb]:
                        piece(at.sc + 1, 1 - at.par, at.nxt[0], PIECE_AT[at.nb][i])
                if not at.nxt:
                    pe.wait_ge(at_copied, at.before(at.nb))
                    pe.wait_ge(acc_added, at.sc * CT + START)
                    pe.wait_ge(v_copied, at.before(at.nb))
                    project(at.sc, at.r)

            def layer_norm2(b, p):
                n0 = b * NCH + p * 2
                pe.wait_ge(n2_done, n0 + START)
                for j in range(2):
                    pe.wait_ge(t_done, n0 + j + 1 + START)
                    tc = [acc[:, k, bass.ds(p * (2 * CH_ROWS) + j * CH_ROWS, CH_ROWS), :] for k in range(CT)]
                    for t in range(CT):
                        for k in range(CT):
                            last = mm(bank[3 * j + t][:, :], cdiag if t == k else coff, tc[k], start=(k == 0), stop=(k == CT - 1))
                    last.then_inc(cen2_ready, 1)
                for j in range(2):
                    pe.wait_ge(sq2_done, n0 + j + 1 + START)
                    for k in range(CT):
                        last = mm(bank[3 * j + 2][:, :], meanm, sq2[j][:, k, :], start=(k == 0), stop=(k == CT - 1))
                    last.then_inc(var2_ready, 1)

            def tail(b, s, rows, fresh, before, more):
                n = b * NCH + s
                f = b * TAIL_STRIPS + s

                def up(m):
                    if m == 0:
                        pe.wait_ge(n2_stored, (b + 1) * NCH + START)
                        pe.wait_ge(gelu1_done, n * HT + START)
                    else:
                        pe.wait_ge(gelu1_done, n * HT + m - 1 + START)
                    j = m % HT
                    for i, (s0, s1, k) in enumerate([(0, 0, 0), (0, 1, 0), (1, 0, 0), (0, 0, 1), (0, 1, 1), (1, 0, 1)]):
                        last = mm(bank[3 + m % 2][:, :], c1_w[:, s0, k, j * P:(j + 1) * P],
                                  n1p[:, s1, k, bass.ds(s * CH_ROWS + (m // HT * CH_ROWS + HALO), CH_ROWS), HALO:HALO + W], start=(i == 0), stop=(i == 5))
                    last.then_inc(c1_ready, 1)

                def taps(m, k0, k1):
                    if fresh:
                        pe.wait_ge(h_done, n * HT + m + 1 + START)
                    if m == 0:
                        pe.wait_ge(diag_done, b + 1 + START)
                        if not fresh:
                            pe.wait_ge(hs_zero, b * 2 + 2 + START)
                    if before or m >= 2:
                        pe.wait_ge(tap_done, f * STRIP_TAPS + (taps_before(m - 2) + 1) + START)
                    for k in range(PE_TAPS[m % 2]):
                        last = mm(bank[m % 2][:, k0 * W:k1 * W], diag[m // 2 * sum(PE_TAPS) + m % 2 * PE_TAPS[0] + k],
                                  hs[:, m, k0 + k // 3:k1 + k // 3, k % 3:k % 3 + W], start=(k == 0), stop=(k == PE_TAPS[m % 2] - 1))
                    last.then_inc(dw_ready, 1)

                def down(m, k0, k1):
                    pe.wait_ge(gelu2_done, f * HT + m + 1 + START)
                    if m == 0:
                        pe.wait_ge(res_done, f * CT + START)
                    j = m % HT
                    for t in range(CT):
                        last = mm(bank[5 + t][:, k0 * W:k1 * W], c2_w[:, j, t * P:(t + 1) * P], h2[m % 2][:, k0 * W:k1 * W],
                                  start=(j == 0), stop=(j == HT - 1))
                    last.then_inc(c2_ready, 1)
                if not before:
                    up(0)
                for m in range(HT):
                    if fresh and (m + 1 < HT or more):
                        up(m + 1)
                    taps(m, *rows)
                    if m >= 1:
                        down(m - 1, *rows)
                    elif before:
                        down(-1, *before)
                if not fresh:
                    down(HT - 1, *rows)

            with pe.Fori(0, B) as b:
                gn_and_pool(b)
                with pe.Fori(0, NCH) as c:
                    front(b, c)
                pe.wait_ge(acc_init, (b + 1) * NCH + START)
                pe.sem_inc(pe_passed, 1)
                walk(pe, b, first, strip)
                with pe.Fori(0, NCH // 2) as p:
                    layer_norm2(b, p)
                walk_mlp(pe, b, tail)

        @block.vector
        def _(dve):
            for q in (stats, g_ready, pool_done, tb3_done, rs_done, n_done, n1_high, n1_done, acc_init, lo_done, max_done,
                      mt_copied, rec_done, norm_done, at_copied, acc_added, tap_done, res_done, fin_done, rs2_done,
                      n2_done, n2_high, n2_stored, diag_done):
                dve.sem_inc(q, START)
            v = nc.vector
            dve.wait_ge(w_in, 10 * 16)
            nchain = [0]

            def link(ins):
                nchain[0] += 1
                ins.then_inc(gn_chain, 1)
                dve.wait_ge(gn_chain, nchain[0])

            def cc(name):
                a, e = CO[name]
                return cst[:, a:e]
            v.memset(eps, EPS)
            for i, n in enumerate(("ident", "cdiag", "coff", "mean", "group")):
                v.tensor_copy(matc[:, i, :], cc(n))
            v.tensor_copy(identb[:], cc("ident"))
            v.tensor_copy(pair_b[:], cc("pairI")[0:NQ, :])
            v.tensor_copy(mask_b[:], cc("mask")[0:NQ, :])
            v.tensor_copy(left_b[:].rearrange("p j n -> p (j n)"), cc("left")[0:96, :])
            for i in range(2):
                v.tensor_copy(right_b[:, i, :], cc("right")[0:96, :])
            v.tensor_copy(t0_w[:].rearrange("p k c -> p (k c)"), tr_w[:, 0:2, :].rearrange("p k c -> p (k c)"))
            link(v.tensor_tensor(tsum_w[:], tr_w[:, 2:4, :], tr_w[:, 4:6, :], ALU.add))
            v.tensor_tensor(tsum_w[:], tsum_w[:], tr_w[:, 6:8, :], ALU.add).then_inc(setup_v, 1)
            for i in range(3):
                last = v.tensor_copy(qkv_w[:, 0, i], qkv32[:, i])
            link(last)
            for i in range(3):
                v.tensor_tensor(qkv_w[:, 1, i], qkv32[:, i], qkv_w[:, 0, i], ALU.subtract)
            for dst, n in ((s1, "tc_bn1_g"), (s2, "tc_bn2_g"), (s3, "tc_bn3_g"), (f3, "mlp_bn3_g")):
                v.tensor_scalar(dst, V[n], BN_SCALE, None, ALU.mult)
            v.tensor_scalar(hs1, HV["mlp_bn1_g"], BN_SCALE, None, ALU.mult)
            link(v.tensor_scalar(hs2, HV["mlp_bn2_g"], BN_SCALE, None, ALU.mult))
            link(v.tensor_tensor(b1c, s1, V["tc_conv_b"], ALU.mult))
            link(v.tensor_tensor(b1c, b1c, V["tc_bn1_b"], ALU.add))
            dve.wait_ge(setup_p, 2)
            for i in range(3):
                v.tensor_copy(comp_w[:, i].rearrange("p e c -> p (e c)"), bank[i][:, :])
            v.tensor_tensor(bias0, bank[3][:, 0:CT], V["tc_trans_b"], ALU.add)
            v.tensor_tensor(hb, bank[4][:, 0:HT], HV["mlp_c1_b"], ALU.add)
            link(v.tensor_tensor(fb, bank[5][:, 0:CT], V["mlp_c2_b"], ALU.add))
            link(v.tensor_tensor(fb, fb, f3, ALU.mult))
            link(v.tensor_tensor(fb, fb, V["mlp_bn3_b"], ALU.add))
            for k in range(CT):
                last = v.tensor_scalar(c132[:, k, :], c132[:, k, :], V["ln2_w"][:, k:k + 1], None, ALU.mult)
            link(last)
            link(v.tensor_copy(c1_w[:, 0], c132))
            v.tensor_tensor(c1_w[:, 1], c132, c1_w[:, 0], ALU.subtract)
            for m in range(HT):
                v.tensor_scalar(c2_w[:, m, :], c2_w[:, m, :], hs2[:, m:m + 1], None, ALU.mult)
            v.tensor_scalar(dw_w[:, :, 4:5], dw_w[:, :, 4:5], 1.0, None, ALU.add).then_inc(setup_v, 2)
            dve.wait_ge(setup_v, 3)
            SETUP = nchain[0]
            assert SETUP == SETUP_LINKS
            PER_B = [0]

            def group_norm(b):
                cnt = [0]

                def step(ins):
                    cnt[0] += 1
                    ins.then_inc(gn_chain, 1)
                    dve.wait_ge(gn_chain, b * GN_STEPS + (SETUP + cnt[0]))
                dve.wait_ge(x_in, (b + 1) * CT * 16)
                for t in range(CT):
                    for c in range(NCH):
                        last = v.bn_stats(st[:, t, c, :], g[:, t, c * CHUNK:(c + 1) * CHUNK])
                step(last)
                dve.sem_inc(dve_passed, 1)
                for t in range(CT):
                    last = v.bn_aggr(mv[:, t, :], st[:, t, :, :])
                step(last)
                v.tensor_copy(gstat[:, 0:2], mv[:, :, 0])
                step(v.tensor_tensor(gt2, mv[:, :, 0], mv[:, :, 0], ALU.mult))
                v.tensor_tensor(gstat[:, 2:4], gt2, mv[:, :, 1], ALU.add).then_inc(stats, 1)
                dve.wait_ge(group_ready, b + 1 + START)
                step(v.tensor_copy(gm, bank[7][:, 0:2]))
                step(v.tensor_tensor(gt2, gm, gm, ALU.mult))
                step(v.scalar_tensor_tensor(gt2, bank[7][:, 2:4], EPS, gt2, ALU.add, ALU.subtract))
                dve.wait_ge(gstd_done, b + 1 + START)
                step(v.reciprocal(gr, gsd))
                step(v.tensor_tensor(gnb, gm, gr, ALU.mult))
                v.tensor_tensor(pin, mv[:, :, 0], gm, ALU.subtract)
                for t in range(CT):
                    last = v.tensor_scalar(g[:, t, :], g[:, t, :], gr[:, t:t + 1], gnb[:, t:t + 1], ALU.mult, ALU.subtract)
                step(last)
                v.tensor_tensor(pg, pin, gr, ALU.mult).then_inc(g_ready, 1)
                dve.wait_ge(pool_ready, b + 1 + START)
                step(v.tensor_tensor(pv_, bank[7][:, 8:10], s2, ALU.mult))
                step(v.tensor_tensor(pv_, pv_, V["tc_bn2_b"], ALU.add))
                v.tensor_scalar(pv_, pv_, 0.0, None, ALU.max).then_inc(pool_done, 1)
                dve.wait_ge(tbias_ready, b + 1 + START)
                step(v.tensor_tensor(tb3, bank[7][:, 16:18], bias0, ALU.add))
                step(v.tensor_tensor(tb3, tb3, s3, ALU.mult))
                v.tensor_tensor(tb3, tb3, V["tc_bn3_b"], ALU.add).then_inc(tb3_done, 1)
                return cnt[0]

            GN_STEPS = 13

            def front(b, c):
                n = b * NCH + c
                dve.wait_ge(std_done, n + 1 + START)
                v.reciprocal(rstd, std).then_inc(rs_done, 1)
                dve.wait_ge(rs_done, n + 1 + START)
                dve.wait_ge(n1_done, n + START)
                for t in range(CT):
                    last = v.tensor_tensor(nt[:, t, :], bank[t][:, :], rstd, ALU.mult)
                last.then_inc(n_done, 1)
                dve.wait_ge(init_ready, n + 1 + START)
                for t in range(CT):
                    last = v.tensor_copy(acc[:, t, bass.ds(c * CH_ROWS, CH_ROWS), :], bank[5 + t][:, :].rearrange("p (r w) -> p r w", r=CH_ROWS))
                last.then_inc(acc_init, 1)
                dve.wait_ge(affine_done, n + 1 + START)
                rows = [[n1p[:, h, t, bass.ds(c * CH_ROWS + HALO, CH_ROWS), HALO:HALO + W] for t in range(CT)] for h in range(2)]
                nr = [nt[:, t, :].rearrange("p (r w) -> p r w", r=CH_ROWS) for t in range(CT)]
                for t in range(CT):
                    last = v.tensor_copy(rows[0][t], nr[t])
                last.then_inc(n1_high, 1)
                dve.wait_ge(n1_high, n + 1 + START)
                for t in range(CT):
                    last = v.tensor_tensor(rows[1][t], nr[t], rows[0][t], ALU.subtract)
                last.then_inc(n1_done, 1)

            def low_part(sc, par, r, n):
                kind, t, half = PIECES[n]
                nb = len(BLOCKS[r])
                q, kk = qd[par], ks[par]
                dve.wait_ge(hi_done, sc * NP + n + 1 + START)

                def queries(i0, i1, psum):
                    for h in range(4):
                        hp = slice(HD * h, HD * h + HD)
                        last = v.tensor_tensor(q[hp, 1, t, i0:i1, h, :], psum[hp, :].rearrange("p (i q) -> p i q", q=NQ), q[hp, 0, t, i0:i1, h, :], ALU.subtract)
                    return last
                if kind == "q":
                    last = queries(0, 8, bank[3])
                else:
                    i0, i1 = halves(nb)[half]
                    n_ = (i1 - i0) * NK
                    last = v.tensor_tensor(kk[:, 1, t, i0:i1, :].rearrange("p i n -> p (i n)"), bank[3][:, 0:n_],
                                           kk[:, 0, t, i0:i1, :].rearrange("p i n -> p (i n)"), ALU.subtract)
                    if half == 1 and nb > 8:
                        last = queries(8, 9, bank[3][:, 448:512])
                last.then_inc(lo_done, 1)

            def first(b):
                for n in range(NP):
                    low_part(b * STRIPS_PER_B, 0, 1, n)

            def strip(at):
                def take_max(i):
                    dve.wait_ge(s_ready, at.before(i + 1))
                    dve.wait_ge(mt_ready, at.before(i - 1))
                    v.tensor_reduce(mx[:, at.turn(i), :], bank[at.turn(i)][:, 0:4 * NK].rearrange("p (j n) -> p j n", j=PAIRS), AX_X, ALU.max).then_inc(max_done, 1)

                def copy_max(i):
                    dve.wait_ge(mt_ready, at.before(i + 1))
                    dve.wait_ge(st_ready, at.before(i - 1))
                    v.tensor_copy(right_b[0:PAIRS, at.turn(i), :], bank[7][0:PAIRS, 128:128 + P // 2].bitcast(BF16)).then_inc(mt_copied, 1)

                def normalise(i):
                    o_ = bank[6][:, 0:PAIRS * 65].rearrange("p (j c) -> p j c", j=PAIRS)
                    dve.wait_ge(pv_ready, at.before(i + 1))
                    v.reciprocal(rec[:, at.turn(i), :], o_[:, :, 64]).then_inc(rec_done, 1)
                    dve.wait_ge(rec_done, at.before(i + 1))
                    dve.wait_ge(at_ready, at.before(i - 1))
                    for hp in range(2):
                        q = slice(NQ * hp, NQ * hp + NQ)
                        last = v.tensor_tensor(an[q, at.turn(i)], o_[q, :, HD * hp:HD * hp + HD],
                                               rec[q, at.turn(i), :].unsqueeze(2).to_broadcast([NQ, PAIRS, HD]), ALU.mult)
                    last.then_inc(norm_done, 1)

                def copy_out(i):
                    r, _, n = at.owner(i)
                    c0, skip = BLOCKS[r][n]
                    dve.wait_ge(at_ready, at.before(i + 1))
                    if i == 0:
                        dve.wait_ge(comp_ready, at.sc * CT + START)
                    a = c0 + skip * r
                    v.tensor_copy(attn[:, :, :, a:c0 + (QB - 1) * r + 1:r],
                                  bank[7][:, 0:P].rearrange("p (e y x) -> p e y x", e=2, y=QB)[:, :, :, skip:]).then_inc(at_copied, 1)

                def add(sc, r, row):
                    for t in range(CT):
                        dve.wait_ge(comp_ready, sc * CT + t + 1 + START)
                        dve.wait_ge(acc_added, sc * CT + t + START)
                        a = acc[:, t, bass.ds(row, QB, r), :]
                        v.tensor_tensor(a, bank[3 - t][:, :].rearrange("p (r w) -> p r w", r=QB), a, ALU.add).then_inc(acc_added, 1)

                for i in at.steps:
                    if at.has(i - 2):
                        copy_max(i - 2)
                    if i < at.nb:
                        take_max(i)
                    made = PIECE_AT[at.nb].get(i - 1) if at.nxt else None
                    if made is not None and PIECES[made][0] == "k":
                        low_part(at.sc + 1, 1 - at.par, at.nxt[0], made)
                    if i == COMP_AT and at.prev:
                        add(at.sc - 1, *at.prev)
                    if at.has(i - 3):
                        normalise(i - 3)
                    if at.has(i - 4):
                        copy_out(i - 4)
                    if made is not None and PIECES[made][0] == "q":
                        low_part(at.sc + 1, 1 - at.par, at.nxt[0], made)
                if not at.nxt:
                    add(at.sc, at.r, at.row)

            def layer_norm2(b, p):
                n0 = b * NCH + p * 2
                for j in range(2):
                    dve.wait_ge(std2_done, n0 + j + 1 + START)
                    v.reciprocal(std2[j], std2[j]).then_inc(rs2_done, 1)
                    dve.wait_ge(rs2_done, n0 + j + 1 + START)
                    for t in range(CT):
                        last = v.tensor_tensor(nt2[j][:, t, :], bank[3 * j + t][:, :], std2[j], ALU.mult)
                    last.then_inc(n2_done, 1)
                rows = [[[n1p[:, h, t, bass.ds(p * (2 * CH_ROWS) + (j * CH_ROWS + HALO), CH_ROWS), HALO:HALO + W] for t in range(CT)] for h in range(2)] for j in range(2)]
                nr = [[nt2[j][:, t, :].rearrange("p (r w) -> p r w", r=CH_ROWS) for t in range(CT)] for j in range(2)]
                dve.wait_ge(n2_done, n0 + 2 + START)
                for j in range(2):
                    for t in range(CT):
                        last = v.tensor_copy(rows[j][0][t], nr[j][t])
                    last.then_inc(n2_high, 1)
                for j in range(2):
                    dve.wait_ge(n2_high, n0 + j + 1 + START)
                    for t in range(CT):
                        last = v.tensor_tensor(rows[j][1][t], nr[j][t], rows[j][0][t], ALU.subtract)
                    last.then_inc(n2_stored, 1)

            def diagonals(b):
                for m in range(HT):
                    for k in range(PE_TAPS[m % 2]):
                        last = v.tensor_scalar(diag[m // 2 * sum(PE_TAPS) + m % 2 * PE_TAPS[0] + k], ident, dw_w[:, m, k:k + 1], None, ALU.mult)
                last.then_inc(diag_done, 1)

            def tail(b, s, rows, fresh, before, more):
                n = b * NCH + s
                f = b * TAIL_STRIPS + s

                def taps(m, k0, k1):
                    tap0 = f * STRIP_TAPS + taps_before(m)
                    if fresh:
                        dve.wait_ge(h_done, n * HT + m + 1 + START)
                    elif m == 0:
                        dve.wait_ge(hs_zero, b * 2 + 2 + START)
                    dve.wait_ge(gelu2_done, f * HT + (m - 1 if before else max(m - 1, 0)) + START)
                    dve.wait_ge(dw_ready, f * HT + m + 1 + START)
                    cvm = cv[m % 2][:, k0 * W:k1 * W].rearrange("p (r w) -> p r w", r=k1 - k0)
                    for i, k in enumerate(range(PE_TAPS[m % 2], 9)):
                        win = hs[:, m, k0 + k // 3:k1 + k // 3, k % 3:k % 3 + W]
                        so_far = bank[m % 2][:, k0 * W:k1 * W].rearrange("p (r w) -> p r w", r=k1 - k0) if i == 0 else cvm
                        if i:
                            dve.wait_ge(tap_done, tap0 + i + START)
                        v.scalar_tensor_tensor(cvm, win, dw_w[:, m, k:k + 1], so_far, ALU.mult, ALU.add).then_inc(tap_done, 1)

                def residuals(ago, k0, k1):
                    dve.wait_ge(c2_ready, (f + (1 - ago)) * HT + START)
                    for t in range(CT):
                        o_ = obv[:, t, k0:k1, :]
                        dve.wait_ge(out_sent, (f - ago) * (CT * 16) + START)
                        v.scalar_tensor_tensor(o_, bank[5 + t][:, k0 * W:k1 * W].rearrange("p (r w) -> p r w", r=k1 - k0), f3[:, t:t + 1],
                                               acc[:, t, bass.ds((s - ago) * CH_ROWS - 1 + k0, k1 - k0), :], ALU.mult, ALU.add).then_inc(res_done, 1)
                    dve.wait_ge(xr_in, (f + (1 - ago)) * (CT * 16))
                    for t in range(CT):
                        o_ = obv[:, t, k0:k1, :]
                        dve.wait_ge(res_done, (f - ago) * CT + t + 1 + START)
                        v.scalar_tensor_tensor(o_, o_, fb[:, t:t + 1], xr[:, t, k0:k1, :], ALU.add, ALU.add).then_inc(fin_done, 1)

                for m in range(HT):
                    taps(m, *rows)
                    if m == 0 and before:
                        residuals(1, *before)
                if not fresh:
                    residuals(0, *rows)

            with dve.Fori(0, B) as b:
                assert group_norm(b) == GN_STEPS
                with dve.Fori(0, NCH) as c:
                    front(b, c)
                dve.wait_ge(n1_done, (b + 1) * NCH + START)
                dve.wait_ge(init_ready, (b + 1) * NCH + START)
                dve.wait_ge(acc_init, (b + 1) * NCH + START)
                for i in range(2):
                    v.memset(vb[i][:, :, 64:65], 1.0)
                walk(dve, b, first, strip)
                with dve.Fori(0, NCH // 2) as p:
                    layer_norm2(b, p)
                dve.wait_ge(n2_stored, (b + 1) * NCH + START)
                diagonals(b)
                walk_mlp(dve, b, tail)

        @block.scalar
        def _(act):
            for q in (gstd_done, sq_done, xc_done, std_done, affine_done, hi_done, strip_in, v_copied, exp_done, gelu1_done,
                      gelu2_done, t_done, sq2_done, std2_done):
                act.sem_inc(q, START)
            fn = nc.scalar.activation
            act.wait_ge(setup_v, 3)

            def group_std(b):
                act.wait_ge(gn_chain, b * 13 + GN_BASE + 6)
                fn(gsd, gt2, ACT.Sqrt).then_inc(gstd_done, 1)

            def front(b, c):
                n = b * NCH + c
                act.wait_ge(cen_ready, n + 1 + START)
                act.wait_ge(var_ready, n + START)
                for t in range(CT):
                    last = fn(sq[:, t, :], bank[t][:, :], ACT.Square)
                last.then_inc(sq_done, 1)
                act.wait_ge(conv_ready, n + 1 + START)
                act.wait_ge(init_ready, n + START)
                for t in range(CT):
                    last = fn(xc[:, t, :], bank[3 + t][:, :], ACT.Relu, bias=b1c[:, t:t + 1], scale=s1[:, t:t + 1])
                last.then_inc(xc_done, 1)
                act.wait_ge(var_ready, n + 1 + START)
                act.wait_ge(rs_done, n + START)
                fn(std, bank[2][:, :], ACT.Sqrt, bias=eps).then_inc(std_done, 1)
                act.wait_ge(n_done, n + 1 + START)
                for t in range(CT):
                    last = fn(nt[:, t, :], nt[:, t, :], ACT.Identity, scale=V["ln1_w"][:, t:t + 1], bias=V["ln1_b"][:, t:t + 1])
                last.then_inc(affine_done, 1)

            def copy_blocks(par, r, row0, blocks):
                for i in blocks:
                    a = BLOCKS[r][i][0] + HALO - r
                    last = fn(nbk[par][:, :, :, i, :].rearrange("p s k (y x) -> p (s k) y x", y=KB),
                              n1p[:, :, :, bass.ds(row0 + HALO - r, KB, r), a:a + (KB - 1) * r + 1:r].rearrange("p s k y x -> p (s k) y x"), ACT.Copy)
                return last

            def high_part(sc, par, r, n):
                kind, t, half = PIECES[n]
                nb = len(BLOCKS[r])
                q, kk = qd[par], ks[par]
                act.wait_ge(piece_ready, sc * NP + n + 1 + START)

                def queries(i0, i1, psum):
                    for h in range(4):
                        hp = slice(HD * h, HD * h + HD)
                        last = fn(q[hp, 0, t, i0:i1, h, :], psum[hp, :].rearrange("p (i q) -> p i q", q=NQ), ACT.Copy)
                    return last
                if kind == "q":
                    last = queries(0, 8, bank[3])
                else:
                    i0, i1 = halves(nb)[half]
                    last = fn(kk[:, 0, t, i0:i1, :].rearrange("p i n -> p (i n)"), bank[3][:, 0:(i1 - i0) * NK], ACT.Copy)
                    if half == 1 and nb > 8:
                        last = queries(8, 9, bank[3][:, 448:512])
                last.then_inc(hi_done, 1)

            def first(b):
                act.wait_ge(n1_done, (b + 1) * NCH + START)
                act.wait_ge(init_ready, (b + 1) * NCH + START)
                act.sem_inc(act_passed, 1)
                copy_blocks(0, 1, 0, range(len(BLOCKS[1]))).then_inc(strip_in, 2)
                for n in range(NP):
                    high_part(b * STRIPS_PER_B, 0, 1, n)
                act.wait_ge(qd_zero, b + 1 + START)

            def strip(at):
                def exps(i):
                    act.wait_ge(st_ready, at.before(i + 1))
                    act.wait_ge(pv_ready, at.before(i - 1))
                    fn(pb[at.turn(i)], bank[4 + at.turn(i)][0:NK, :], ACT.Exp, scale=HD ** -0.5).then_inc(exp_done, 1)

                def copy_v(i):
                    act.wait_ge(v_ready, at.before(i + 1))
                    act.wait_ge(pv_ready, at.before(i - 1))
                    fn(vb[at.turn(i)][:, :, 0:64], bank[2][0:NK, 0:C].rearrange("p (j c) -> p j c", j=PAIRS), ACT.Copy).then_inc(v_copied, 1)

                for i in at.steps:
                    if at.has(i - 2):
                        exps(i - 2)
                    if at.has(i - 1):
                        copy_v(i - 1)
                    if at.nxt:
                        todo = copies(len(BLOCKS[at.nxt[0]]), i)
                        if todo:
                            copy_blocks(1 - at.par, at.nxt[0], at.nxt[1], todo).then_inc(strip_in, 1)
                        if i in PIECE_AT[at.nb]:
                            high_part(at.sc + 1, 1 - at.par, at.nxt[0], PIECE_AT[at.nb][i])

            def layer_norm2(b, p):
                n0 = b * NCH + p * 2
                act.wait_ge(acc_added, (b + 1) * STRIPS_PER_B * CT + START)
                act.wait_ge(tb3_done, b + 1 + START)
                act.sem_inc(act_passed, 1)
                for j in range(2):
                    for t in range(CT):
                        a = acc[:, t, bass.ds(p * (2 * CH_ROWS) + j * CH_ROWS, CH_ROWS), :]
                        last = fn(a, a, ACT.Relu, bias=tb3[:, t:t + 1], scale=s3[:, t:t + 1])
                    last.then_inc(t_done, 1)
                for j in range(2):
                    act.wait_ge(cen2_ready, n0 + j + 1 + START)
                    for t in range(CT):
                        last = fn(sq2[j][:, t, :], bank[3 * j + t][:, :], ACT.Square)
                    last.then_inc(sq2_done, 1)
                for j in range(2):
                    act.wait_ge(var2_ready, n0 + j + 1 + START)
                    act.wait_ge(n2_stored, n0 + START)
                    fn(std2[j], bank[3 * j + 2][:, :], ACT.Sqrt, bias=eps).then_inc(std2_done, 1)

            def tail(b, s, rows, fresh, before, more):
                n = b * NCH + s
                f = b * TAIL_STRIPS + s

                def gelu1(m):
                    act.wait_ge(c1_ready, n * HT + m + 1 + START)
                    act.wait_ge(h_done, n * HT + max(m - 1, 0) + START)
                    if m == 0:
                        act.wait_ge(hs_zero, b * 2 + 1 + START)
                    fn(gt[m % 2], bank[3 + m % 2][:, :], ACT.Gelu, bias=hb[:, m % HT:m % HT + 1]).then_inc(gelu1_done, 1)

                def gelu2(m, k0, k1):
                    act.wait_ge(tap_done, f * STRIP_TAPS + taps_before(m + 1) + START)
                    if before or m >= 2:
                        act.wait_ge(c2_ready, f * HT + m - 1 + START)
                    fn(h2[m % 2][:, k0 * W:k1 * W], cv[m % 2][:, k0 * W:k1 * W], ACT.Gelu, bias=HV["mlp_dw_b"][:, m:m + 1]).then_inc(gelu2_done, 1)

                if not before:
                    gelu1(0)
                for m in range(HT):
                    if fresh and (m + 1 < HT or more):
                        gelu1(m + 1)
                    gelu2(m, *rows)

            GN_BASE = SETUP_LINKS
            with act.Fori(0, B) as b:
                group_std(b)
                with act.Fori(0, NCH) as c:
                    front(b, c)
                walk(act, b, first, strip)
                with act.Fori(0, NCH // 2) as p:
                    layer_norm2(b, p)
                walk_mlp(act, b, tail)


SETUP_LINKS = 10


def constants():
    import numpy as np
    c = np.zeros((P, CONST_COLS), np.float32)

    def put(name, a):
        c[:a.shape[0], CO[name][0]:CO[name][0] + a.shape[1]] = a
    eye = np.eye(P, dtype=np.float32)
    put("ident", eye)
    put("cdiag", eye - np.float32(1 / C))
    put("coff", np.full((P, P), -1 / C, np.float32))
    put("mean", np.full((P, P), 1 / C, np.float32))
    per = C // 32
    put("group", np.kron(np.eye(P // per), np.full((per, per), 1 / per)).astype(np.float32))
    i64 = np.eye(NQ, dtype=np.float32)
    put("pairI", np.concatenate([i64, i64], 1))
    mask = np.full((QB, QB, KB, KB), -1e30, np.float32)
    for y in range(QB):
        for x in range(QB):
            mask[y, x, y:y + 3, x:x + 3] = 0
    mask = mask.reshape(NQ, NK)
    put("mask", np.tile(mask, (1, 4)))
    left = np.zeros((96, 4, NK), np.float32)
    for j in range(4):
        left[j, j] = -1
        left[32:96, j] = mask
    put("left", left.reshape(96, 4 * NK))
    right = np.zeros((96, P), np.float32)
    right[32:96] = np.concatenate([i64, i64], 1)
    put("right", right)
    return c


def kernel(**inputs):
    import numpy as np
    import concourse.bacc as bacc
    from concourse import mybir as mb
    from concourse.bass_utils import run_bass_kernel_spmd

    w = {k[len("L0_conv_"):]: np.asarray(a) for k, a in inputs.items() if k != "x"}

    def transposed(a):
        a = np.transpose(a)
        return np.ascontiguousarray(a.reshape(-1, P, a.shape[1]).transpose(1, 0, 2))
    arrays = {
        "x": np.ascontiguousarray(inputs["x"]),
        "wqkv": np.ascontiguousarray(np.stack([transposed(w[f"qkv{i}_w"]) for i in (1, 2, 3)], 1)),
        "wproj": np.ascontiguousarray(np.stack([w[f"proj{i}_w"].reshape(CT, P, C).transpose(1, 0, 2) for i in (1, 2, 3)], 1)),
        "wtrans": transposed(w["tc_trans_w"]),
        "wconv": transposed(w["tc_conv_w"]),
        "wpool": transposed(w["tc_pool_w"]),
        "wc1": transposed(w["mlp_c1_w"]),
        "wc2": transposed(w["mlp_c2_w"]),
        "wdw": np.ascontiguousarray(w["mlp_dw_w"].reshape(HT, P, 9).transpose(1, 0, 2)),
        "vecs": np.ascontiguousarray(np.stack([w[n].reshape(CT, P).T for n in VECS], 1)),
        "hvecs": np.ascontiguousarray(np.stack([w[n].reshape(HT, P).T for n in HVECS], 1)),
        "consts": constants(),
    }
    nc = bacc.Bacc("TRN2", target_bir_lowering=False, num_devices=1)
    feed, args = {}, []
    for name, a in arrays.items():
        feed[f"{name}_dram"] = a
        args.append(nc.dram_tensor(f"{name}_dram", a.shape, mb.dt.from_np(a.dtype), kind="ExternalInput").ap())
    args.append(nc.dram_tensor("out_dram", (B, C, H, W), F32, kind="ExternalOutput").ap())
    build(nc, *args)
    r = run_bass_kernel_spmd(nc, [feed], core_ids=[0])
    return r.results[0]["out_dram"]
```
